# Optimizing a Trainium2 kernel written in Bass

```python
import numpy as np
import jax
import jax.numpy as jnp

def _softmax(x, axis=-1):
    return jax.nn.softmax(x, axis=axis)

def _gelu(x):
    return jax.nn.gelu(x, approximate=True)

def _silu(x):
    return jax.nn.silu(x)

def _sigmoid(x):
    return jax.nn.sigmoid(x)

def _layernorm(x, axis=-1, eps=1e-05):
    m = jnp.mean(x, axis=axis, keepdims=True)
    v = jnp.var(x, axis=axis, keepdims=True)
    return (x - m) / jnp.sqrt(v + eps)

def _scatter_add(tgt, idx, src, axis=0):
    return tgt.at[idx].add(src)

def _segment_sum(src, seg, n):
    return jax.ops.segment_sum(src, seg, n)
kernel_name = 'mk_flamingo_gated_d4_seqx_r8_9209a3'

def setup_inputs(seed: int=0):
    np.random.seed(seed)
    _w = jnp.asarray

    def _rec_inputs():
        import jax
        import jax.numpy as jnp
        _rk = jax.random.key(seed)
        x = -0.0003929 + 0.9999 * jax.random.normal(jax.random.fold_in(_rk, 1), (32, 128, 128), jnp.float32)
        _lenS = 128 - jax.random.randint(jax.random.fold_in(_rk, 7), (32,), 0, max(1, 128 // 4) + 1, jnp.int32)
        _lenS2 = 128 - jax.random.randint(jax.random.fold_in(_rk, 8), (32,), 0, max(1, 128 // 4) + 1, jnp.int32)
        _ctx_768P = jax.random.normal(jax.random.fold_in(_rk, 11), (32, 16, 96), jnp.float32)
        _ctx_768c = jax.random.dirichlet(jax.random.fold_in(_rk, 511), 0.3 * jnp.ones((16,), jnp.float32), (32, 128))
        _ctx_768t = jnp.einsum('bsk,bkd->bsd', _ctx_768c, _ctx_768P)
        _ctx_768t = _ctx_768t * jax.lax.rsqrt(jnp.mean(jnp.square(_ctx_768t)) + 1e-12) * 0.953939
        ctx_768 = -7.36909e-05 + 0.999899 * (_ctx_768t + 0.3 * jax.random.normal(jax.random.fold_in(_rk, 611), (32, 128, 96), jnp.float32))
        _validS = jnp.arange(128)[None, :] < _lenS[:, None]
        _validS2 = jnp.arange(128)[None, :] < _lenS2[:, None]
        _causal = jnp.tril(jnp.ones((128, 128), dtype=bool))
        mask_BxS2_bk0 = jnp.logical_not(jnp.broadcast_to(_validS2[:, :], (32, 128)))
        _g = jax.random.normal(jax.random.fold_in(_rk, 9001), (2, 4), jnp.float32)
        _g = jnp.sign(_g) * jnp.maximum(jnp.abs(_g), 1.0) + (_g == 0) * 1.0
        g_xattn = _g[0]
        g_ffn = _g[1]
        return (x, ctx_768, mask_BxS2_bk0, g_xattn, g_ffn)
    x, ctx_768, mask_BxS2_bk0, g_xattn, g_ffn = _rec_inputs()

    def _L0_xattn_setup():
        import jax, jax.numpy as jnp
        import numpy as np
        EPS = 1e-08
        key = jax.random.key(seed)
        kv, kt, k1, k2, k3, k4 = jax.random.split(key, 6)
        B, S = (16, 128)
        VD, TD, H = (128, 96, 64)
        visual_features = jax.random.normal(kv, (B, S, VD), dtype=jnp.float32)
        text_features = jax.random.normal(kt, (B, S, TD), dtype=jnp.float32)
        Wv = jax.random.normal(k1, (H, VD), dtype=jnp.float32) * (1.0 / np.sqrt(VD))
        bv = jax.random.normal(k2, (H,), dtype=jnp.float32) * 0.01
        Wt = jax.random.normal(k3, (H, TD), dtype=jnp.float32) * (1.0 / np.sqrt(TD))
        bt = jax.random.normal(k4, (H,), dtype=jnp.float32) * 0.01
        return {'visual_features': visual_features, 'text_features': text_features, 'Wv': Wv, 'bv': bv, 'Wt': Wt, 'bt': bt}
    _L0_xattn_all = _L0_xattn_setup()
    _L0_xattn_in = {k: v for k, v in _L0_xattn_all.items() if k in ('Wv', 'bv', 'Wt', 'bt')}
    del _L0_xattn_all

    def _L0_ffn_setup():
        import jax, jax.numpy as jnp
        import numpy as np
        B, M, D = (4, 256, 128)
        N, P = (64, 32)
        key = jax.random.key(seed)
        k1, k2, k3, k4 = jax.random.split(key, 4)
        x = jax.random.normal(k1, (B, M, D), dtype=jnp.float32)
        phi = jax.random.normal(k2, (D, N, P), dtype=jnp.float32) * (1.0 / np.sqrt(D))
        W = jax.random.normal(k3, (N, D, D), dtype=jnp.float32) * (1.0 / np.sqrt(D))
        b = jax.random.normal(k4, (N, D), dtype=jnp.float32) * 0.01
        return {'x': x, 'phi': phi, 'W': W, 'b': b}
    _L0_ffn_all = _L0_ffn_setup()
    _L0_ffn_in = {k: v for k, v in _L0_ffn_all.items() if k in ('phi', 'W', 'b')}
    del _L0_ffn_all

    def _L1_xattn_setup():
        import jax, jax.numpy as jnp
        import numpy as np
        IMAGE_DIM = 128
        TEXT_DIM = 96
        NUM_HEADS = 16
        HEAD_DIM = IMAGE_DIM // NUM_HEADS
        key = jax.random.key(seed)
        ks = jax.random.split(key, 14)
        B, N, M = (4, 512, 64)
        s_img = 1.0 / np.sqrt(IMAGE_DIM)
        s_txt = 1.0 / np.sqrt(TEXT_DIM)
        s_ff = 1.0 / np.sqrt(2 * IMAGE_DIM)
        return {'x': jax.random.normal(ks[0], (B, N, IMAGE_DIM), jnp.float32), 'y': jax.random.normal(ks[1], (B, M, TEXT_DIM), jnp.float32), 'Wq': jax.random.normal(ks[2], (IMAGE_DIM, IMAGE_DIM), jnp.float32) * s_img, 'bq': jax.random.normal(ks[3], (IMAGE_DIM,), jnp.float32) * s_img, 'Wk': jax.random.normal(ks[4], (TEXT_DIM, IMAGE_DIM), jnp.float32) * s_txt, 'bk': jax.random.normal(ks[5], (IMAGE_DIM,), jnp.float32) * s_txt, 'Wv': jax.random.normal(ks[6], (TEXT_DIM, IMAGE_DIM), jnp.float32) * s_txt, 'bv': jax.random.normal(ks[7], (IMAGE_DIM,), jnp.float32) * s_txt, 'W1': jax.random.normal(ks[8], (IMAGE_DIM, 2 * IMAGE_DIM), jnp.float32) * s_img, 'b1': jax.random.normal(ks[9], (2 * IMAGE_DIM,), jnp.float32) * s_img, 'W2': jax.random.normal(ks[10], (2 * IMAGE_DIM, IMAGE_DIM), jnp.float32) * s_ff, 'b2': jax.random.normal(ks[11], (IMAGE_DIM,), jnp.float32) * s_ff}
    _L1_xattn_all = _L1_xattn_setup()
    _L1_xattn_in = {k: v for k, v in _L1_xattn_all.items() if k in ('Wq', 'bq', 'Wk', 'bk', 'Wv', 'bv', 'W1', 'b1', 'W2', 'b2')}
    del _L1_xattn_all

    def _L1_ffn_setup():
        import jax, jax.numpy as jnp
        import numpy as np
        B, S, H = (2, 256, 128)
        I = 64
        E_R, E_Z = (32, 8)
        E_T = E_R + E_Z
        K = 6
        SCALE = 2.5
        W_INIT = 0.02
        key = jax.random.key(seed)
        k0, k1, k2, k3 = jax.random.split(key, 4)
        return {'hidden_states': jax.random.normal(k0, (B, S, H), jnp.float32), 'classifier_weight': jax.random.normal(k1, (E_T, H), jnp.float32) * W_INIT, 'e_score_correction_bias': jnp.zeros((E_T,), jnp.float32), 'gate_up_proj': jax.random.normal(k2, (E_T, 2 * I, H), jnp.float32) * W_INIT, 'down_proj': jax.random.normal(k3, (E_R, H, I), jnp.float32) * W_INIT}
    _L1_ffn_all = _L1_ffn_setup()
    _L1_ffn_in = {k: v for k, v in _L1_ffn_all.items() if k in ('classifier_weight', 'e_score_correction_bias', 'gate_up_proj', 'down_proj')}
    del _L1_ffn_all

    def _L2_xattn_setup():
        import jax, jax.numpy as jnp
        import numpy as np
        DIM_IN, DIM_LAT, DIM_HEAD = (96, 128, 64)
        INNER = max(DIM_LAT, DIM_IN)
        HEADS = INNER // DIM_HEAD
        SCALE = DIM_HEAD ** (-0.5)
        RMS_EPS = 1e-08
        LN_EPS = 1e-05

        def layernorm(x, g, b):
            mu = jnp.mean(x, axis=-1, keepdims=True)
            var = jnp.mean((x - mu) ** 2, axis=-1, keepdims=True)
            return (x - mu) * jax.lax.rsqrt(var + LN_EPS) * g + b

        def rmsnorm(x, gamma):
            norm = jnp.sqrt(jnp.sum(x * x, axis=-1, keepdims=True)) * x.shape[-1] ** (-0.5)
            return x / jnp.maximum(norm, RMS_EPS) * gamma
        key = jax.random.key(seed)
        ks = jax.random.split(key, 12)
        b, n, m = (4, 512, 64)
        x = jax.random.normal(ks[0], (b, n, DIM_IN), jnp.float32)
        latents = jax.random.normal(ks[1], (b, m, DIM_LAT), jnp.float32)
        mask = jax.random.randint(ks[2], (b, n), 0, 2).astype(bool)
        s = lambda k, sh, fan: jax.random.normal(k, sh, jnp.float32) * fan ** (-0.5)
        return {'x': x, 'latents': latents, 'mask': mask, 'ln_x_g': jnp.ones((DIM_IN,), jnp.float32), 'ln_x_b': jnp.zeros((DIM_IN,), jnp.float32), 'ln_l_g': jnp.ones((DIM_LAT,), jnp.float32), 'ln_l_b': jnp.zeros((DIM_LAT,), jnp.float32), 'qn_g': jnp.ones((DIM_HEAD,), jnp.float32), 'kn_g': jnp.ones((DIM_HEAD,), jnp.float32), 'Wq': s(ks[3], (INNER, DIM_LAT), DIM_LAT), 'Wkv': s(ks[4], (2 * INNER, DIM_IN), DIM_IN), 'Wlkv': s(ks[5], (2 * INNER, DIM_LAT), DIM_LAT), 'Wo': s(ks[6], (DIM_LAT, INNER), INNER), 'bo': jnp.zeros((DIM_LAT,), jnp.float32)}
    _L2_xattn_all = _L2_xattn_setup()
    _L2_xattn_in = {k: v for k, v in _L2_xattn_all.items() if k in ('ln_x_g', 'ln_x_b', 'ln_l_g', 'ln_l_b', 'qn_g', 'kn_g', 'Wq', 'Wkv', 'Wlkv', 'Wo', 'bo')}
    del _L2_xattn_all

    def _L2_ffn_setup():
        import jax, jax.numpy as jnp
        import numpy as np
        CAPACITY_FACTOR = 1.25
        key = jax.random.key(seed)
        ks = jax.random.split(key, 6)
        B, S, H, E = (4, 512, 128, 8)
        scale = 1.0 / np.sqrt(H)
        return {'tokens': jax.random.normal(ks[0], (B, S, H), dtype=jnp.float32), 'gate_w': jax.random.normal(ks[1], (E, H), dtype=jnp.float32) * scale, 'w1': jax.random.normal(ks[2], (E, H, H), dtype=jnp.float32) * scale, 'b1': jax.random.normal(ks[3], (E, H), dtype=jnp.float32) * 0.01, 'w2': jax.random.normal(ks[4], (E, H, H), dtype=jnp.float32) * scale, 'b2': jax.random.normal(ks[5], (E, H), dtype=jnp.float32) * 0.01}
    _L2_ffn_all = _L2_ffn_setup()
    _L2_ffn_in = {k: v for k, v in _L2_ffn_all.items() if k in ('gate_w', 'w1', 'b1', 'w2', 'b2')}
    del _L2_ffn_all

    def _L3_xattn_setup():
        import jax, jax.numpy as jnp
        import numpy as np
        NUM_HEADS = 16
        HEAD_DIM = 64
        INNER = NUM_HEADS * HEAD_DIM
        QUERY_DIM = 128
        CONTEXT_DIM = 96
        SCALE = HEAD_DIM ** (-0.5)
        key = jax.random.key(seed)
        ks = jax.random.split(key, 6)
        B, NQ, NKV = (8, 128, 256)
        query = jax.random.normal(ks[0], (B, NQ, QUERY_DIM), dtype=jnp.float32)
        context = jax.random.normal(ks[1], (B, NKV, CONTEXT_DIM), dtype=jnp.float32)
        w_q = jax.random.normal(ks[2], (QUERY_DIM, INNER), dtype=jnp.float32) * QUERY_DIM ** (-0.5)
        w_kv = jax.random.normal(ks[3], (CONTEXT_DIM, 2 * INNER), dtype=jnp.float32) * CONTEXT_DIM ** (-0.5)
        w_out = jax.random.normal(ks[4], (INNER, QUERY_DIM), dtype=jnp.float32) * INNER ** (-0.5)
        b_out = jax.random.normal(ks[5], (QUERY_DIM,), dtype=jnp.float32) * 0.01
        return {'query': query, 'context': context, 'w_q': w_q, 'w_kv': w_kv, 'w_out': w_out, 'b_out': b_out}
    _L3_xattn_all = _L3_xattn_setup()
    _L3_xattn_in = {k: v for k, v in _L3_xattn_all.items() if k in ('w_q', 'w_kv', 'w_out', 'b_out')}
    del _L3_xattn_all

    def _L3_ffn_setup():
        import jax, jax.numpy as jnp
        import numpy as np
        CAPACITY_RATIO = 0.75
        key = jax.random.key(seed)
        k1, k2, k3 = jax.random.split(key, 3)
        B, L, D = (4, 1024, 128)
        x = jax.random.normal(k1, (B, L, D), dtype=jnp.float32)
        w_router = jax.random.normal(k2, (D,), dtype=jnp.float32) * 0.02
        w_block = jax.random.normal(k3, (D, D), dtype=jnp.float32) * 0.02
        return {'x': x, 'w_router': w_router, 'w_block': w_block}
    _L3_ffn_all = _L3_ffn_setup()
    _L3_ffn_in = {k: v for k, v in _L3_ffn_all.items() if k in ('w_router', 'w_block')}
    del _L3_ffn_all
    return {'x': x, 'ctx_768': ctx_768, 'mask_BxS2_bk0': mask_BxS2_bk0, 'g_xattn': g_xattn, 'g_ffn': g_ffn, 'L0_xattn_Wv': _L0_xattn_in['Wv'], 'L0_xattn_bv': _L0_xattn_in['bv'], 'L0_xattn_Wt': _L0_xattn_in['Wt'], 'L0_xattn_bt': _L0_xattn_in['bt'], 'L0_ffn_phi': _L0_ffn_in['phi'], 'L0_ffn_W': _L0_ffn_in['W'], 'L0_ffn_b': _L0_ffn_in['b'], 'L1_xattn_Wq': _L1_xattn_in['Wq'], 'L1_xattn_bq': _L1_xattn_in['bq'], 'L1_xattn_Wk': _L1_xattn_in['Wk'], 'L1_xattn_bk': _L1_xattn_in['bk'], 'L1_xattn_Wv': _L1_xattn_in['Wv'], 'L1_xattn_bv': _L1_xattn_in['bv'], 'L1_xattn_W1': _L1_xattn_in['W1'], 'L1_xattn_b1': _L1_xattn_in['b1'], 'L1_xattn_W2': _L1_xattn_in['W2'], 'L1_xattn_b2': _L1_xattn_in['b2'], 'L1_ffn_classifier_weight': _L1_ffn_in['classifier_weight'], 'L1_ffn_e_score_correction_bias': _L1_ffn_in['e_score_correction_bias'], 'L1_ffn_gate_up_proj': _L1_ffn_in['gate_up_proj'], 'L1_ffn_down_proj': _L1_ffn_in['down_proj'], 'L2_xattn_ln_x_g': _L2_xattn_in['ln_x_g'], 'L2_xattn_ln_x_b': _L2_xattn_in['ln_x_b'], 'L2_xattn_ln_l_g': _L2_xattn_in['ln_l_g'], 'L2_xattn_ln_l_b': _L2_xattn_in['ln_l_b'], 'L2_xattn_qn_g': _L2_xattn_in['qn_g'], 'L2_xattn_kn_g': _L2_xattn_in['kn_g'], 'L2_xattn_Wq': _L2_xattn_in['Wq'], 'L2_xattn_Wkv': _L2_xattn_in['Wkv'], 'L2_xattn_Wlkv': _L2_xattn_in['Wlkv'], 'L2_xattn_Wo': _L2_xattn_in['Wo'], 'L2_xattn_bo': _L2_xattn_in['bo'], 'L2_ffn_gate_w': _L2_ffn_in['gate_w'], 'L2_ffn_w1': _L2_ffn_in['w1'], 'L2_ffn_b1': _L2_ffn_in['b1'], 'L2_ffn_w2': _L2_ffn_in['w2'], 'L2_ffn_b2': _L2_ffn_in['b2'], 'L3_xattn_w_q': _L3_xattn_in['w_q'], 'L3_xattn_w_kv': _L3_xattn_in['w_kv'], 'L3_xattn_w_out': _L3_xattn_in['w_out'], 'L3_xattn_b_out': _L3_xattn_in['b_out'], 'L3_ffn_w_router': _L3_ffn_in['w_router'], 'L3_ffn_w_block': _L3_ffn_in['w_block']}

def reference(x, ctx_768, mask_BxS2_bk0, g_xattn, g_ffn, L0_xattn_Wv, L0_xattn_bv, L0_xattn_Wt, L0_xattn_bt, L0_ffn_phi, L0_ffn_W, L0_ffn_b, L1_xattn_Wq, L1_xattn_bq, L1_xattn_Wk, L1_xattn_bk, L1_xattn_Wv, L1_xattn_bv, L1_xattn_W1, L1_xattn_b1, L1_xattn_W2, L1_xattn_b2, L1_ffn_classifier_weight, L1_ffn_e_score_correction_bias, L1_ffn_gate_up_proj, L1_ffn_down_proj, L2_xattn_ln_x_g, L2_xattn_ln_x_b, L2_xattn_ln_l_g, L2_xattn_ln_l_b, L2_xattn_qn_g, L2_xattn_kn_g, L2_xattn_Wq, L2_xattn_Wkv, L2_xattn_Wlkv, L2_xattn_Wo, L2_xattn_bo, L2_ffn_gate_w, L2_ffn_w1, L2_ffn_b1, L2_ffn_w2, L2_ffn_b2, L3_xattn_w_q, L3_xattn_w_kv, L3_xattn_w_out, L3_xattn_b_out, L3_ffn_w_router, L3_ffn_w_block):
    import jax
    import jax.numpy as jnp

    def _L0_xattn_ref(visual_features, text_features, Wv, bv, Wt, bt):
        import jax, jax.numpy as jnp
        import numpy as np
        EPS = 1e-08
        v = jnp.einsum('bsd,hd->bsh', visual_features, Wv) + bv
        t = jnp.einsum('bsd,hd->bsh', text_features, Wt) + bt
        dots = jnp.einsum('bih,bjh->bij', v, t)
        vn = jnp.linalg.norm(v, axis=-1)
        tn = jnp.linalg.norm(t, axis=-1)
        denom = jnp.maximum(vn[:, :, None] * tn[:, None, :], EPS)
        return dots / denom

    def _L0_ffn_ref(x, phi, W, b):
        import jax, jax.numpy as jnp
        import numpy as np
        B, M, D = (4, 256, 128)
        N, P = (64, 32)
        logits = jnp.einsum('bmd,dnp->bmnp', x, phi)
        dispatch = jax.nn.softmax(logits, axis=0)
        bsz, m, n, p = logits.shape
        combine = jax.nn.softmax(logits.reshape(bsz, m, n * p), axis=-1).reshape(bsz, m, n, p)
        slots = jnp.einsum('bmd,bmnp->bnpd', x, dispatch)
        y = jnp.einsum('bnpd,nde->bnpe', slots, W) + b[None, :, None, :]
        out = jnp.einsum('bnpd,bmnp->bmd', y, combine)
        return out

    def _L1_xattn_ref(x, y, Wq, bq, Wk, bk, Wv, bv, W1, b1, W2, b2):
        import jax, jax.numpy as jnp
        import numpy as np
        IMAGE_DIM = 128
        TEXT_DIM = 96
        NUM_HEADS = 16
        HEAD_DIM = IMAGE_DIM // NUM_HEADS
        B, N, _ = x.shape
        M = y.shape[1]
        q = (x @ Wq + bq).reshape(B, N, NUM_HEADS, HEAD_DIM)
        k = (y @ Wk + bk).reshape(B, M, NUM_HEADS, HEAD_DIM)
        v = (y @ Wv + bv).reshape(B, M, NUM_HEADS, HEAD_DIM)
        scale = 1.0 / np.sqrt(HEAD_DIM)
        scores = jnp.einsum('bnhd,bmhd->bhnm', q, k) * scale
        attn = jax.nn.softmax(scores, axis=-1)
        out = jnp.einsum('bhnm,bmhd->bnhd', attn, v).reshape(B, N, IMAGE_DIM)
        h = jax.nn.relu(out @ W1 + b1)
        return h @ W2 + b2

    def _L1_ffn_ref(hidden_states, classifier_weight, e_score_correction_bias, gate_up_proj, down_proj):
        import jax, jax.numpy as jnp
        import numpy as np
        B, S, H = (2, 256, 128)
        I = 64
        E_R, E_Z = (32, 8)
        E_T = E_R + E_Z
        K = 6
        SCALE = 2.5
        W_INIT = 0.02
        orig_shape = hidden_states.shape
        x = hidden_states.reshape(-1, H).astype(jnp.float32)
        T = x.shape[0]
        logits = x @ classifier_weight.T
        scores = jax.nn.softmax(logits, axis=-1)
        _, topk_idx = jax.lax.top_k(scores + e_score_correction_bias[None, :], K)
        topk_w = jnp.take_along_axis(scores, topk_idx, axis=1) * SCALE
        w_full = jnp.zeros((T, E_T), jnp.float32).at[jnp.arange(T)[:, None], topk_idx].add(topk_w)
        zero_w = w_full[:, E_R:].sum(axis=-1, keepdims=True)
        out0 = x * zero_w
        routed_w = w_full[:, :E_R].T

        def body(out, xs):
            Wgu, Wd, we = xs
            gate, up = jnp.split(x @ Wgu.T, 2, axis=-1)
            y = jax.nn.silu(gate) * up @ Wd.T
            return (out + we[:, None] * y, None)
        out, _ = jax.lax.scan(body, out0, (gate_up_proj[:E_R], down_proj, routed_w))
        return out.reshape(orig_shape).astype(hidden_states.dtype)

    def _L2_xattn_ref(x, latents, mask, ln_x_g, ln_x_b, ln_l_g, ln_l_b, qn_g, kn_g, Wq, Wkv, Wlkv, Wo, bo):
        import jax, jax.numpy as jnp
        import numpy as np
        DIM_IN, DIM_LAT, DIM_HEAD = (96, 128, 64)
        INNER = max(DIM_LAT, DIM_IN)
        HEADS = INNER // DIM_HEAD
        SCALE = DIM_HEAD ** (-0.5)
        RMS_EPS = 1e-08
        LN_EPS = 1e-05

        def layernorm(x, g, b):
            mu = jnp.mean(x, axis=-1, keepdims=True)
            var = jnp.mean((x - mu) ** 2, axis=-1, keepdims=True)
            return (x - mu) * jax.lax.rsqrt(var + LN_EPS) * g + b

        def rmsnorm(x, gamma):
            norm = jnp.sqrt(jnp.sum(x * x, axis=-1, keepdims=True)) * x.shape[-1] ** (-0.5)
            return x / jnp.maximum(norm, RMS_EPS) * gamma
        b, n, _ = x.shape
        m = latents.shape[1]
        xn = layernorm(x, ln_x_g, ln_x_b)
        ln = layernorm(latents, ln_l_g, ln_l_b)
        q = ln @ Wq.T
        kv = jnp.concatenate([xn @ Wkv.T, ln @ Wlkv.T], axis=1)
        k, v = (kv[..., :INNER], kv[..., INNER:])
        split_heads = lambda t: t.reshape(t.shape[0], t.shape[1], HEADS, DIM_HEAD).transpose(0, 2, 1, 3)
        q, k, v = (split_heads(q), split_heads(k), split_heads(v))
        qn = rmsnorm(q, qn_g) * SCALE
        kn = rmsnorm(k, kn_g)
        attn = jnp.einsum('bhid,bhjd->bhij', qn, kn)
        full_mask = jnp.pad(mask, ((0, 0), (0, m)), constant_values=True)
        attn = jnp.where(full_mask[:, None, None, :], attn, -jnp.finfo(attn.dtype).max)
        attn = jax.nn.softmax(attn, axis=-1)
        out = jnp.einsum('bhij,bhjd->bhid', attn, v)
        out = out.transpose(0, 2, 1, 3).reshape(b, m, INNER)
        return out @ Wo.T + bo

    def _L2_ffn_ref(tokens, gate_w, w1, b1, w2, b2):
        import jax, jax.numpy as jnp
        import numpy as np
        CAPACITY_FACTOR = 1.25
        B, S, H = tokens.shape
        E = gate_w.shape[0]
        N = B * S
        cap = int(CAPACITY_FACTOR * N / E)
        x = tokens.reshape(N, H)
        probs = jax.nn.softmax(x @ gate_w.T, axis=-1)
        top2_w, top2_idx = jax.lax.top_k(probs, 2)
        a_e = top2_idx.reshape(-1)
        a_w = top2_w.reshape(-1)
        tok_id = jnp.arange(2 * N) // 2
        counts = jnp.bincount(a_e, length=E)
        keep = counts <= cap
        valid = keep[a_e]
        onehot = jax.nn.one_hot(a_e, E, dtype=jnp.int32)
        pos = jnp.take_along_axis(jnp.cumsum(onehot, axis=0) - 1, a_e[:, None], axis=1)[:, 0]
        p = jnp.where(valid, jnp.minimum(pos, cap - 1), cap)
        x_a = x[tok_id]
        buf = jnp.zeros((E, cap + 1, H), dtype=x.dtype).at[a_e, p].set(x_a)
        h = jax.nn.silu(jnp.einsum('ech,efh->ecf', buf, w1) + b1[:, None, :])
        y = jnp.einsum('ecf,egf->ecg', h, w2) + b2[:, None, :]
        contrib = y[a_e, p] * (a_w * valid.astype(x.dtype))[:, None]
        out = contrib.reshape(N, 2, H).sum(axis=1)
        return out.reshape(B, S, H)

    def _L3_xattn_ref(query, context, w_q, w_kv, w_out, b_out):
        import jax, jax.numpy as jnp
        import numpy as np
        NUM_HEADS = 16
        HEAD_DIM = 64
        INNER = NUM_HEADS * HEAD_DIM
        QUERY_DIM = 128
        CONTEXT_DIM = 96
        SCALE = HEAD_DIM ** (-0.5)
        B, NQ, _ = query.shape
        NKV = context.shape[1]
        q = query @ w_q
        kv = context @ w_kv
        k, v = jnp.split(kv, 2, axis=-1)
        q = q.reshape(B, NQ, NUM_HEADS, HEAD_DIM).transpose(0, 2, 1, 3)
        k = k.reshape(B, NKV, NUM_HEADS, HEAD_DIM).transpose(0, 2, 1, 3)
        v = v.reshape(B, NKV, NUM_HEADS, HEAD_DIM).transpose(0, 2, 1, 3)
        scores = jnp.einsum('bhqd,bhkd->bhqk', q, k) * SCALE
        attn = jax.nn.softmax(scores, axis=-1)
        out = jnp.einsum('bhqk,bhkd->bhqd', attn, v)
        out = out.transpose(0, 2, 1, 3).reshape(B, NQ, INNER)
        return out @ w_out + b_out

    def _L3_ffn_ref(x, w_router, w_block):
        import jax, jax.numpy as jnp
        import numpy as np
        CAPACITY_RATIO = 0.75
        B, L, D = x.shape
        k = max(1, int(L * CAPACITY_RATIO))
        scores = jnp.einsum('bld,d->bl', x, w_router)
        _, top_idx = jax.lax.top_k(scores, k)
        selected = jnp.take_along_axis(x, top_idx[:, :, None], axis=1)
        processed = jax.nn.gelu(jnp.einsum('bkd,de->bke', selected, w_block))
        batch_idx = jnp.arange(B)[:, None]
        out = x.at[batch_idx, top_idx].set(processed)
        return out
    x = x + jnp.tanh(g_xattn[0]) * _L0_xattn_ref(_layernorm(x, axis=-1), ctx_768, L0_xattn_Wv, L0_xattn_bv, L0_xattn_Wt, L0_xattn_bt)
    x = x + jnp.tanh(g_ffn[0]) * _L0_ffn_ref(_layernorm(x, axis=-1), L0_ffn_phi, L0_ffn_W, L0_ffn_b)
    x = x + jnp.tanh(g_xattn[1]) * _L1_xattn_ref(_layernorm(x, axis=-1), ctx_768, L1_xattn_Wq, L1_xattn_bq, L1_xattn_Wk, L1_xattn_bk, L1_xattn_Wv, L1_xattn_bv, L1_xattn_W1, L1_xattn_b1, L1_xattn_W2, L1_xattn_b2)
    x = x + jnp.tanh(g_ffn[1]) * _L1_ffn_ref(_layernorm(x, axis=-1), L1_ffn_classifier_weight, L1_ffn_e_score_correction_bias, L1_ffn_gate_up_proj, L1_ffn_down_proj)
    x = x + jnp.tanh(g_xattn[2]) * _L2_xattn_ref(ctx_768, _layernorm(x, axis=-1), mask_BxS2_bk0, L2_xattn_ln_x_g, L2_xattn_ln_x_b, L2_xattn_ln_l_g, L2_xattn_ln_l_b, L2_xattn_qn_g, L2_xattn_kn_g, L2_xattn_Wq, L2_xattn_Wkv, L2_xattn_Wlkv, L2_xattn_Wo, L2_xattn_bo)
    x = x + jnp.tanh(g_ffn[2]) * _L2_ffn_ref(_layernorm(x, axis=-1), L2_ffn_gate_w, L2_ffn_w1, L2_ffn_b1, L2_ffn_w2, L2_ffn_b2)
    x = x + jnp.tanh(g_xattn[3]) * _L3_xattn_ref(_layernorm(x, axis=-1), ctx_768, L3_xattn_w_q, L3_xattn_w_kv, L3_xattn_w_out, L3_xattn_b_out)
    x = x + jnp.tanh(g_ffn[3]) * _L3_ffn_ref(_layernorm(x, axis=-1), L3_ffn_w_router, L3_ffn_w_block)
    return x

_drawn_inputs = setup_inputs


def setup_inputs(seed=0):
    import zlib

    import numpy as np

    out = dict(_drawn_inputs(seed))
    spreads = {'L1_ffn_e_score_correction_bias': (0.0, 0.1),
     'L2_xattn_ln_x_g': (1.0, 0.2),
     'L2_xattn_ln_x_b': (0.0, 0.1),
     'L2_xattn_ln_l_g': (1.0, 0.2),
     'L2_xattn_ln_l_b': (0.0, 0.1),
     'L2_xattn_qn_g': (1.0, 0.2),
     'L2_xattn_kn_g': (1.0, 0.2),
     'L2_xattn_bo': (0.0, 0.1)}
    factors = {'g_ffn': 30.04,
     'L0_xattn_bv': 21.949,
     'L0_xattn_bt': 38.58,
     'L0_ffn_b': 6.193,
     'L1_xattn_bk': 64.0,
     'L1_ffn_gate_up_proj': 6.218,
     'L1_ffn_down_proj': 6.219,
     'L2_ffn_b1': 39.205,
     'L2_ffn_b2': 45.021,
     'L3_xattn_b_out': 4.851}
    for name, (base, spread) in spreads.items():
        noise = np.random.default_rng([zlib.crc32(name.encode()), seed]).standard_normal(out[name].shape)
        drawn = base * np.exp(spread * noise) if base else spread * noise
        out[name] = jnp.asarray(drawn.astype(out[name].dtype))
    for name, factor in factors.items():
        out[name] = (out[name] * factor).astype(out[name].dtype)
    return out
```

```python
from contextlib import ExitStack

import numpy as np

import concourse.bass as bass
from concourse import mybir

F32 = mybir.dt.float32
ALU = mybir.AluOpType
ACT = mybir.ActivationFunctionType
AX = mybir.AxisListType

B, S, D, C = 32, 128, 128, 96
G = 4
GROUPS = B // G
PAIRS = GROUPS // 2
N = G * S
LN_EPS = 1e-5
BIG = 3.0e38


class Core:

    def __init__(self, nc, ctx):
        self.nc, self.ctx, self.layer_semaphores = nc, ctx, []
        self.X = self.sbuf("x_resident", [S, B, D])
        self.ident = self.sbuf("ident", [128, 128])
        self.ones = self.sbuf("ones", [128, 128])
        self.gates = self.sbuf("gates", [128, 8])
        self.eps = self.sbuf("eps", [128, B])
        self.minus_half = self.sbuf("minus_half", [128, B])
        self.X_groups = self.X[:, :, :].rearrange("p (i s j) d -> p i s j d", s=2, j=G)

    def sbuf(self, name, shape, dt=F32, ctx=None):
        return (ctx or self.ctx).enter_context(self.nc.sbuf_tensor(name, shape, dt))

    def psum(self, ctx, name, shape):
        return ctx.enter_context(self.nc.psum_tensor(name, shape, F32))

    def sem(self, ctx, name):
        handle = self.nc.alloc_semaphore(name)
        self.layer_semaphores.append(handle)
        return handle

    def end_layer(self):
        self.nc.clear_and_free_semaphores(self.layer_semaphores)
        self.layer_semaphores = []
        self.nc.all_engine_barrier()


def turns(eng, body):
    with eng.Fori(0, PAIRS - 1) as i:
        body(i, 0, i * 2, (i, 1, i * 2 + 1))
        body(i, 1, i * 2 + 1, (i + 1, 0, i * 2 + 2))
    i = PAIRS - 1
    body(i, 0, i * 2, (i, 1, i * 2 + 1))
    body(i, 1, i * 2 + 1, None)


def settled(eng, sem, value, passed):
    eng.wait_ge(sem, value)
    eng.sem_inc(passed, 1)


class Norm:

    def __init__(self, core, ctx, layer, bank, width=D, slots=2, source=None):
        self.core, self.nc, self.bank, self.width = core, core.nc, bank, width
        self.source = source or (lambda i, s: core.X_groups[:, i, s])
        sb = lambda name, shape: core.sbuf(f"{layer}_{name}", shape, ctx=ctx)
        self.stats = sb("stats", [S, slots, G, 6])
        self.mv = sb("mean_var", [S, slots, G, 2])
        self.veps = sb("var_eps", [S, slots, G])
        self.rstd = sb("rstd", [S, slots, G])
        self.xn = sb("xn", [S, slots, G, width])
        self.xT = sb("xT", [width, slots, N])
        sem = lambda name: core.sem(ctx, f"{layer}_{name}")
        self.stats_done, self.mv_done, self.veps_done = sem("stats_done"), sem("mv_done"), sem("veps_done")
        self.rstd_done, self.xn_done = sem("rstd_done"), sem("xn_done")
        self.turned, self.xT_ready = sem("turned"), sem("xT_ready")
        self.passed = sem("passed")

    def vector_stats(self, dve, i, s, it):
        x = self.source(i, s)
        for j in range(G):
            last = self.nc.vector.bn_stats(self.stats[:, s, j, :], x[:, j, :])
        last.then_inc(self.stats_done, 1)
        settled(dve, self.stats_done, it + 1, self.passed)
        for j in range(G):
            last = self.nc.vector.bn_aggr(self.mv[:, s, j, :], self.stats[:, s, j, :])
        last.then_inc(self.mv_done, 1)

    def gpsimd_rstd(self, pool, i, s, it):
        core = self.core
        pool.wait_ge(self.mv_done, it + 1)
        self.nc.gpsimd.tensor_tensor(self.veps[:, s, :], self.mv[:, s, :, 1], core.eps[:, 0:G],
                                     ALU.add).then_inc(self.veps_done, 1)
        pool.wait_ge(self.veps_done, it + 1)
        self.nc.gpsimd.tensor_tensor(self.rstd[:, s, :], self.veps[:, s, :], core.minus_half[:, 0:G],
                                     ALU.pow).then_inc(self.rstd_done, 1)

    def vector_normalise(self, dve, i, s, it):
        x = self.source(i, s)
        dve.wait_ge(self.rstd_done, it + 1)
        for j in range(G):
            last = self.nc.vector.tensor_scalar(self.xn[:, s, j, :], x[:, j, :], self.mv[:, s, j, 0:1],
                                                self.rstd[:, s, j:j + 1], ALU.subtract, ALU.mult)
        last.then_inc(self.xn_done, 1)

    def vector(self, dve, i, s, it):
        self.vector_stats(dve, i, s, it)
        self.vector_normalise(dve, i, s, it)

    def tensor_turn(self, pe, i, s, it):
        pe.wait_ge(self.xn_done, it + 1)
        for j in range(G):
            last = self.nc.tensor.transpose(self.bank[0:self.width, j * S:(j + 1) * S],
                                            self.xn[:, s, j, :], self.core.ident[:, :])
        last.then_inc(self.turned, 1)

    def scalar_copy(self, act, i, s, it):
        act.wait_ge(self.turned, it + 1)
        self.nc.scalar.activation(self.xT[:, s, :], self.bank[0:self.width, :],
                                  ACT.Copy).then_inc(self.xT_ready, 1)


def load(eng, sem, pairs):
    for to, source in pairs:
        eng.dma_start(to, source).then_inc(sem, 16)
    return 16 * len(pairs)


def setup(core, x, gates):
    nc, X = core.nc, core.X
    with ExitStack() as ctx:
        raw = core.sbuf("raw_gates", [128, 8], ctx=ctx)
        landed, made = core.sem(ctx, "inputs_landed"), core.sem(ctx, "constants_made")
        with nc.Block() as block:
            @block.sync
            def _(sp):
                sp.dma_start(raw[:, :], gates).then_inc(landed, 16)
                sp.dma_start(X[:, :, :], x.rearrange("b s d -> s b d")).then_inc(landed, 16)
                sp.wait_ge(landed, 32)

            @block.gpsimd
            def _(pool):
                nc.gpsimd.memset(core.ones[:, :], 1.0)
                nc.gpsimd.memset(core.eps[:, :], LN_EPS)
                nc.gpsimd.memset(core.minus_half[:, :], -0.5)
                nc.gpsimd.memset(core.ident[:, :], 0.0).then_inc(made, 1)
                pool.wait_ge(made, 1)
                nc.gpsimd.affine_select(out=core.ident[:, :], in_=core.ident[:, :], compare_op=ALU.not_equal,
                                        fill=1.0, base=0, pattern=[[-1, 128]], channel_multiplier=1)

            @block.scalar
            def _(act):
                act.wait_ge(landed, 32)
                nc.scalar.activation(core.gates[:, :], raw[:, :], ACT.Tanh)


def layer0_cosine(core, ctxT, wvT, bv, wtT, bt):
    nc, H, EPS = core.nc, 64, 1e-8
    with ExitStack() as ctx:
        sb = lambda name, shape: core.sbuf("c0_" + name, shape, ctx=ctx)
        sem = lambda name: core.sem(ctx, "c0_" + name)
        bank = [core.psum(ctx, f"c0_bank{k}", [128, 512]) for k in range(8)]
        norm = Norm(core, ctx, "c0", bank[0])
        wv, wt, bvc, btc = sb("wv", [D, H]), sb("wt", [C, H]), sb("bv", [H, 1]), sb("bt", [H, 1])
        cT = sb("cT", [C, 2, N])
        vT, tT, v2, t2 = (sb(n, [H, 2, N]) for n in ("vT", "tT", "v2", "t2"))
        tn, vn = sb("tn", [S, 2, N]), sb("vn", [S, 2, G])
        den, rden, cosine = sb("den", [S, 2, N]), sb("rden", [S, 2, N]), sb("cosine", [S, 2, N])
        vps, tps = bank[1], bank[2]
        dots, tn2 = bank[3:5], bank[5:7]
        vn2 = bank[7]
        weights, ctx_landed = sem("weights"), [sem("ctx_landed0"), sem("ctx_landed1")]
        projected, squared, summed, rooted = (sem(n) for n in ("projected", "squared", "summed", "rooted"))
        den_done, rden_done, cosine_done, updated = (
            sem(n) for n in ("den_done", "rden_done", "cosine_done", "updated"))
        ctx_groups = ctxT.rearrange("c (i s n) -> c i s n", s=2, n=N)
        with nc.Block() as block:
            @block.sync
            def _(sp):
                load(sp, weights, [(wv[:, :], wvT), (wt[:, :], wtT), (bvc[:, :], bv), (btc[:, :], bt)])

                def group(i, s, it, nxt):
                    sp.wait_ge(updated, it + 1)
                    sp.dma_start(cT[:, s, :], ctx_groups[:, i, s, :]).then_inc(ctx_landed[s], 16)
                turns(sp, group)

            @block.gpsimd
            def _(pool):
                turns(pool, lambda i, s, it, nxt: norm.gpsimd_rstd(pool, i, s, it))

            @block.vector
            def _(dve):
                dve.sem_inc(updated, 2)
                norm.vector(dve, 0, 0, 0)

                def group(i, s, it, nxt):
                    x = core.X_groups[:, i, s]
                    if nxt:
                        norm.vector(dve, *nxt)
                    dve.wait_ge(rooted, it + 1)
                    for j in range(G):
                        js = slice(j * S, (j + 1) * S)
                        last = nc.vector.tensor_scalar(den[:, s, js], tn[:, s, js], vn[:, s, j:j + 1], EPS,
                                                       ALU.mult, ALU.max)
                    last.then_inc(den_done, 1)
                    dve.wait_ge(den_done, it + 1)
                    nc.vector.reciprocal(rden[:, s, :], den[:, s, :]).then_inc(rden_done, 1)
                    dve.wait_ge(rden_done, it + 1)
                    nc.vector.tensor_tensor(cosine[:, s, :], dots[s][:, :], rden[:, s, :],
                                            ALU.mult).then_inc(cosine_done, 1)
                    dve.wait_ge(cosine_done, it + 1)
                    nc.vector.scalar_tensor_tensor(
                        out=x, in0=cosine[:, s, :].rearrange("p (j d) -> p j d", j=G), scalar=core.gates[:, 0:1],
                        in1=x, op0=ALU.mult, op1=ALU.add).then_inc(updated, 1)
                turns(dve, group)

            @block.scalar
            def _(act):
                act.wait_ge(weights, 64)
                norm.scalar_copy(act, 0, 0, 0)

                def group(i, s, it, nxt):
                    act.wait_ge(projected, it + 1)
                    for out, ps, bias, func in ((vT, vps, bvc, ACT.Identity), (v2, vps, bvc, ACT.Square),
                                                (tT, tps, btc, ACT.Identity), (t2, tps, btc, ACT.Square)):
                        last = nc.scalar.activation(out[:, s, :], ps[0:H, :], func, bias=bias[:, 0:1])
                    last.then_inc(squared, 1)
                    if nxt:
                        norm.scalar_copy(act, *nxt)
                    act.wait_ge(summed, it + 1)
                    nc.scalar.activation(tn[:, s, :], tn2[s][:, :], ACT.Sqrt)
                    nc.scalar.activation(vn[:, s, :], vn2[:, 8 * s:8 * s + G], ACT.Sqrt).then_inc(rooted, 1)
                turns(act, group)

            @block.tensor
            def _(pe):
                pe.wait_ge(weights, 64)
                norm.tensor_turn(pe, 0, 0, 0)

                def group(i, s, it, nxt):
                    pe.wait_ge(ctx_landed[s], i * 16 + 16)
                    nc.tensor.matmul(tps[0:H, :], wt[:, :], cT[:, s, :], start=True, stop=True)
                    pe.wait_ge(norm.xT_ready, it + 1)
                    nc.tensor.matmul(vps[0:H, :], wv[:, :], norm.xT[:, s, :], start=True,
                                     stop=True).then_inc(projected, 1)
                    if nxt:
                        norm.tensor_turn(pe, *nxt)
                    pe.wait_ge(squared, it + 1)
                    for j in range(G):
                        js = slice(j * S, (j + 1) * S)
                        nc.tensor.matmul(dots[s][:, js], vT[:, s, js], tT[:, s, js], start=True, stop=True)
                        nc.tensor.matmul(vn2[:, 8 * s + j:8 * s + j + 1], v2[:, s, js], core.ones[0:H, 0:1],
                                         start=True, stop=True)
                    nc.tensor.matmul(tn2[s][:, :], core.ones[0:H, :], t2[:, s, :], start=True,
                                     stop=True).then_inc(summed, 1)
                turns(pe, group)


QUADS = 4
UNITS = G * QUADS


class Attention:

    def __init__(self, core, ctx, layer, score_banks, turn_banks, scale):
        self.core, self.nc, self.scale = core, core.nc, scale
        self.score_banks, self.turn_banks = score_banks, turn_banks
        sb = lambda name, shape: core.sbuf(f"{layer}_{name}", shape, ctx=ctx)
        sem = lambda name: core.sem(ctx, f"{layer}_{name}")
        self.negmax = sb("negmax", [S, 2, 4])
        self.shifted = sb("shifted", [S, 2, 4, S])
        self.weights = sb("probs", [S, 2, 4, S])
        self.turned = sb("probsT", [S, 2, 4, S])
        self.scored, self.maxed, self.shifts = sem("scored"), sem("maxed"), sem("shifts")
        self.exps, self.flips, self.copies, self.weighed = sem("exps"), sem("flips"), sem("copies"), sem("weighed")

    def tensor_scores(self, pe, it, u, matmuls):
        pe.wait_ge(self.shifts, it * UNITS + u + 1)
        matmuls(self.score_banks[u % 2], u // QUADS, u % QUADS).then_inc(self.scored, 1)

    def vector_shift(self, dve, it, u):
        scores = self.score_banks[u % 2][:, :].rearrange("p (h k) -> p h k", h=4)
        negmax = self.negmax[:, u % 2, :]
        dve.wait_ge(self.scored, it * UNITS + u + 1)
        self.nc.vector.tensor_reduce(negmax, scores, AX.X, ALU.max, negate=True).then_inc(self.maxed, 1)
        dve.wait_ge(self.exps, it * UNITS + u + 1)
        dve.wait_ge(self.maxed, it * UNITS + u + 1)
        self.nc.vector.tensor_tensor(self.shifted[:, u % 2], scores,
                                     negmax.unsqueeze(2).to_broadcast([S, 4, S]), ALU.add).then_inc(self.shifts, 1)

    def scalar_exp(self, act, it, u):
        act.wait_ge(self.flips, it * UNITS + u + 1)
        act.wait_ge(self.shifts, it * UNITS + u + 3)
        self.nc.scalar.activation(self.weights[:, u % 2], self.shifted[:, u % 2], ACT.Exp,
                                  scale=self.scale).then_inc(self.exps, 1)

    def tensor_turn(self, pe, it, u):
        pe.wait_ge(self.copies, it * UNITS + u + 1)
        pe.wait_ge(self.exps, it * UNITS + u + 3)
        for h in range(4):
            last = self.nc.tensor.transpose(self.turn_banks[u % 2][:, h * S:(h + 1) * S],
                                            self.weights[:, u % 2, h, :], self.core.ident[:, :])
        last.then_inc(self.flips, 1)

    def scalar_copy(self, act, it, u):
        act.wait_ge(self.weighed, it * UNITS + u + 1)
        act.wait_ge(self.flips, it * UNITS + u + 3)
        self.nc.scalar.activation(self.turned[:, u % 2], self.turn_banks[u % 2][:, :], ACT.Copy).then_inc(self.copies, 1)

    def tensor_weigh(self, pe, it, u, out, values):
        pe.wait_ge(self.copies, it * UNITS + u + 3)
        for k in range(4):
            last = self.nc.tensor.matmul(out(u // QUADS, u % QUADS * 4 + k), self.turned[:, u % 2, k, :],
                                         values(u // QUADS, u % QUADS * 4 + k), start=True, stop=True)
        last.then_inc(self.weighed, 1)

    def vector_start(self, dve):
        dve.sem_inc(self.shifts, 2)

    def scalar_start(self, act):
        act.sem_inc(self.exps, 2)
        act.sem_inc(self.copies, 2)

    def tensor_start(self, pe):
        pe.sem_inc(self.flips, 2)
        pe.sem_inc(self.weighed, 2)


TURN_LAG, WEIGH_LAG = 2, 3


def layer2_attention(core, ctxT, wq, bq, wk, bk, wv, bv_rows, w1, b1, w2, b2_row, head_mask):
    nc, HEADS, DH, FF = core.nc, 16, 8, 2 * D
    with ExitStack() as ctx:
        sb = lambda name, shape: core.sbuf("a1_" + name, shape, ctx=ctx)
        sem = lambda name: core.sem(ctx, "a1_" + name)
        bank = [core.psum(ctx, f"a1_bank{k}", [128, 512]) for k in range(8)]
        norm = Norm(core, ctx, "a1", bank[0])
        att = Attention(core, ctx, "a1", bank[1:3], bank[3:5], DH ** -0.5)
        out_banks, oT_bank = bank[5:7], bank[7]
        wq_s, wk_s, wv_s = sb("wq", [D, D]), sb("wk", [C, D]), sb("wv", [C, D])
        bq_s, bk_s, bv_s = sb("bq", [D, 1]), sb("bk", [D, 1]), sb("bv", [S, D])
        w1_s, b1_s = sb("w1", [D, FF]), sb("b1", [128, 2])
        w2_s, b2_s = sb("w2", [128, 2, D]), sb("b2", [1, D])
        mask = sb("mask", [D, HEADS])
        cT = sb("cT", [C, 2, N])
        qT, kT = sb("qT", [D, 2, N]), sb("kT", [D, 2, N])
        km = sb("k_masked", [D, HEADS, G, S])
        v = sb("v_ones", [S, 2, G, HEADS, DH + 1])
        rsum, o = sb("rsum", [S, 2, HEADS]), sb("o", [S, 2, G, D])
        oT, hT = sb("oT", [D, 2, N]), sb("hT", [128, 2, 2, N])
        weights, ctx_landed, ones_set = sem("weights"), [sem("ctx_landed0"), sem("ctx_landed1")], sem("ones_set")
        k_projected, q_projected, v_projected = sem("k_projected"), sem("q_projected"), sem("v_projected")
        k_ready, q_ready, v_ready, k_masked = sem("k_ready"), sem("q_ready"), sem("v_ready"), sem("k_masked")
        sums_inverted, normalised = sem("sums_inverted"), sem("normalised")
        o_turned, oT_ready, hidden, h_ready, mixed, updated = (
            sem(n) for n in ("o_turned", "oT_ready", "hidden", "h_ready", "mixed", "updated"))
        ctx_groups = ctxT.rearrange("c (i s n) -> c i s n", s=2, n=N)
        loads = [(wq_s[:, :], wq), (wk_s[:, :], wk), (wv_s[:, :], wv), (bq_s[:, :], bq), (bk_s[:, :], bk),
                 (bv_s[:, :], bv_rows), (w1_s[:, :], w1), (b1_s[:, :], b1), (w2_s[:, :, :], w2), (b2_s[:, :], b2_row),
                 (mask[:, :], head_mask)]
        LOADED = 16 * len(loads)

        def out_of(b, h):
            return out_banks[b % 2][:, h * (DH + 1):(h + 1) * (DH + 1)]

        with nc.Block() as block:
            @block.sync
            def _(sp):
                load(sp, weights, loads)

                def group(i, s, it, nxt):
                    sp.wait_ge(updated, it + 1)
                    sp.dma_start(cT[:, s, :], ctx_groups[:, i, s, :]).then_inc(ctx_landed[s], 16)
                turns(sp, group)

            @block.gpsimd
            def _(pool):
                nc.gpsimd.memset(v[:, :, :, :, :], 1.0).then_inc(ones_set, 1)
                turns(pool, lambda i, s, it, nxt: norm.gpsimd_rstd(pool, i, s, it))

            @block.vector
            def _(dve):
                dve.sem_inc(updated, 2)
                dve.sem_inc(normalised, 2)
                att.vector_start(dve)
                norm.vector(dve, 0, 0, 0)
                dve.wait_ge(weights, LOADED)
                dve.wait_ge(ones_set, 1)

                def normalise(s, it, b):
                    heads = out_banks[b % 2][:, 0:HEADS * (DH + 1)].rearrange("p (h e) -> p h e", h=HEADS)
                    dve.wait_ge(att.weighed, it * UNITS + 4 * b + 4 + 2)
                    nc.vector.reciprocal(rsum[:, b % 2, :], heads[:, :, DH]).then_inc(sums_inverted, 1)
                    dve.wait_ge(sums_inverted, it * G + b + 1)
                    nc.vector.tensor_tensor(o[:, s, b, :].rearrange("p (h e) -> p h e", h=HEADS), heads[:, :, 0:DH],
                                            rsum[:, b % 2, :].unsqueeze(2).to_broadcast([S, HEADS, DH]),
                                            ALU.mult).then_inc(normalised, 1)

                def group(i, s, it, nxt):
                    dve.wait_ge(v_projected, it + 1)
                    nc.vector.tensor_tensor(
                        v[:, s, :, :, 0:DH], bank[3][:, :].rearrange("p (b h e) -> p b h e", b=G, h=HEADS),
                        bv_s[:, :].rearrange("p (h e) -> p h e", h=HEADS).unsqueeze(1).to_broadcast([S, G, HEADS, DH]),
                        ALU.add).then_inc(v_ready, 1)
                    dve.wait_ge(k_ready, it + 1)
                    for h in range(HEADS):
                        nc.vector.tensor_scalar(km[:, h, :, :], kT[:, s, :].rearrange("p (b k) -> p b k", b=G),
                                                mask[:, h:h + 1], None, ALU.mult).then_inc(k_masked, 1)
                    for step in range(UNITS + WEIGH_LAG + 1):
                        if step < UNITS:
                            att.vector_shift(dve, it, step)
                        if step >= 4 + WEIGH_LAG and (step - WEIGH_LAG) % 4 == 0:
                            normalise(s, it, (step - WEIGH_LAG) // 4 - 1)
                        if step == 8 and nxt:
                            norm.vector_stats(dve, *nxt)
                        if step == 12 and nxt:
                            norm.vector_normalise(dve, *nxt)
                    dve.wait_ge(mixed, it + 1)
                    x = core.X_groups[:, i, s]
                    nc.vector.scalar_tensor_tensor(
                        out=x, in0=oT_bank[:, :].rearrange("p (j d) -> p j d", j=G), scalar=core.gates[:, 1:2],
                        in1=x, op0=ALU.mult, op1=ALU.add).then_inc(updated, 1)
                turns(dve, group)

            @block.scalar
            def _(act):
                att.scalar_start(act)
                act.wait_ge(weights, LOADED)
                norm.scalar_copy(act, 0, 0, 0)

                def group(i, s, it, nxt):
                    act.wait_ge(k_projected, it + 1)
                    nc.scalar.activation(kT[:, s, :], bank[1][:, :], ACT.Identity, bias=bk_s[:, 0:1]).then_inc(k_ready, 1)
                    act.wait_ge(q_projected, it + 1)
                    nc.scalar.activation(qT[:, s, :], bank[2][:, :], ACT.Identity, bias=bq_s[:, 0:1]).then_inc(q_ready, 1)
                    for step in range(UNITS + 1):
                        if step < UNITS:
                            att.scalar_exp(act, it, step)
                        if step >= 1:
                            att.scalar_copy(act, it, step - 1)
                        if step == 15 and nxt:
                            norm.scalar_copy(act, *nxt)
                    act.wait_ge(o_turned, it + 1)
                    nc.scalar.activation(oT[:, s, :], oT_bank[:, :], ACT.Copy).then_inc(oT_ready, 1)
                    for f in range(2):
                        act.wait_ge(hidden, it * 2 + f + 1)
                        nc.scalar.activation(hT[:, s, f, :], bank[1 + f][:, :], ACT.Relu,
                                             bias=b1_s[:, f:f + 1]).then_inc(h_ready, 1)
                turns(act, group)

            @block.tensor
            def _(pe):
                att.tensor_start(pe)
                pe.wait_ge(weights, LOADED)
                norm.tensor_turn(pe, 0, 0, 0)

                def group(i, s, it, nxt):
                    pe.wait_ge(ctx_landed[s], i * 16 + 16)
                    nc.tensor.matmul(bank[1][:, :], wk_s[:, :], cT[:, s, :], start=True, stop=True).then_inc(k_projected, 1)
                    pe.wait_ge(norm.xT_ready, it + 1)
                    nc.tensor.matmul(bank[2][:, :], wq_s[:, :], norm.xT[:, s, :], start=True,
                                     stop=True).then_inc(q_projected, 1)
                    for b in range(G):
                        last = nc.tensor.matmul(bank[3][:, b * S:(b + 1) * S], cT[:, s, b * S:(b + 1) * S], wv_s[:, :],
                                                start=True, stop=True)
                    last.then_inc(v_projected, 1)
                    pe.wait_ge(q_ready, it + 1)
                    pe.wait_ge(v_ready, it + 1)

                    def scores(ps, b, quad):
                        if b == 0:
                            pe.wait_ge(k_masked, it * HEADS + 4 * quad + 4)
                        return nc.tensor.matmul(ps[:, :], qT[:, s, b * S:(b + 1) * S],
                                                km[:, 4 * quad:4 * quad + 4, b, :], start=True, stop=True)

                    for step in range(UNITS + WEIGH_LAG):
                        if step < UNITS:
                            att.tensor_scores(pe, it, step, scores)
                        if 0 <= step - TURN_LAG < UNITS:
                            att.tensor_turn(pe, it, step - TURN_LAG)
                        if step >= WEIGH_LAG:
                            u = step - WEIGH_LAG
                            if u % 4 == 0:
                                pe.wait_ge(normalised, it * G + u // 4 + 1)
                            att.tensor_weigh(pe, it, u, out_of, lambda b, h: v[:, s, b, h, :])
                        if step == 14 and nxt:
                            norm.tensor_turn(pe, *nxt)
                    pe.wait_ge(normalised, it * G + G + 2)
                    for b in range(G):
                        last = nc.tensor.transpose(oT_bank[:, b * S:(b + 1) * S], o[:, s, b, :], core.ident[:, :])
                    last.then_inc(o_turned, 1)
                    pe.wait_ge(oT_ready, it + 1)
                    for f in range(2):
                        nc.tensor.matmul(bank[1 + f][:, :], w1_s[:, f * 128:(f + 1) * 128], oT[:, s, :], start=True,
                                         stop=True).then_inc(hidden, 1)
                    pe.wait_ge(h_ready, it * 2 + 2)
                    for b in range(G):
                        nc.tensor.matmul(oT_bank[:, b * S:(b + 1) * S], core.ones[0:1, :], b2_s[0:1, :],
                                         start=True, stop=False)
                        for f in range(2):
                            last = nc.tensor.matmul(oT_bank[:, b * S:(b + 1) * S], hT[:, s, f, b * S:(b + 1) * S],
                                                    w2_s[:, f, :], start=False, stop=f == 1)
                    last.then_inc(mixed, 1)
                turns(pe, group)



class Ring:

    def __init__(self, core, ctx, layer, banks, uses):
        self.nc, self.banks, self.half = core.nc, banks, uses // 2
        sem = lambda name: core.sem(ctx, f"{layer}_{name}")
        self.full = [sem("ring_full_even"), sem("ring_full_odd")]
        self.emptied = [sem("ring_emptied_by_scalar"), sem("ring_emptied_by_vector")]

    def tensor_free(self, pe, it, n):
        pe.wait_ge(self.emptied[n % 2], it * self.half + (n - 4) // 2 + 1)
        return self.banks[n % 4]

    def tensor_wait_emptied(self, pe, it, uses):
        for k in range(2):
            pe.wait_ge(self.emptied[k], it * self.half + uses // 2)

    def scalar_empty(self, act, it, n, out):
        act.wait_ge(self.full[0], it * self.half + n // 2 + 1)
        self.nc.scalar.activation(out, self.view(n, out), ACT.Copy).then_inc(self.emptied[0], 1)

    def vector_empty(self, dve, it, n, out):
        dve.wait_ge(self.full[1], it * self.half + n // 2 + 1)
        self.nc.vector.tensor_copy(out, self.view(n, out)).then_inc(self.emptied[1], 1)

    def view(self, n, out):
        bank = self.banks[n % 4][:, :]
        return bank if len(out.shape) == 2 else bank.rearrange("p (h e) -> p h e", h=out.shape[1])


def layer6_attention(core, ctxT, wq, wk, wv, wo, bo_row):
    nc, HEADS, DH = core.nc, 16, 64
    TILES = HEADS * DH // 128
    PROJECTIONS, USES = 3 * TILES, 4 * TILES
    BANK_HEADS = (6, 5, 5)
    FIRST = (0, 6, 11)
    with ExitStack() as ctx:
        sb = lambda name, shape: core.sbuf("a3_" + name, shape, ctx=ctx)
        sem = lambda name: core.sem(ctx, "a3_" + name)
        bank = [core.psum(ctx, f"a3_bank{k}", [128, 512]) for k in range(8)]
        norm = Norm(core, ctx, "a3", bank[0])
        att = Attention(core, ctx, "a3", bank[1:3], bank[3:5], DH ** -0.5)
        ring = Ring(core, ctx, "a3", bank[1:5], USES)
        out_banks, mix_bank = bank[5:8], bank[0]
        wq_s, wk_s, wv_s = sb("wq", [D, HEADS * DH]), sb("wk", [C, HEADS * DH]), sb("wv", [C, HEADS * DH])
        wo_s, bo_s = sb("wo", [128, TILES, D]), sb("bo", [1, D])
        cT = sb("cT", [C, 2, N])
        qT, kT = sb("qT", [128, TILES, N]), sb("kT", [128, TILES, N])
        v = sb("v_ones", [S, G, HEADS, DH + 1])
        rsum, o, oT = sb("rsum", [S, HEADS]), sb("o", [S, G, HEADS * DH]), sb("oT", [128, TILES, N])
        weights, ctx_landed, ones_set = sem("weights"), [sem("ctx_landed0"), sem("ctx_landed1")], sem("ones_set")
        sums_inverted, normalised, mixed, updated = (
            sem(n) for n in ("sums_inverted", "normalised", "mixed", "updated"))
        ctx_groups = ctxT.rearrange("c (i s n) -> c i s n", s=2, n=N)
        loads = [(wq_s[:, :], wq), (wk_s[:, :], wk), (wv_s[:, :], wv), (wo_s[:, :, :], wo), (bo_s[:, :], bo_row)]
        LOADED = 16 * len(loads)

        def out_of(b, h):
            k = 0 if h < 6 else 1 if h < 11 else 2
            return out_banks[k][:, (h - FIRST[k]) * (DH + 1):(h - FIRST[k] + 1) * (DH + 1)]

        def ring_out(n):
            if n < TILES:
                return qT[:, n, :]
            if n < 2 * TILES:
                return kT[:, n - TILES, :]
            if n < 3 * TILES:
                b, half = divmod(n - 2 * TILES, 2)
                return v[:, b, 8 * half:8 * half + 8, 0:DH]
            return oT[:, n - 3 * TILES, :]

        with nc.Block() as block:
            @block.sync
            def _(sp):
                load(sp, weights, loads)

                def group(i, s, it, nxt):
                    sp.wait_ge(updated, it + 1)
                    sp.dma_start(cT[:, s, :], ctx_groups[:, i, s, :]).then_inc(ctx_landed[s], 16)
                turns(sp, group)

            @block.gpsimd
            def _(pool):
                nc.gpsimd.memset(v[:, :, :, :], 1.0).then_inc(ones_set, 1)
                turns(pool, lambda i, s, it, nxt: norm.gpsimd_rstd(pool, i, s, it))

            @block.vector
            def _(dve):
                dve.sem_inc(updated, 2)
                dve.sem_inc(normalised, 1)
                att.vector_start(dve)
                norm.vector(dve, 0, 0, 0)
                dve.wait_ge(ones_set, 1)

                def normalise(it, b):
                    heads = [out_banks[k][:, 0:c * (DH + 1)].rearrange("p (h e) -> p h e", h=c)
                             for k, c in enumerate(BANK_HEADS)]
                    dve.wait_ge(att.weighed, it * UNITS + 4 * b + 4 + 2)
                    for k, c in enumerate(BANK_HEADS):
                        last = nc.vector.reciprocal(rsum[:, FIRST[k]:FIRST[k] + c], heads[k][:, :, DH])
                    last.then_inc(sums_inverted, 1)
                    dve.wait_ge(sums_inverted, it * G + b + 1)
                    for k, c in enumerate(BANK_HEADS):
                        last = nc.vector.tensor_tensor(
                            o[:, b, FIRST[k] * DH:(FIRST[k] + c) * DH].rearrange("p (h e) -> p h e", h=c),
                            heads[k][:, :, 0:DH],
                            rsum[:, FIRST[k]:FIRST[k] + c].unsqueeze(2).to_broadcast([S, c, DH]), ALU.mult)
                    last.then_inc(normalised, 1)

                def group(i, s, it, nxt):
                    for n in range(1, PROJECTIONS, 2):
                        ring.vector_empty(dve, it, n, ring_out(n))
                    for step in range(UNITS + WEIGH_LAG + 1):
                        if step < UNITS:
                            att.vector_shift(dve, it, step)
                        if step >= 4 + WEIGH_LAG and (step - WEIGH_LAG) % 4 == 0:
                            normalise(it, (step - WEIGH_LAG) // 4 - 1)
                        if step == 8 and nxt:
                            norm.vector_stats(dve, *nxt)
                        if step == 12 and nxt:
                            norm.vector_normalise(dve, *nxt)
                    for n in range(PROJECTIONS + 1, USES, 2):
                        ring.vector_empty(dve, it, n, ring_out(n))
                    dve.wait_ge(mixed, it + 1)
                    x = core.X_groups[:, i, s]
                    nc.vector.scalar_tensor_tensor(
                        out=x, in0=mix_bank[:, :].rearrange("p (j d) -> p j d", j=G), scalar=core.gates[:, 3:4],
                        in1=x, op0=ALU.mult, op1=ALU.add).then_inc(updated, 1)
                turns(dve, group)

            @block.scalar
            def _(act):
                att.scalar_start(act)
                norm.scalar_copy(act, 0, 0, 0)
                act.wait_ge(ones_set, 1)

                def group(i, s, it, nxt):
                    for n in range(0, PROJECTIONS, 2):
                        ring.scalar_empty(act, it, n, ring_out(n))
                    for step in range(UNITS + 1):
                        if step < UNITS:
                            att.scalar_exp(act, it, step)
                        if step >= 1:
                            att.scalar_copy(act, it, step - 1)
                        if step == 15 and nxt:
                            norm.scalar_copy(act, *nxt)
                    for n in range(PROJECTIONS, USES, 2):
                        ring.scalar_empty(act, it, n, ring_out(n))
                turns(act, group)

            @block.tensor
            def _(pe):
                att.tensor_start(pe)
                pe.wait_ge(weights, LOADED)
                norm.tensor_turn(pe, 0, 0, 0)

                def group(i, s, it, nxt):
                    pe.wait_ge(ctx_landed[s], i * 16 + 16)
                    pe.wait_ge(norm.xT_ready, it + 1)
                    for n in range(PROJECTIONS):
                        ps = ring.tensor_free(pe, it, n) if n >= 4 else ring.banks[n]
                        kind, t = divmod(n, TILES)
                        if kind < 2:
                            w, tokens = ((wq_s, norm.xT), (wk_s, cT))[kind]
                            mm = nc.tensor.matmul(ps[:, :], w[:, t * 128:(t + 1) * 128], tokens[:, s, :],
                                                  start=True, stop=True)
                        else:
                            b, half = divmod(t, 2)
                            mm = nc.tensor.matmul(ps[:, :], cT[:, s, b * S:(b + 1) * S],
                                                  wv_s[:, half * 512:half * 512 + 512], start=True, stop=True)
                        mm.then_inc(ring.full[n % 2], 1)
                    ring.tensor_wait_emptied(pe, it, PROJECTIONS)

                    def scores(ps, b, quad):
                        r = 64 * (quad % 2)
                        for k in range(4):
                            t = 4 * (quad // 2) + k
                            last = nc.tensor.matmul(ps[:, k * S:(k + 1) * S], qT[r:r + 64, t, b * S:(b + 1) * S],
                                                    kT[r:r + 64, t, b * S:(b + 1) * S], start=True, stop=True)
                        return last

                    for step in range(UNITS + WEIGH_LAG):
                        if step < UNITS:
                            att.tensor_scores(pe, it, step, scores)
                        if 0 <= step - TURN_LAG < UNITS:
                            att.tensor_turn(pe, it, step - TURN_LAG)
                        if step >= WEIGH_LAG:
                            u = step - WEIGH_LAG
                            if u % 4 == 0:
                                pe.wait_ge(normalised, it * G + u // 4 + 1)
                            att.tensor_weigh(pe, it, u, out_of, lambda b, h: v[:, b, h, :])
                        if step == 14 and nxt:
                            pe.wait_ge(updated, it + 2)
                            norm.tensor_turn(pe, *nxt)
                    pe.wait_ge(normalised, it * G + G + 1)
                    for n in range(PROJECTIONS, USES):
                        t = n - PROJECTIONS
                        ps = ring.tensor_free(pe, it, n) if t >= 4 else ring.banks[n % 4]
                        for b in range(G):
                            last = nc.tensor.transpose(ps[:, b * S:(b + 1) * S], o[:, b, t * 128:(t + 1) * 128],
                                                       core.ident[:, :])
                        last.then_inc(ring.full[n % 2], 1)
                    ring.tensor_wait_emptied(pe, it, USES)
                    if nxt:
                        pe.wait_ge(norm.xT_ready, it + 2)
                    for b in range(G):
                        bs = slice(b * S, (b + 1) * S)
                        nc.tensor.matmul(mix_bank[:, bs], core.ones[0:1, :], bo_s[0:1, :], start=True, stop=False)
                        for t in range(TILES):
                            last = nc.tensor.matmul(mix_bank[:, bs], oT[:, t, bs], wo_s[:, t, :], start=False,
                                                    stop=t == TILES - 1)
                    last.then_inc(mixed, 1)
                turns(pe, group)


def layer7_selected_gelu(core, w_router, w_block):
    nc, SELECTED = core.nc, S * 3 // 4
    ROUNDS = SELECTED // 8
    with ExitStack() as ctx:
        sb = lambda name, shape: core.sbuf("f3_" + name, shape, ctx=ctx)
        sem = lambda name: core.sem(ctx, "f3_" + name)
        bank = [core.psum(ctx, f"f3_bank{k}", [128, 512]) for k in range(8)]
        norm = Norm(core, ctx, "f3", bank[0])
        wr, wb = sb("wr", [D, 1]), sb("wb", [D, D])
        scores = sb("scores", [S, B])
        scores_v = scores[:, :].rearrange("p (i s j) -> p i s j", s=2, j=G)
        gelu, diff = sb("gelu", [S, 2, G, D]), sb("diff", [S, B, D])
        diff_v = diff[:, :, :].rearrange("p (i s j) d -> p i s j d", s=2, j=G)
        cand, top8, selected, pick = sb("cand", [B, 2, S]), sb("top8", [B, 8]), sb("selected", [B, S]), sb("pick", [S, B])
        weights, scored, score_kept, gelu_done, diff_done, updated = (
            sem(n) for n in ("weights", "scored", "score_kept", "gelu_done", "diff_done", "updated"))
        turned, chain, selected_done, selected_turned, pick_done = (
            sem(n) for n in ("scores_turned", "ranking", "selected_done", "selected_turned", "pick_done"))
        with nc.Block() as block:
            @block.sync
            def _(sp):
                load(sp, weights, [(wr[:, :], w_router), (wb[:, :], w_block)])

            @block.gpsimd
            def _(pool):
                turns(pool, lambda i, s, it, nxt: norm.gpsimd_rstd(pool, i, s, it))

            @block.vector
            def _(dve):
                dve.sem_inc(diff_done, 2)
                norm.vector(dve, 0, 0, 0)

                def group(i, s, it, nxt):
                    if nxt:
                        norm.vector(dve, *nxt)
                    x = core.X_groups[:, i, s]
                    dve.wait_ge(scored, it + 1)
                    nc.vector.tensor_copy(scores_v[:, i, s, :], bank[4 + s][:, 0:G]).then_inc(score_kept, 1)
                    dve.wait_ge(gelu_done, it + 1)
                    nc.vector.tensor_tensor(diff_v[:, i, s], gelu[:, s], norm.xn[:, s], ALU.subtract)\
                        .then_inc(diff_done, 1)
                    nc.vector.scalar_tensor_tensor(out=x, in0=norm.xn[:, s], scalar=core.gates[:, 7:8], in1=x,
                                                   op0=ALU.mult, op1=ALU.add).then_inc(updated, 1)
                turns(dve, group)
                dve.wait_ge(turned, 1)
                nc.vector.tensor_copy(cand[:, 0, :], bank[6][0:B, 0:S]).then_inc(chain, 1)
                for r in range(ROUNDS):
                    dve.wait_ge(chain, 2 * r + 1)
                    nc.vector.max(top8[:, :], cand[:, r % 2, :]).then_inc(chain, 1)
                    dve.wait_ge(chain, 2 * r + 2)
                    nc.vector.match_replace(cand[:, 1 - r % 2, :], top8[:, :], cand[:, r % 2, :], -BIG)\
                        .then_inc(chain, 1)
                dve.wait_ge(chain, 2 * ROUNDS + 1)
                nc.vector.tensor_scalar(selected[:, :], cand[:, ROUNDS % 2, :], -BIG, None, ALU.is_equal)\
                    .then_inc(selected_done, 1)
                dve.wait_ge(selected_turned, 1)
                nc.vector.tensor_scalar(pick[:, :], bank[7][:, 0:B], core.gates[:, 7:8], None, ALU.mult)\
                    .then_inc(pick_done, 1)
                dve.wait_ge(pick_done, 1)
                dve.wait_ge(updated, GROUPS)
                dve.wait_ge(diff_done, GROUPS + 2)
                for b in range(B):
                    nc.vector.scalar_tensor_tensor(out=core.X[:, b, :], in0=diff[:, b, :], scalar=pick[:, b:b + 1],
                                                   in1=core.X[:, b, :], op0=ALU.mult, op1=ALU.add)

            @block.scalar
            def _(act):
                norm.scalar_copy(act, 0, 0, 0)

                def group(i, s, it, nxt):
                    if nxt:
                        norm.scalar_copy(act, *nxt)
                    act.wait_ge(diff_done, it + 1)
                    act.wait_ge(scored, it + 1)
                    nc.scalar.activation(gelu[:, s].rearrange("p j d -> p (j d)"), bank[2 + s][:, :],
                                         ACT.Gelu_apprx_tanh).then_inc(gelu_done, 1)
                turns(act, group)

            @block.tensor
            def _(pe):
                pe.wait_ge(weights, 32)
                norm.tensor_turn(pe, 0, 0, 0)

                def group(i, s, it, nxt):
                    pe.wait_ge(norm.xT_ready, it + 1)
                    if nxt:
                        norm.tensor_turn(pe, *nxt)
                    pe.wait_ge(diff_done, it + 1)
                    for b in range(G):
                        xT = norm.xT[:, s, b * S:(b + 1) * S]
                        nc.tensor.matmul(bank[2 + s][:, b * S:(b + 1) * S], xT, wb[:, :], start=True, stop=True)
                        last = nc.tensor.matmul(bank[4 + s][:, b:b + 1], xT, wr[:, :], start=True, stop=True)
                    last.then_inc(scored, 1)
                turns(pe, group)
                pe.wait_ge(score_kept, GROUPS)
                nc.tensor.transpose(bank[6][0:B, 0:S], scores[:, :], core.ident[:, :]).then_inc(turned, 1)
                pe.wait_ge(selected_done, 1)
                nc.tensor.transpose(bank[7][:, 0:B], selected[:, :], core.ident[0:B, 0:B]).then_inc(selected_turned, 1)


def layer5_experts(core, gate_wT, w1T, b1, w2T, b2):
    nc, E, TOP = core.nc, 8, 2
    CAPACITY = int(1.25 * B * S / E)
    PAD = 8 - TOP
    with ExitStack() as ctx:
        sb = lambda name, shape: core.sbuf("f2_" + name, shape, ctx=ctx)
        sem = lambda name: core.sem(ctx, "f2_" + name)
        bank = [core.psum(ctx, f"f2_bank{k}", [128, 512]) for k in range(8)]
        norm = Norm(core, ctx, "f2", bank[0])
        gw, w1, b1_s, w2, b2_s = (sb("gw", [D, E]), sb("w1", [D, E, D]), sb("b1", [D, E]), sb("w2", [D, E, D]),
                                  sb("b2", [E, D]))
        xT_all = sb("xT_all", [D, B * S])
        xT_groups = xT_all[:, :].rearrange("d (i s n) -> d i s n", s=2, n=N)
        logits = sb("logits", [S, B, E])
        logits_v = logits[:, :, :].rearrange("p (i s j) e -> p i s (j e)", s=2, j=G)
        negmax, shifted, exps, sums, rsums = (sb("negmax", [S, B]), sb("shifted", [S, B, E]), sb("exps", [S, B, E]),
                                              sb("sums", [S, B]), sb("rsums", [S, B]))
        cand, top8, marked = sb("cand", [S, B, PAD + E]), sb("top8", [S, B, 8]), sb("marked", [S, B, PAD + E])
        chosen, counts, keep = sb("chosen", [S, B, E]), sb("counts", [S, E]), sb("keep", [S, E])
        w, wk, wg = sb("w", [S, B, E]), sb("w_kept", [S, B, E]), sb("w_gated", [S, B, E])
        wg_v = wg[:, :, :].rearrange("p (i s j) e -> p i s j e", s=2, j=G)
        wT = sb("wT", [E, B * S])
        h = sb("h", [D, 2, N])
        weights, scored, kept, all_turned = sem("weights"), sem("scored"), sem("logits_kept"), sem("xT_kept")
        chain, exp_done, ready, counts_in, counted, wg_done = (
            sem(n) for n in ("weighting", "exp_done", "ready_for_exp", "counts_in", "counted", "wg_done"))
        wT_turned, wT_kept, biased, bias_added = (sem(n) for n in ("wT_turned", "wT_kept", "biased", "bias_added"))
        hidden, activated, mixed, added = (sem(n) for n in ("hidden", "activated", "mixed", "added"))
        loads = [(gw[:, :], gate_wT), (w1[:, :, :], w1T), (b1_s[:, :], b1), (w2[:, :, :], w2T), (b2_s[:, :], b2)]
        LOADED = 16 * len(loads)
        with nc.Block() as block:
            @block.sync
            def _(sp):
                load(sp, weights, loads)

            @block.gpsimd
            def _(pool):
                turns(pool, lambda i, s, it, nxt: norm.gpsimd_rstd(pool, i, s, it))

            @block.scalar
            def _(act):
                norm.scalar_copy(act, 0, 0, 0)

                def group(i, s, it, nxt):
                    act.wait_ge(norm.xT_ready, it + 1)
                    nc.scalar.activation(xT_groups[:, i, s, :], norm.xT[:, s, :], ACT.Copy).then_inc(all_turned, 1)
                    if nxt:
                        norm.scalar_copy(act, *nxt)
                turns(act, group)
                act.wait_ge(ready, 1)
                nc.scalar.activation(exps[:, :, :], shifted[:, :, :], ACT.Exp).then_inc(exp_done, 1)
                for g in range(GROUPS):
                    act.wait_ge(wT_turned, g + 1)
                    nc.scalar.activation(wT[:, g * N:(g + 1) * N], bank[2 + g % 2][0:E, :], ACT.Copy).then_inc(wT_kept, 1)

            @block.vector
            def _(dve):
                norm.vector(dve, 0, 0, 0)

                def group(i, s, it, nxt):
                    if nxt:
                        norm.vector(dve, *nxt)
                    dve.wait_ge(scored, it + 1)
                    nc.vector.tensor_copy(logits_v[:, i, s, :], bank[4 + s][:, 0:G * E]).then_inc(kept, 1)
                turns(dve, group)
                wide = lambda a: a.unsqueeze(2).to_broadcast([S, B, E])
                dve.wait_ge(kept, GROUPS)
                nc.vector.tensor_reduce(negmax[:, :], logits[:, :, :], AX.X, ALU.max, negate=True).then_inc(chain, 1)
                dve.wait_ge(chain, 1)
                nc.vector.tensor_tensor(shifted[:, :, :], logits[:, :, :], wide(negmax[:, :]), ALU.add).then_inc(ready, 1)
                nc.vector.memset(cand[:, :, :], BIG).then_inc(chain, 1)
                dve.wait_ge(exp_done, 1)
                nc.vector.tensor_reduce(sums[:, :], exps[:, :, :], AX.X, ALU.add).then_inc(chain, 1)
                dve.wait_ge(chain, 3)
                nc.vector.reciprocal(rsums[:, :], sums[:, :]).then_inc(chain, 1)
                dve.wait_ge(chain, 4)
                nc.vector.tensor_tensor(cand[:, :, PAD:], exps[:, :, :], wide(rsums[:, :]), ALU.mult).then_inc(chain, 1)
                dve.wait_ge(chain, 5)
                for b in range(B):
                    nc.vector.max(top8[:, b, :], cand[:, b, :]).then_inc(chain, 1)
                dve.wait_ge(chain, 5 + B)
                for b in range(B):
                    nc.vector.match_replace(marked[:, b, :], top8[:, b, :], cand[:, b, :], -BIG).then_inc(chain, 1)
                dve.wait_ge(chain, 5 + 2 * B)
                nc.vector.tensor_scalar(chosen[:, :, :], marked[:, :, PAD:], -BIG, None, ALU.is_equal).then_inc(chain, 1)
                dve.wait_ge(chain, 6 + 2 * B)
                nc.vector.tensor_reduce(counts[:, :], chosen[:, :, :].rearrange("p b e -> p e b"), AX.X,
                                        ALU.add).then_inc(counts_in, 1)
                nc.vector.tensor_tensor(w[:, :, :], chosen[:, :, :], cand[:, :, PAD:], ALU.mult).then_inc(chain, 1)
                dve.wait_ge(counted, 1)
                nc.vector.tensor_scalar(keep[:, :], bank[6][:, 0:E], float(CAPACITY), None, ALU.is_le).then_inc(chain, 1)
                dve.wait_ge(chain, 8 + 2 * B)
                nc.vector.tensor_tensor(wk[:, :, :], w[:, :, :], keep[:, :].unsqueeze(1).to_broadcast([S, B, E]),
                                        ALU.mult).then_inc(chain, 1)
                dve.wait_ge(chain, 9 + 2 * B)
                nc.vector.tensor_scalar(wg[:, :, :], wk[:, :, :], core.gates[:, 6:7], None, ALU.mult).then_inc(wg_done, 1)
                for g in range(GROUPS):
                    x = core.X[:, g * G:(g + 1) * G, :]
                    dve.wait_ge(biased, g + 1)
                    nc.vector.tensor_tensor(x, bank[4 + g % 2][:, :].rearrange("p (j d) -> p j d", j=G), x,
                                            ALU.add).then_inc(bias_added, 1)

            @block.tensor
            def _(pe):
                pe.wait_ge(weights, LOADED)
                norm.tensor_turn(pe, 0, 0, 0)

                def group(i, s, it, nxt):
                    pe.wait_ge(norm.xT_ready, it + 1)
                    for b in range(G):
                        last = nc.tensor.matmul(bank[4 + s][:, b * E:(b + 1) * E], norm.xT[:, s, b * S:(b + 1) * S],
                                                gw[:, :], start=True, stop=True)
                    last.then_inc(scored, 1)
                    if nxt:
                        pe.wait_ge(kept, it + 1)
                        pe.wait_ge(all_turned, it + 1)
                        norm.tensor_turn(pe, *nxt)
                turns(pe, group)
                pe.wait_ge(counts_in, 1)
                nc.tensor.matmul(bank[6][:, 0:E], core.ones[:, :], counts[:, :], start=True, stop=True)\
                    .then_inc(counted, 1)
                pe.wait_ge(wg_done, 1)

                def turn(g):
                    if g >= 2:
                        pe.wait_ge(wT_kept, g - 1)
                    for j in range(G):
                        last = nc.tensor.transpose(bank[2 + g % 2][0:E, j * S:(j + 1) * S], wg[:, g * G + j, :],
                                                   core.ident[:, :])
                    last.then_inc(wT_turned, 1)

                turn(0)
                for g in range(GROUPS):
                    if g + 1 < GROUPS:
                        turn(g + 1)
                    pe.wait_ge(wT_kept, g + 1)
                    if g >= 2:
                        pe.wait_ge(bias_added, g - 1)
                    for j in range(G):
                        b = g * G + j
                        last = nc.tensor.matmul(bank[4 + g % 2][:, j * S:(j + 1) * S], wT[:, b * S:(b + 1) * S],
                                                b2_s[:, :], start=True, stop=True)
                    last.then_inc(biased, 1)

        with nc.Block() as block:
            @block.tensor
            def _(pe):
                pe.sem_inc(mixed, 2)

                def expand(i, s, it, e):
                    pe.wait_ge(activated, it * E + e + 1)
                    nc.tensor.matmul(bank[e % 2][:, :], w1[:, e, :], xT_groups[:, i, s, :], start=True,
                                     stop=True).then_inc(hidden, 1)

                expand(0, 0, 0, 0)

                def group(i, s, it, nxt):
                    for e in range(E):
                        if e + 1 < E:
                            expand(i, s, it, e + 1)
                        elif nxt:
                            expand(nxt[0], nxt[1], nxt[2], 0)
                        pe.wait_ge(activated, it * E + e + 3)
                        pe.wait_ge(added, it * E + e + 1)
                        for j in range(G):
                            last = nc.tensor.matmul(bank[2 + e % 2][:, j * S:(j + 1) * S],
                                                    h[:, e % 2, j * S:(j + 1) * S], w2[:, e, :], start=True, stop=True)
                        last.then_inc(mixed, 1)
                turns(pe, group)

            @block.scalar
            def _(act):
                act.sem_inc(activated, 2)

                def group(i, s, it, nxt):
                    for e in range(E):
                        act.wait_ge(mixed, it * E + e + 1)
                        act.wait_ge(hidden, it * E + e + 1)
                        nc.scalar.activation(h[:, e % 2, :], bank[e % 2][:, :], ACT.Silu,
                                             bias=b1_s[:, e:e + 1]).then_inc(activated, 1)
                turns(act, group)

            @block.vector
            def _(dve):
                dve.sem_inc(added, 2)

                def group(i, s, it, nxt):
                    x = core.X_groups[:, i, s]
                    for e in range(E):
                        dve.wait_ge(mixed, it * E + e + 3)
                        if e >= 1:
                            dve.wait_ge(added, it * E + e + 2)
                        for j in range(G):
                            last = nc.vector.scalar_tensor_tensor(
                                out=x[:, j, :], in0=bank[2 + e % 2][:, j * S:(j + 1) * S],
                                scalar=wg_v[:, i, s, j, e:e + 1], in1=x[:, j, :], op0=ALU.mult, op1=ALU.add)
                        last.then_inc(added, 1)
                turns(dve, group)


def layer3_experts(core, routerT, bias_rows, guT, downT):
    nc, ER, EZ, TOP, I, SCALE = core.nc, 32, 8, 6, 64, 2.5
    E, OCT, PAD = ER + EZ, 8, 8 - TOP
    PER = ER // OCT
    LAG, DOWN_LAG = 3, 4
    with ExitStack() as ctx:
        sb = lambda name, shape: core.sbuf("f1_" + name, shape, ctx=ctx)
        sem = lambda name: core.sem(ctx, "f1_" + name)
        norm_bank = core.psum(ctx, "f1_norm_bank", [128, 512])
        acc = core.psum(ctx, "f1_acc", [128, 512])
        turn_banks = [core.psum(ctx, f"f1_turn{k}", [128, 512]) for k in range(2)]
        gu_ps = [core.psum(ctx, f"f1_gu{k}", [128, 1024]) for k in range(2)]
        norm = Norm(core, ctx, "f1", norm_bank)
        rw, bias, gu_w, down_w = (sb("router", [D, E]), sb("bias", [S, E]), sb("gate_up", [D, ER, 2 * I]),
                                  sb("down", [2 * I, ER // 2, D]))
        gscale = sb("gate_scale", [128, 1])
        negmax, shifted, exps = sb("negmax", [S, G]), sb("shifted", [S, G, E]), sb("exps", [S, G, E])
        sums, rsums, probs = sb("sums", [S, G]), sb("rsums", [S, G]), sb("probs", [S, G, E])
        cand, top8, marked = sb("cand", [S, G, PAD + E]), sb("top8", [S, G, 8]), sb("marked", [S, G, PAD + E])
        chosen, w, wz = sb("chosen", [S, G, E]), sb("w", [S, 2, G, E]), sb("w_identity", [S, 2, G])
        silu, gated, h, hT = (sb("silu", [S, 2, OCT, I]), sb("gated", [S, 2, OCT, I]), sb("h", [S, 2, OCT, I]),
                              sb("hT", [2 * I, 2, OCT // 2, S]))
        weights, logits_in, shift_done, exp_done, routed, chain = (
            sem(n) for n in ("weights", "logits_in", "shift_done", "exp_done", "routed", "routing"))
        gu_done, silus, gateds, weighted, flips, copies, downs = (
            sem(n) for n in ("gate_up_done", "silus", "gateds", "weighteds", "flips", "copies", "downs"))
        identity_added, updated, passed = (sem(n) for n in ("identity_added", "updated", "passed_routing"))
        CHAIN = 15
        loads = [(rw[:, :], routerT), (bias[:, :], bias_rows), (gu_w[:, :, :], guT), (down_w[:, :, :], downT)]
        LOADED = 16 * len(loads)
        with nc.Block() as block:
            @block.sync
            def _(sp):
                load(sp, weights, loads)

            @block.gpsimd
            def _(pool):
                pool.sem_inc(weighted, 2)
                norm.gpsimd_rstd(pool, 0, 0, 0)

                def group(i, s, it, nxt):
                    for u in range(G * PER):
                        if u == 4 and nxt:
                            norm.gpsimd_rstd(pool, *nxt)
                        b, o = divmod(u, PER)
                        unit = it * G * PER + u
                        pool.wait_ge(flips, unit + 1)
                        if u == 0:
                            pool.wait_ge(routed, it + 1)
                        pool.wait_ge(gateds, unit + 3)
                        nc.gpsimd.tensor_tensor(
                            h[:, u % 2], gated[:, u % 2],
                            w[:, s, b, o * OCT:(o + 1) * OCT].unsqueeze(2).to_broadcast([S, OCT, I]),
                            ALU.mult).then_inc(weighted, 1)
                turns(pool, group)

            @block.vector
            def _(dve):
                dve.sem_inc(gateds, 2)
                dve.sem_inc(updated, 2)
                nc.vector.memset(cand[:, :, :], BIG).then_inc(chain, 1)
                nc.vector.tensor_scalar(gscale[:, :], core.gates[:, 5:6], SCALE, None, ALU.mult).then_inc(chain, 1)
                dve.wait_ge(weights, LOADED)
                wide = lambda a: a.unsqueeze(2).to_broadcast([S, G, E])

                def route(s, it):
                    step = lambda n: it * CHAIN + n + 2
                    logits = norm_bank[:, 0:G * E].rearrange("p (j e) -> p j e", j=G)
                    dve.wait_ge(logits_in, it + 1)
                    nc.vector.tensor_reduce(negmax[:, :], logits, AX.X, ALU.max, negate=True).then_inc(chain, 1)
                    dve.wait_ge(chain, step(1))
                    nc.vector.tensor_tensor(shifted[:, :, :], logits, wide(negmax[:, :]), ALU.add).then_inc(shift_done, 1)
                    dve.wait_ge(exp_done, it + 1)
                    nc.vector.tensor_reduce(sums[:, :], exps[:, :, :], AX.X, ALU.add).then_inc(chain, 1)
                    dve.wait_ge(chain, step(2))
                    nc.vector.reciprocal(rsums[:, :], sums[:, :]).then_inc(chain, 1)
                    dve.wait_ge(chain, step(3))
                    nc.vector.tensor_tensor(probs[:, :, :], exps[:, :, :], wide(rsums[:, :]), ALU.mult).then_inc(chain, 1)
                    dve.wait_ge(chain, step(4))
                    nc.vector.tensor_tensor(cand[:, :, PAD:], probs[:, :, :],
                                            bias[:, :].unsqueeze(1).to_broadcast([S, G, E]), ALU.add).then_inc(chain, 1)
                    settled(dve, chain, step(5), passed)
                    for j in range(G):
                        nc.vector.max(top8[:, j, :], cand[:, j, :]).then_inc(chain, 1)
                    settled(dve, chain, step(5 + G), passed)
                    for j in range(G):
                        nc.vector.match_replace(marked[:, j, :], top8[:, j, :], cand[:, j, :], -BIG).then_inc(chain, 1)
                    dve.wait_ge(chain, step(5 + 2 * G))
                    nc.vector.tensor_scalar(chosen[:, :, :], marked[:, :, PAD:], -BIG, gscale[:, 0:1], ALU.is_equal,
                                            ALU.mult).then_inc(chain, 1)
                    dve.wait_ge(chain, step(6 + 2 * G))
                    nc.vector.tensor_tensor(w[:, s], chosen[:, :, :], probs[:, :, :], ALU.mult).then_inc(chain, 1)
                    dve.wait_ge(chain, step(7 + 2 * G))
                    nc.vector.tensor_reduce(wz[:, s, :], w[:, s, :, ER:], AX.X, ALU.add).then_inc(routed, 1)

                norm.vector(dve, 0, 0, 0)
                route(0, 0)

                def group(i, s, it, nxt):
                    x = core.X_groups[:, i, s]
                    for u in range(G * PER):
                        unit = it * G * PER + u
                        up = gu_ps[u % 2][:, :].rearrange("p (e c) -> p e c", e=OCT)[:, :, I:]
                        dve.wait_ge(weighted, unit + 1)
                        dve.wait_ge(silus, unit + 1)
                        nc.vector.tensor_tensor(gated[:, u % 2], silu[:, u % 2], up, ALU.mult).then_inc(gateds, 1)
                        if nxt and u == 2:
                            norm.vector_stats(dve, *nxt)
                        if nxt and u == 5:
                            norm.vector_normalise(dve, *nxt)
                        if nxt and u == 12:
                            route(nxt[1], nxt[2])
                    dve.wait_ge(routed, it + 1)
                    for j in range(G):
                        last = nc.vector.scalar_tensor_tensor(out=x[:, j, :], in0=norm.xn[:, s, j, :],
                                                              scalar=wz[:, s, j:j + 1], in1=x[:, j, :],
                                                              op0=ALU.mult, op1=ALU.add)
                    last.then_inc(identity_added, 1)
                    dve.wait_ge(identity_added, it + 1)
                    dve.wait_ge(downs, (it + 1) * G * PER + 2)
                    nc.vector.tensor_tensor(x, acc[:, :].rearrange("p (j d) -> p j d", j=G), x, ALU.add)\
                        .then_inc(updated, 1)
                turns(dve, group)

            @block.scalar
            def _(act):
                act.sem_inc(copies, 2)

                def exp_of(it):
                    act.wait_ge(shift_done, it + 1)
                    nc.scalar.activation(exps[:, :, :], shifted[:, :, :], ACT.Exp).then_inc(exp_done, 1)

                norm.scalar_copy(act, 0, 0, 0)
                exp_of(0)

                def group(i, s, it, nxt):
                    for step in range(G * PER + LAG + 1):
                        if step < G * PER:
                            unit = it * G * PER + step
                            gate = gu_ps[step % 2][:, :].rearrange("p (e c) -> p e c", e=OCT)[:, :, 0:I]
                            act.wait_ge(gateds, unit + 1)
                            act.wait_ge(gu_done, unit + 1)
                            nc.scalar.activation(silu[:, step % 2], gate, ACT.Silu).then_inc(silus, 1)
                        if nxt and step == 8:
                            norm.scalar_copy(act, *nxt)
                        if nxt and step == 12:
                            exp_of(nxt[2])
                        if 0 <= step - LAG < G * PER:
                            u = step - LAG
                            unit = it * G * PER + u
                            act.wait_ge(downs, unit + 1)
                            act.wait_ge(flips, unit + 3)
                            nc.scalar.activation(hT[:, u % 2].rearrange("p e t -> p (e t)"), turn_banks[u % 2][:, :],
                                                 ACT.Copy).then_inc(copies, 1)
                turns(act, group)

            @block.tensor
            def _(pe):
                pe.sem_inc(flips, 2)
                pe.sem_inc(downs, 2)
                pe.wait_ge(weights, LOADED)

                def router(s, it):
                    pe.wait_ge(norm.xT_ready, it + 1)
                    for j in range(G):
                        last = nc.tensor.matmul(norm_bank[:, j * E:(j + 1) * E], norm.xT[:, s, j * S:(j + 1) * S],
                                                rw[:, :], start=True, stop=True)
                    last.then_inc(logits_in, 1)

                norm.tensor_turn(pe, 0, 0, 0)
                router(0, 0)

                def group(i, s, it, nxt):
                    for step in range(G * PER + DOWN_LAG):
                        if step < G * PER:
                            b, o = divmod(step, PER)
                            unit = it * G * PER + step
                            pe.wait_ge(gateds, unit + 1)
                            for k in range(2):
                                last = nc.tensor.matmul(
                                    gu_ps[step % 2][:, k * 512:(k + 1) * 512], norm.xT[:, s, b * S:(b + 1) * S],
                                    gu_w[:, o * OCT + 4 * k:o * OCT + 4 * k + 4, :], start=True, stop=True)
                            last.then_inc(gu_done, 1)
                        if nxt and step == 7:
                            pe.wait_ge(routed, it + 1)
                            norm.tensor_turn(pe, *nxt)
                        if nxt and step == 10:
                            router(nxt[1], nxt[2])
                        if 0 <= step - LAG < G * PER:
                            u = step - LAG
                            unit = it * G * PER + u
                            pe.wait_ge(copies, unit + 1)
                            pe.wait_ge(weighted, unit + 3)
                            hw = h[:, u % 2].rearrange("p e c -> p (e c)")
                            for k in range(OCT // 2):
                                last = nc.tensor.transpose(turn_banks[u % 2][:, k * S:(k + 1) * S],
                                                           hw[:, k * 2 * I:(k + 1) * 2 * I], core.ident[:, :])
                            last.then_inc(flips, 1)
                        if step >= DOWN_LAG:
                            u = step - DOWN_LAG
                            unit = it * G * PER + u
                            b, o = divmod(u, PER)
                            if u == 0:
                                pe.wait_ge(updated, it + 2)
                            pe.wait_ge(copies, unit + 3)
                            for k in range(OCT // 2):
                                p = o * OCT // 2 + k
                                last = nc.tensor.matmul(acc[:, b * S:(b + 1) * S], hT[:, u % 2, k, :], down_w[:, p, :],
                                                        start=p == 0, stop=p == ER // 2 - 1)
                            last.then_inc(downs, 1)
                turns(pe, group)


def layer4_perceiver(core, ctx_nat, mask_rows, lnx_g, lnx_b, lnl_g, lnl_b, q_gamma, k_gamma, w_ctx, w_lat, woT, bo_row):
    nc, H, DH = core.nc, 2, 64
    MASKED = 3.4e38
    QK_TINY = 1e-8 ** 2
    with ExitStack() as ctx:
        sb = lambda name, shape, dt=F32: core.sbuf("a2_" + name, shape, dt, ctx=ctx)
        sem = lambda name: core.sem(ctx, "a2_" + name)
        bank = [core.psum(ctx, f"a2_bank{k}", [128, 512]) for k in range(8)]
        c_nat = sb("ctx", [S, 2, G, C])
        n_x = Norm(core, ctx, "a2x", None)
        n_l = Norm(core, ctx, "a2l", bank[0], source=lambda i, s: n_x.xn[:, s])
        n_c = Norm(core, ctx, "a2c", bank[1], width=C, source=lambda i, s: c_nat[:, s])
        q_gain = sb("q_gain", [128, 1])
        vecs = sb("vecs", [128, 6])
        wc, wl, wo, bo = sb("w_ctx", [C, 2 * D]), sb("w_lat", [D, 3 * D]), sb("wo", [D, D]), sb("bo", [1, D])
        mask_u8, neg = sb("mask", [S, B, S], mybir.dt.uint8), sb("neg", [S, B, 2, S])
        neg_v = neg[:, :, :, :].rearrange("p (i s j) c k -> p i s j (c k)", s=2, j=G)
        lT, cT = sb("latT", [D, 2, N]), sb("ctxT", [C, 2, N])
        qk = sb("qk", [S, 2, G, 3, D])
        v = sb("v", [S, 2, G, 2, D])
        sq, ss, ms, rn, qkn = (sb("sq", [S, G * 3 * D]), sb("ss", [S, G * 6]), sb("ms", [S, G * 6]),
                               sb("rn", [S, 2, G * 6]), sb("qkn", [S, 2, G, 3, D]))
        qT, kT = sb("qT", [D, 2, G, S]), sb("kT", [D, 2, G, 2, S])
        sc, negmax = sb("scores", [S, 2, H, G, 2 * S]), sb("negmax", [S, H, G])
        probs, psum_, rsum = sb("probs", [S, 2, H, G, 2 * S]), sb("prob_sums", [S, 2, G, H]), sb("rsum", [S, G, H])
        pT = sb("probsT", [S, 2, 4, 4, S])
        o, oT = sb("o", [S, 2, G, D]), sb("oT", [D, 2, N])
        weights, ctx_landed = sem("weights"), [sem("ctx_landed0"), sem("ctx_landed1")]
        neg_done, gain_done, chain = sem("neg_done"), sem("gain_done"), sem("chain")
        lT_ready, cT_ready, lat_proj, ctx_proj, lat_kept, ctx_kept = (
            sem(n) for n in ("lT_ready", "cT_ready", "lat_projected", "ctx_projected", "lat_kept", "ctx_kept"))
        squares, ms_done, rn_done, qkn_done, qk_turned, qkT_ready = (
            sem(n) for n in ("squares", "ms_done", "rn_done", "qkn_done", "qk_turned", "qkT_ready"))
        scored, masked, shift_ready, exps, flips, pT_act, pT_dve, weighed = (
            sem(n) for n in ("scored", "masked", "shift_ready", "exps", "flips", "pT_by_scalar", "pT_by_vector",
                             "weighed"))
        normalised, o_turned, oT_ready, mixed, updated = (
            sem(n) for n in ("normalised", "o_turned", "oT_ready", "mixed", "updated"))
        CHAIN = 2
        nat_groups = ctx_nat.rearrange("(i s j) t c -> t i s j c", s=2, j=G)
        loads = [(wc[:, :], w_ctx), (wl[:, :], w_lat), (wo[:, :], woT), (bo[:, :], bo_row),
                 (mask_u8[:, :, :], mask_rows), (vecs[0:C, 0:1], lnx_g), (vecs[0:C, 1:2], lnx_b),
                 (vecs[:, 2:3], lnl_g), (vecs[:, 3:4], lnl_b), (vecs[:, 4:5], q_gamma), (vecs[:, 5:6], k_gamma)]
        LOADED = 16 * len(loads)
        with nc.Block() as block:
            @block.sync
            def _(sp):
                load(sp, weights, loads)

                def group(i, s, it, nxt):
                    sp.wait_ge(updated, it + 1)
                    sp.dma_start(c_nat[:, s], nat_groups[:, i, s]).then_inc(ctx_landed[s], 16)
                turns(sp, group)

            @block.gpsimd
            def _(pool):
                nc.gpsimd.memset(neg[:, :, 1, :], 0.0).then_inc(neg_done, 1)

                def norms(i, s, it):
                    n_x.gpsimd_rstd(pool, i, s, it)
                    n_c.gpsimd_rstd(pool, i, s, it)
                    n_l.gpsimd_rstd(pool, i, s, it)
                norms(0, 0, 0)

                def group(i, s, it, nxt):
                    pool.wait_ge(ms_done, it + 1)
                    nc.gpsimd.tensor_tensor(rn[:, s, :], ms[:, :], core.minus_half[:, 0:G * 6], ALU.pow)\
                        .then_inc(rn_done, 1)
                    if nxt:
                        norms(*nxt)
                turns(pool, group)

            @block.vector
            def _(dve):
                dve.sem_inc(updated, 2)
                dve.wait_ge(weights, LOADED)
                nc.vector.tensor_scalar(neg[:, :, 0, :], mask_u8[:, :, :], 1.0, MASKED, ALU.subtract, ALU.mult)\
                    .then_inc(neg_done, 1)
                nc.vector.tensor_scalar(q_gain[:, :], vecs[:, 4:5], DH ** -0.5, None, ALU.mult).then_inc(gain_done, 1)

                def norms(i, s, it):
                    n_x.vector_stats(dve, i, s, it)
                    dve.wait_ge(ctx_landed[s], i * 16 + 16)
                    n_c.vector_stats(dve, i, s, it)
                    n_x.vector_normalise(dve, i, s, it)
                    n_c.vector_normalise(dve, i, s, it)
                    dve.wait_ge(n_x.xn_done, it + 1)
                    n_l.vector_stats(dve, i, s, it)
                    n_l.vector_normalise(dve, i, s, it)

                norms(0, 0, 0)
                dve.wait_ge(neg_done, 2)

                def group(i, s, it, nxt):
                    for b in range(G):
                        dve.wait_ge(ctx_proj, it * G + b + 1)
                        nc.vector.tensor_copy(qk[:, s, b, 2, :], bank[4 + b % 2][:, 0:D])
                        nc.vector.tensor_copy(v[:, s, b, 0, :], bank[4 + b % 2][:, D:2 * D]).then_inc(ctx_kept, 1)
                    dve.wait_ge(squares, it + 1)
                    nc.vector.tensor_reduce(ss[:, :], sq[:, :].rearrange("p (n e) -> p n e", e=DH), AX.X, ALU.add)\
                        .then_inc(chain, 1)
                    dve.wait_ge(chain, it * CHAIN + 1)
                    nc.vector.tensor_scalar(ms[:, :], ss[:, :], 1.0 / DH, QK_TINY, ALU.mult, ALU.max).then_inc(ms_done, 1)
                    dve.wait_ge(rn_done, it + 1)
                    nc.vector.tensor_tensor(
                        qkn[:, s].rearrange("p b c (h e) -> p (b c h) e", h=H),
                        qk[:, s].rearrange("p b c (h e) -> p (b c h) e", h=H),
                        rn[:, s, :].unsqueeze(2).to_broadcast([S, G * 6, DH]), ALU.mult).then_inc(qkn_done, 1)
                    if nxt:
                        norms(*nxt)
                    for h in range(H):
                        for p in range(2):
                            dve.wait_ge(scored, it * 4 + 2 * h + p + 1)
                            last = nc.vector.tensor_tensor(
                                sc[:, s, h, 2 * p:2 * p + 2, :],
                                bank[2 + 2 * h + p][:, :].rearrange("p (b k) -> p b k", b=2),
                                neg_v[:, i, s, 2 * p:2 * p + 2, :], ALU.add)
                    last.then_inc(masked, 1)
                    dve.wait_ge(masked, it + 1)
                    nc.vector.tensor_reduce(negmax[:, :, :].rearrange("p h b -> p (h b)"), sc[:, s].rearrange("p h b k -> p (h b) k"), AX.X, ALU.max,
                                            negate=True).then_inc(shift_ready, 1)
                    for n in (1, 3):
                        dve.wait_ge(flips, it * 4 + n + 1)
                        nc.vector.tensor_copy(pT[:, s, n].rearrange("p a k -> p (a k)"), bank[6 + n % 2][:, :])\
                            .then_inc(pT_dve, 1)
                    dve.wait_ge(exps, it + 1)
                    nc.vector.reciprocal(rsum[:, :, :], psum_[:, s]).then_inc(chain, 1)
                    dve.wait_ge(weighed, it + 1)
                    dve.wait_ge(chain, it * CHAIN + 2)
                    nc.vector.tensor_tensor(o[:, s].rearrange("p b (h e) -> p (b h) e", h=H),
                                            bank[2][:, :].rearrange("p (n e) -> p n e", e=DH),
                                            rsum[:, :, :].rearrange("p b h -> p (b h)").unsqueeze(2)
                                            .to_broadcast([S, G * H, DH]), ALU.mult).then_inc(normalised, 1)
                    dve.wait_ge(mixed, it + 1)
                    x = core.X_groups[:, i, s]
                    nc.vector.scalar_tensor_tensor(
                        out=x, in0=bank[4][:, :].rearrange("p (j d) -> p j d", j=G), scalar=core.gates[:, 2:3],
                        in1=x, op0=ALU.mult, op1=ALU.add).then_inc(updated, 1)
                turns(dve, group)

            @block.scalar
            def _(act):
                act.wait_ge(weights, LOADED)
                act.wait_ge(gain_done, 1)

                def turned(i, s, it):
                    act.wait_ge(n_l.turned, it + 1)
                    nc.scalar.activation(lT[:, s, :], bank[0][:, :], ACT.Identity, bias=vecs[:, 3:4],
                                         scale=vecs[:, 2:3]).then_inc(lT_ready, 1)
                    act.wait_ge(n_c.turned, it + 1)
                    nc.scalar.activation(cT[:, s, :], bank[1][0:C, :], ACT.Identity, bias=vecs[0:C, 1:2],
                                         scale=vecs[0:C, 0:1]).then_inc(cT_ready, 1)
                turned(0, 0, 0)

                def group(i, s, it, nxt):
                    for b in range(G):
                        act.wait_ge(lat_proj, it * G + b + 1)
                        nc.scalar.activation(qk[:, s, b, 0:2, :].rearrange("p c d -> p (c d)"), bank[2 + b % 2][:, 0:2 * D],
                                             ACT.Copy)
                        nc.scalar.activation(v[:, s, b, 1, :], bank[2 + b % 2][:, 2 * D:3 * D], ACT.Copy)\
                            .then_inc(lat_kept, 1)
                    act.wait_ge(lat_kept, it * G + G)
                    act.wait_ge(ctx_kept, it * G + G)
                    nc.scalar.activation(sq[:, :], qk[:, s].rearrange("p b c d -> p (b c d)"), ACT.Square)\
                        .then_inc(squares, 1)
                    for c, (out, gain) in enumerate(((qT[:, s], q_gain[:, 0:1]), (kT[:, s, :, 1, :], vecs[:, 5:6]),
                                                      (kT[:, s, :, 0, :], vecs[:, 5:6]))):
                        act.wait_ge(qk_turned, it * 3 + c + 1)
                        nc.scalar.activation(out, bank[5 + c][:, :].rearrange("p (b k) -> p b k", b=G), ACT.Copy,
                                             scale=gain).then_inc(qkT_ready, 1)
                    if nxt:
                        turned(*nxt)
                    act.wait_ge(shift_ready, it + 1)
                    for b in range(G):
                        for h in range(H):
                            last = nc.scalar.activation(probs[:, s, h, b, :], sc[:, s, h, b, :], ACT.Exp,
                                                        bias=negmax[:, h, b:b + 1], accum_out=psum_[:, s, b, h:h + 1])
                    last.then_inc(exps, 1)
                    for n in (0, 2):
                        act.wait_ge(flips, it * 4 + n + 1)
                        nc.scalar.activation(pT[:, s, n].rearrange("p a k -> p (a k)"), bank[6 + n % 2][:, :], ACT.Copy)\
                            .then_inc(pT_act, 1)
                    act.wait_ge(o_turned, it + 1)
                    nc.scalar.activation(oT[:, s, :], bank[3][:, :], ACT.Copy).then_inc(oT_ready, 1)
                turns(act, group)

            @block.tensor
            def _(pe):
                pe.wait_ge(weights, LOADED)

                def turned(i, s, it):
                    n_c.tensor_turn(pe, i, s, it)
                    n_l.tensor_turn(pe, i, s, it)
                turned(0, 0, 0)

                def group(i, s, it, nxt):
                    pe.wait_ge(lT_ready, it + 1)
                    pe.wait_ge(cT_ready, it + 1)
                    pe.wait_ge(updated, it + 1 + 1)
                    for b in range(G):
                        bs = slice(b * S, (b + 1) * S)
                        if b >= 2:
                            pe.wait_ge(lat_kept, it * G + b - 1)
                        nc.tensor.matmul(bank[2 + b % 2][:, 0:3 * D], lT[:, s, bs], wl[:, :], start=True, stop=True)\
                            .then_inc(lat_proj, 1)
                        if b >= 2:
                            pe.wait_ge(ctx_kept, it * G + b - 1)
                        nc.tensor.matmul(bank[4 + b % 2][:, 0:2 * D], cT[:, s, bs], wc[:, :], start=True, stop=True)\
                            .then_inc(ctx_proj, 1)
                    pe.wait_ge(qkn_done, it + 1)
                    for c in range(3):
                        for b in range(G):
                            last = nc.tensor.transpose(bank[5 + c][:, b * S:(b + 1) * S], qkn[:, s, b, c, :],
                                                       core.ident[:, :])
                        last.then_inc(qk_turned, 1)
                    pe.wait_ge(qkT_ready, it * 3 + 3)
                    for h in range(H):
                        r = slice(DH * h, DH * h + DH)
                        for p in range(2):
                            for b in (2 * p, 2 * p + 1):
                                last = nc.tensor.matmul(bank[2 + 2 * h + p][:, (b % 2) * 256:(b % 2) * 256 + 256],
                                                        qT[r, s, b, :], kT[r, s, b, :, :].rearrange("p c k -> p (c k)"),
                                                        start=True, stop=True)
                            last.then_inc(scored, 1)
                    if nxt:
                        turned(*nxt)
                    pe.wait_ge(exps, it + 1)
                    for n in range(4):
                        if n >= 2:
                            pe.wait_ge((pT_act, pT_dve)[n % 2], it * 2 + 1)
                        for k in range(4):
                            last = nc.tensor.transpose(bank[6 + n % 2][:, k * S:(k + 1) * S],
                                                       probs[:, s, k // 2, n, (k % 2) * S:(k % 2) * S + S],
                                                       core.ident[:, :])
                        last.then_inc(flips, 1)
                    pe.wait_ge(pT_act, it * 2 + 2)
                    pe.wait_ge(pT_dve, it * 2 + 2)
                    for b in range(G):
                        for h in range(H):
                            for half in range(2):
                                last = nc.tensor.matmul(bank[2][:, (b * H + h) * DH:(b * H + h + 1) * DH],
                                                        pT[:, s, b, 2 * h + half, :], v[:, s, b, half, h * DH:(h + 1) * DH],
                                                        start=half == 0, stop=half == 1)
                    last.then_inc(weighed, 1)
                    pe.wait_ge(normalised, it + 1)
                    for b in range(G):
                        last = nc.tensor.transpose(bank[3][:, b * S:(b + 1) * S], o[:, s, b, :], core.ident[:, :])
                    last.then_inc(o_turned, 1)
                    pe.wait_ge(oT_ready, it + 1)
                    for b in range(G):
                        bs = slice(b * S, (b + 1) * S)
                        nc.tensor.matmul(bank[4][:, bs], core.ones[0:1, :], bo[0:1, :], start=True, stop=False)
                        last = nc.tensor.matmul(bank[4][:, bs], oT[:, s, bs], wo[:, :], start=False, stop=True)
                    last.then_inc(mixed, 1)
                turns(pe, group)


def layer1_soft_moe(core, phi, w, bias):
    nc, E, SLOTS = core.nc, 64, 32
    EC = 8
    CH = EC * SLOTS
    CHUNKS = E // EC
    KT = CH // 128
    NB = B // 2
    with ExitStack() as ctx:
        sb = lambda name, shape: core.sbuf("f0_" + name, shape, ctx=ctx)
        sem = lambda name: core.sem(ctx, "f0_" + name)
        xn, xT = sb("xn", [S, B, D]), sb("xT", [D, B, S])
        phi_s = sb("phi", [D, E * SLOTS])
        slot_max = sb("slot_max", [S, E * SLOTS])
        row_parts, neg_row = sb("row_parts", [S, 4, B]), sb("neg_row_max", [S, B])
        row_sum, acc = sb("row_sum", [S, B]), sb("acc", [S, B, D])
        with ExitStack() as c1:
            sb1 = lambda name, shape: core.sbuf("f0_" + name, shape, ctx=c1)
            bank = [core.psum(c1, f"f0_bank{k}", [128, 512]) for k in range(8)]
            stats, mv, veps, rstd = sb1("stats", [S, B, 6]), sb1("mean_var", [S, B, 2]), sb1("var_eps", [S, B]), sb1("rstd", [S, B])
            weights, stats_done, mv_done, veps_done, rstd_done = (
                sem(n) for n in ("phi_landed", "stats_done", "mv_done", "veps_done", "rstd_done"))
            xn_done, turned, xT_ready, l_done, l_used, row_done, passed = (
                sem(n) for n in ("xn_done", "turned", "xT_ready", "logits", "logits_used", "row_parts_done", "passed1"))
            slot_seen = sem("slot_seen")
            phi_q = phi_s[:, :].rearrange("d (q n) -> d q n", n=512)
            max_q = slot_max[:, :].rearrange("d (q n) -> d q n", n=512)
            with nc.Block() as block:
                @block.sync
                def _(sp):
                    sp.dma_start(phi_s[:, :], phi).then_inc(weights, 16)

                @block.gpsimd
                def _(pool):
                    nc.gpsimd.memset(slot_max[:, :], -BIG).then_inc(slot_seen, 1)
                    nc.gpsimd.memset(acc[:, :, :], 0.0)
                    nc.gpsimd.memset(row_sum[:, :], 0.0)
                    pool.wait_ge(mv_done, 1)
                    nc.gpsimd.tensor_tensor(veps[:, :], mv[:, :, 1], core.eps[:, :], ALU.add).then_inc(veps_done, 1)
                    pool.wait_ge(veps_done, 1)
                    nc.gpsimd.tensor_tensor(rstd[:, :], veps[:, :], core.minus_half[:, :], ALU.pow).then_inc(rstd_done, 1)

                @block.vector
                def _(dve):
                    for b in range(B):
                        last = nc.vector.bn_stats(stats[:, b, :], core.X[:, b, :])
                    last.then_inc(stats_done, 1)
                    dve.wait_ge(stats_done, 1)
                    for b in range(B):
                        last = nc.vector.bn_aggr(mv[:, b, :], stats[:, b, :])
                    last.then_inc(mv_done, 1)
                    dve.wait_ge(rstd_done, 1)
                    for b in range(B):
                        nc.vector.tensor_scalar(xn[:, b, :], core.X[:, b, :], mv[:, b, 0:1], rstd[:, b:b + 1],
                                                ALU.subtract, ALU.mult).then_inc(xn_done, 1)
                    with dve.Fori(0, 4) as q:
                        for b in range(B):
                            ps = bank[2 + b % 6][:, :]
                            dve.wait_ge(l_done, q * B + b + 1)
                            dve.wait_ge(slot_seen, q * B + b + 1)
                            nc.vector.tensor_tensor(max_q[:, q, :], ps, max_q[:, q, :], ALU.max)
                            nc.vector.tensor_reduce(row_parts[:, q, b:b + 1], ps, AX.X, ALU.max).then_inc(slot_seen, 1)
                    dve.wait_ge(slot_seen, 4 * B + 1)
                    nc.vector.tensor_reduce(neg_row[:, :], row_parts[:, :, :].rearrange("p q b -> p b q"), AX.X, ALU.max,
                                            negate=True)

                @block.scalar
                def _(act):
                    for g in range(GROUPS):
                        act.wait_ge(turned, g + 1)
                        nc.scalar.activation(xT[:, g * G:(g + 1) * G, :].rearrange("d b t -> d (b t)"), bank[g % 2][:, :],
                                             ACT.Copy).then_inc(xT_ready, 1)

                @block.tensor
                def _(pe):
                    for g in range(GROUPS):
                        pe.wait_ge(xn_done, g * G + G)
                        if g >= 2:
                            pe.wait_ge(xT_ready, g - 1)
                        for j in range(G):
                            last = nc.tensor.transpose(bank[g % 2][:, j * S:(j + 1) * S], xn[:, g * G + j, :],
                                                       core.ident[:, :])
                        last.then_inc(turned, 1)
                    pe.wait_ge(xT_ready, GROUPS)
                    pe.wait_ge(weights, 16)
                    with pe.Fori(0, 4) as q:
                        for b in range(B):
                            if b < 6:
                                pe.wait_ge(slot_seen, q * B + 1)
                            else:
                                pe.wait_ge(slot_seen, q * B + b - 4)
                            nc.tensor.matmul(bank[2 + b % 6][:, :], xT[:, b, :], phi_q[:, q, :], start=True,
                                             stop=True).then_inc(l_done, 1)

        with ExitStack() as c2:
            sb2 = lambda name, shape: core.sbuf("f0_" + name, shape, ctx=c2)
            bank = [core.psum(c2, f"f0_chunk_bank{k}", [128, 512]) for k in range(8)]
            w_s, bias_s = sb2("w", [D, EC, D]), sb2("bias", [D, EC])
            disp = sb2("dispatch", [S, B, CH])
            y = disp[:, :, :].rearrange("p b n -> p (b n)").rearrange("p (k b d) -> p k b d", k=KT, b=B)
            back = sb2("combine", [S, 4, CH])
            backT = sb2("combineT", [128, KT, B, S])
            part, sums, rsums = sb2("part_sums", [S, 2, CH]), sb2("slot_sums", [S, CH]), sb2("slot_rsums", [S, CH])
            row_part, row_r, row_g = sb2("row_part", [S, B]), sb2("row_r", [S, B]), sb2("row_gate", [S, B])
            slots = sb2("slots", [D, KT, B, 4, SLOTS])
            w_landed, logits, shifts, backs, disps, flips, backTs, pair_sums = (
                sem(n) for n in ("w_landed", "chunk_logits", "shifts", "backs", "disps", "flips", "backTs", "pair_sums"))
            rows_added, sums_done, rsums_done, scaled_dve, scaled_pool = (
                sem(n) for n in ("rows_added", "sums_done", "rsums_done", "scaled_by_vector", "scaled_by_gpsimd"))
            dispatched, slots_act, slots_dve, expanded, biased = (
                sem(n) for n in ("dispatched", "slots_by_scalar", "slots_by_vector", "expanded", "biased"))
            y_flips, y_act, y_dve, returned, added, row_r_done, row_g_done = (
                sem(n) for n in ("y_flips", "y_by_scalar", "y_by_vector", "returned", "added", "row_r_done", "row_g_done"))
            phi_c = phi_s[:, :].rearrange("d (c n) -> d c n", n=CH)
            max_c = slot_max[:, :].rearrange("d (c n) -> d c n", n=CH)
            BY_POOL = (2, 5, 7)
            BY_VECTOR = tuple(g for g in range(GROUPS) if g not in BY_POOL)
            logit_bank = lambda p: bank[(0, 1, 6, 7)[p % 4]]
            pair = lambda p: slice(2 * p, 2 * p + 2)
            half_of_expert = lambda u: slots[:, u // 8, 16 * (u % 2):16 * (u % 2) + 16, u // 2 % 4, :]
            scale_group = lambda g: (disp[:, g * G:(g + 1) * G, :], rsums[:, :].unsqueeze(1).to_broadcast([S, G, CH]))
            with nc.Block() as block:
                @block.sync
                def _(sp):
                    def fetch(c):
                        sp.dma_start(w_s[:, :, :], w[:, c, :, :]).then_inc(w_landed, 16)
                        sp.dma_start(bias_s[:, :], bias[:, c, :]).then_inc(w_landed, 16)
                    fetch(0)
                    with sp.Fori(0, CHUNKS - 1) as c:
                        sp.wait_ge(biased, c * 16 + 16)
                        fetch(c + 1)

                @block.tensor
                def _(pe):
                    with pe.Fori(0, CHUNKS) as c:
                        for step in range(NB + 1):
                            if step < NB:
                                p = step
                                if p >= 4:
                                    pe.wait_ge(shifts, c * NB + p - 3)
                                for k in range(2):
                                    last = nc.tensor.matmul(logit_bank(p)[:, k * CH:(k + 1) * CH], xT[:, 2 * p + k, :],
                                                            phi_c[:, c, :], start=True, stop=True)
                                last.then_inc(logits, 1)
                            if step >= 1:
                                p = step - 1
                                if p >= 2:
                                    pe.wait_ge(backTs, c * NB + p - 1)
                                pe.wait_ge(backs, c * NB + p + 1)
                                for kt in range(KT):
                                    for k in range(2):
                                        at = (kt * 2 + k) * S
                                        last = nc.tensor.transpose(bank[2 + p % 2][:, at:at + S],
                                                                   back[:, 2 * (p % 2) + k, kt * 128:(kt + 1) * 128],
                                                                   core.ident[:, :])
                                last.then_inc(flips, 1)
                        pe.wait_ge(added, c * GROUPS + GROUPS)
                        for p in range(NB):
                            g = p // 2
                            if p % 2 == 0:
                                if g in BY_POOL:
                                    pe.wait_ge(scaled_pool, c * len(BY_POOL) + BY_POOL.index(g) + 1)
                                else:
                                    pe.wait_ge(scaled_dve, c * len(BY_VECTOR) + BY_VECTOR.index(g) + 1)
                            if p >= 2:
                                pe.wait_ge((slots_act, slots_dve)[p % 2], c * (NB // 2) + (p - 2) // 2 + 1)
                            for k in range(2):
                                last = nc.tensor.matmul(bank[4 + p % 2][:, k * CH:(k + 1) * CH], xn[:, 2 * p + k, :],
                                                        disp[:, 2 * p + k, :], start=True, stop=True)
                            last.then_inc(dispatched, 1)
                        pe.wait_ge(slots_act, c * (NB // 2) + NB // 2)
                        pe.wait_ge(slots_dve, c * (NB // 2) + NB // 2)
                        pe.wait_ge(w_landed, c * 32 + 32)

                        def turn_outputs(n):
                            kt, g = divmod(n, GROUPS)
                            if g == 0:
                                pe.wait_ge(biased, c * 16 + 8 * kt + 8)
                            if n == 0:
                                pe.wait_ge(backTs, c * NB + NB)
                            if n >= 2:
                                pe.wait_ge((y_act, y_dve)[n % 2], c * GROUPS + (n - 2) // 2 + 1)
                            for j in range(G):
                                last = nc.tensor.transpose(bank[2 + n % 2][:, j * D:(j + 1) * D],
                                                           slots[:, kt, g * G + j].rearrange("d e s -> d (e s)"), core.ident[:, :])
                            last.then_inc(y_flips, 1)

                        for u in range(16):
                            if u >= 2:
                                pe.wait_ge(biased, c * 16 + u - 1)
                            nc.tensor.matmul(bank[6 + u % 2][:, :], w_s[:, u // 2, :],
                                             half_of_expert(u), start=True,
                                             stop=True).then_inc(expanded, 1)
                            if u >= 9:
                                turn_outputs(u - 9)
                        for n in range(7, 16):
                            turn_outputs(n)
                        pe.wait_ge(y_act, c * GROUPS + GROUPS)
                        pe.wait_ge(y_dve, c * GROUPS + GROUPS)
                        for g in range(GROUPS):
                            if g >= 2:
                                pe.wait_ge(added, c * GROUPS + g - 1 + GROUPS)
                            for j in range(G):
                                for kt in range(KT):
                                    last = nc.tensor.matmul(bank[4 + g % 2][:, j * D:(j + 1) * D],
                                                            backT[:, kt, g * G + j, :], y[:, kt, g * G + j, :],
                                                            start=kt == 0, stop=kt == KT - 1)
                            last.then_inc(returned, 1)

                @block.scalar
                def _(act):
                    with act.Fori(0, CHUNKS) as c:
                        for p in range(NB):
                            if p >= 2:
                                act.wait_ge(flips, c * NB + p - 1)
                            act.wait_ge(logits, c * NB + p + 1)
                            for k in range(2):
                                b = 2 * p + k
                                last = nc.scalar.activation(back[:, b % 4, :], logit_bank(p)[:, k * CH:(k + 1) * CH],
                                                            ACT.Exp, bias=neg_row[:, b:b + 1],
                                                            accum_out=row_part[:, b:b + 1])
                            last.then_inc(backs, 1)
                            act.wait_ge(shifts, c * NB + p + 1)
                            nc.scalar.activation(disp[:, pair(p), :], disp[:, pair(p), :], ACT.Exp).then_inc(disps, 1)
                        for p in range(0, NB, 2):
                            act.wait_ge(dispatched, c * NB + p + 1)
                            nc.scalar.activation(slots[:, :, pair(p)].rearrange("d k b e s -> d b k (e s)"),
                                                 bank[4][:, :].rearrange("d (b k n) -> d b k n", b=2, k=KT),
                                                 ACT.Copy).then_inc(slots_act, 1)
                        act.wait_ge(w_landed, c * 32 + 32)
                        done = 0
                        for u in range(16):
                            act.wait_ge(expanded, c * 16 + u + 1)
                            nc.scalar.activation(half_of_expert(u),
                                                 bank[6 + u % 2][:, :].rearrange("d (b s) -> d b s", b=16), ACT.Identity,
                                                 bias=bias_s[:, u // 2:u // 2 + 1]).then_inc(biased, 1)
                            if u >= 10 and u % 2 == 0:
                                n = u - 10
                                act.wait_ge(y_flips, c * 16 + n + 1)
                                nc.scalar.activation(y[:, 0, n * G:n * G + G, :], bank[2][:, :].rearrange(
                                    "p (j d) -> p j d", j=G), ACT.Copy).then_inc(y_act, 1)
                                done = n + 2
                        for n in range(done, 16, 2):
                            kt, g = divmod(n, GROUPS)
                            act.wait_ge(y_flips, c * 16 + n + 1)
                            nc.scalar.activation(y[:, kt, g * G:g * G + G, :], bank[2][:, :].rearrange(
                                "p (j d) -> p j d", j=G), ACT.Copy).then_inc(y_act, 1)

                @block.gpsimd
                def _(pool):
                    with pool.Fori(0, CHUNKS) as c:
                        for p in range(1, NB):
                            if p >= 2:
                                pool.wait_ge(pair_sums, c * (NB - 1) + p - 1)
                            pool.wait_ge(disps, c * NB + p + 1)
                            nc.gpsimd.tensor_tensor(part[:, :, :], part[:, :, :] if p > 1 else disp[:, pair(0), :],
                                                    disp[:, pair(p), :], ALU.add).then_inc(pair_sums, 1)
                        for g in BY_POOL:
                            pool.wait_ge(rsums_done, c + 1)
                            e, r = scale_group(g)
                            nc.gpsimd.tensor_tensor(e, e, r, ALU.mult).then_inc(scaled_pool, 1)

                @block.vector
                def _(dve):
                    dve.sem_inc(added, GROUPS)
                    dve.sem_inc(rows_added, 1)
                    with dve.Fori(0, CHUNKS) as c:
                        for step in range(NB + 2):
                            if step < NB:
                                p = step
                                dve.wait_ge(backs, c * NB + p + 1)
                                nc.vector.tensor_tensor(disp[:, pair(p), :],
                                                        logit_bank(p)[:, :].rearrange("p (b n) -> p b n", b=2),
                                                        max_c[:, c, :].unsqueeze(1).to_broadcast([S, 2, CH]),
                                                        ALU.subtract).then_inc(shifts, 1)
                            if step >= 2:
                                p = step - 2
                                dve.wait_ge(flips, c * NB + p + 1)
                                nc.vector.tensor_copy(backT[:, :, pair(p), :],
                                                      bank[2 + p % 2][:, :].rearrange("p (k b t) -> p k b t", k=KT, b=2))\
                                    .then_inc(backTs, 1)
                        dve.wait_ge(backs, c * NB + NB)
                        dve.wait_ge(rows_added, c + 1)
                        nc.vector.tensor_tensor(row_sum[:, :], row_sum[:, :], row_part[:, :], ALU.add)\
                            .then_inc(rows_added, 1)
                        dve.wait_ge(pair_sums, (c + 1) * (NB - 1))
                        nc.vector.tensor_tensor(sums[:, :], part[:, 0, :], part[:, 1, :], ALU.add).then_inc(sums_done, 1)
                        dve.wait_ge(sums_done, c + 1)
                        nc.vector.reciprocal(rsums[:, :], sums[:, :]).then_inc(rsums_done, 1)
                        dve.wait_ge(rsums_done, c + 1)
                        for g in BY_VECTOR:
                            e, r = scale_group(g)
                            nc.vector.tensor_tensor(e, e, r, ALU.mult).then_inc(scaled_dve, 1)
                        for p in range(1, NB, 2):
                            dve.wait_ge(dispatched, c * NB + p + 1)
                            nc.vector.tensor_copy(slots[:, :, pair(p)].rearrange("d k b e s -> d b k (e s)"),
                                                  bank[5][:, :].rearrange("d (b k n) -> d b k n", b=2, k=KT))\
                                .then_inc(slots_dve, 1)
                        for n in range(1, 16, 2):
                            kt, g = divmod(n, GROUPS)
                            dve.wait_ge(y_flips, c * 16 + n + 1)
                            nc.vector.tensor_copy(y[:, kt, g * G:g * G + G, :],
                                                  bank[3][:, :].rearrange("p (j d) -> p j d", j=G)).then_inc(y_dve, 1)
                        for g in range(GROUPS):
                            dve.wait_ge(added, c * GROUPS + g + 1)
                            dve.wait_ge(returned, c * GROUPS + g + 1)
                            a = acc[:, g * G:g * G + G, :]
                            nc.vector.tensor_tensor(a, bank[4 + g % 2][:, :].rearrange("p (j d) -> p j d", j=G), a,
                                                    ALU.add).then_inc(added, 1)
                    dve.wait_ge(rows_added, CHUNKS + 1)
                    nc.vector.reciprocal(row_r[:, :], row_sum[:, :]).then_inc(row_r_done, 1)
                    dve.wait_ge(row_r_done, 1)
                    nc.vector.tensor_scalar(row_g[:, :], row_r[:, :], core.gates[:, 4:5], None, ALU.mult)\
                        .then_inc(row_g_done, 1)
                    dve.wait_ge(row_g_done, 1)
                    dve.wait_ge(added, (CHUNKS + 1) * GROUPS)
                    for b in range(B):
                        nc.vector.scalar_tensor_tensor(out=core.X[:, b, :], in0=acc[:, b, :], scalar=row_g[:, b:b + 1],
                                                       in1=core.X[:, b, :], op0=ALU.mult, op1=ALU.add)


def store(core, out):
    nc = core.nc
    with ExitStack() as ctx:
        stored = core.sem(ctx, "stored")
        with nc.Block() as block:
            @block.sync
            def _(sp):
                sp.dma_start(out.rearrange("b s d -> s b d"), core.X[:, :, :]).then_inc(stored, 16)
                sp.wait_ge(stored, 16)


def arrays(inputs):
    a = {k: np.asarray(v) for k, v in inputs.items()}
    col = lambda v: v.reshape(-1, 1)
    rows = lambda v, n=128: np.tile(v.reshape(1, -1), (n, 1))
    in_halves = lambda w: w.reshape(-1, 2, 2, 4, 64).transpose(0, 1, 3, 2, 4).reshape(-1, 1024)
    laid = {
        "x": a["x"],
        "ctxT": a["ctx_768"].transpose(2, 0, 1).reshape(C, B * S),
        "gates": rows(np.concatenate([a["g_xattn"], a["g_ffn"]])),
        "c0_wvT": a["L0_xattn_Wv"].T, "c0_bv": col(a["L0_xattn_bv"]),
        "c0_wtT": a["L0_xattn_Wt"].T, "c0_bt": col(a["L0_xattn_bt"]),
        "a1_wq": a["L1_xattn_Wq"], "a1_bq": col(a["L1_xattn_bq"]),
        "a1_wk": a["L1_xattn_Wk"], "a1_bk": col(a["L1_xattn_bk"]),
        "a1_wv": a["L1_xattn_Wv"], "a1_bv": rows(a["L1_xattn_bv"]),
        "a1_w1": a["L1_xattn_W1"], "a1_b1": a["L1_xattn_b1"].reshape(2, 128).T,
        "a1_w2": a["L1_xattn_W2"].reshape(2, 128, D).transpose(1, 0, 2),
        "a1_b2": a["L1_xattn_b2"].reshape(1, D),
        "a1_mask": np.repeat(np.eye(16, dtype=np.float32), 8, axis=0),
        "f0_phi": a["L0_ffn_phi"].reshape(D, 64 * 32),
        "f0_w": a["L0_ffn_W"].reshape(8, 8, D, D).transpose(2, 0, 1, 3), "f0_bias": a["L0_ffn_b"].reshape(8, 8, D).transpose(2, 0, 1),
        "f1_routerT": a["L1_ffn_classifier_weight"].T, "f1_bias": rows(a["L1_ffn_e_score_correction_bias"]),
        "f1_guT": a["L1_ffn_gate_up_proj"][:32].transpose(2, 0, 1),
        "f1_downT": a["L1_ffn_down_proj"].transpose(0, 2, 1).reshape(16, 128, D).transpose(1, 0, 2),
        "ctx": a["ctx_768"], "a2_mask": np.tile(np.asarray(a["mask_BxS2_bk0"]).reshape(1, B, S), (S, 1, 1)),
        "a2_lnx_g": col(a["L2_xattn_ln_x_g"]), "a2_lnx_b": col(a["L2_xattn_ln_x_b"]),
        "a2_lnl_g": col(a["L2_xattn_ln_l_g"]), "a2_lnl_b": col(a["L2_xattn_ln_l_b"]),
        "a2_qn": col(np.tile(a["L2_xattn_qn_g"], 2)), "a2_kn": col(np.tile(a["L2_xattn_kn_g"], 2)),
        "a2_wc": a["L2_xattn_Wkv"].T, "a2_wl": np.concatenate([a["L2_xattn_Wq"], a["L2_xattn_Wlkv"]]).T,
        "a2_wo": a["L2_xattn_Wo"].T, "a2_bo": a["L2_xattn_bo"].reshape(1, D),
        "f2_gateT": a["L2_ffn_gate_w"].T,
        "f2_w1T": a["L2_ffn_w1"].transpose(2, 0, 1), "f2_b1": a["L2_ffn_b1"].T,
        "f2_w2T": a["L2_ffn_w2"].transpose(2, 0, 1), "f2_b2": a["L2_ffn_b2"],
        "a3_wq": in_halves(a["L3_xattn_w_q"]), "a3_wk": in_halves(a["L3_xattn_w_kv"][:, :1024]),
        "a3_wv": a["L3_xattn_w_kv"][:, 1024:],
        "a3_wo": a["L3_xattn_w_out"].reshape(8, 128, D).transpose(1, 0, 2), "a3_bo": a["L3_xattn_b_out"].reshape(1, D),
        "f3_wr": col(a["L3_ffn_w_router"]), "f3_wb": a["L3_ffn_w_block"],
    }
    return {k: np.ascontiguousarray(v) for k, v in laid.items()}


def build(nc, t, out):
    with ExitStack() as ctx:
        core = Core(nc, ctx)
        setup(core, t["x"], t["gates"])
        core.end_layer()
        layer0_cosine(core, t["ctxT"], t["c0_wvT"], t["c0_bv"], t["c0_wtT"], t["c0_bt"])
        core.end_layer()
        layer1_soft_moe(core, t["f0_phi"], t["f0_w"], t["f0_bias"])
        core.end_layer()
        layer2_attention(core, t["ctxT"], t["a1_wq"], t["a1_bq"], t["a1_wk"], t["a1_bk"], t["a1_wv"], t["a1_bv"],
                         t["a1_w1"], t["a1_b1"], t["a1_w2"], t["a1_b2"], t["a1_mask"])
        core.end_layer()
        layer3_experts(core, t["f1_routerT"], t["f1_bias"], t["f1_guT"], t["f1_downT"])
        core.end_layer()
        layer4_perceiver(core, t["ctx"], t["a2_mask"], t["a2_lnx_g"], t["a2_lnx_b"], t["a2_lnl_g"], t["a2_lnl_b"],
                         t["a2_qn"], t["a2_kn"], t["a2_wc"], t["a2_wl"], t["a2_wo"], t["a2_bo"])
        core.end_layer()
        layer5_experts(core, t["f2_gateT"], t["f2_w1T"], t["f2_b1"], t["f2_w2T"], t["f2_b2"])
        core.end_layer()
        layer6_attention(core, t["ctxT"], t["a3_wq"], t["a3_wk"], t["a3_wv"], t["a3_wo"], t["a3_bo"])
        core.end_layer()
        layer7_selected_gelu(core, t["f3_wr"], t["f3_wb"])
        core.end_layer()
        store(core, out)


def kernel(**inputs):
    import concourse.bacc as bacc
    from concourse.bass_utils import run_bass_kernel_spmd

    nc = bacc.Bacc("TRN2", target_bir_lowering=False, num_devices=1)
    laid = arrays(inputs)
    t = {k: nc.dram_tensor("in_" + k, v.shape, mybir.dt.from_np(v.dtype), kind="ExternalInput").ap() for k, v in laid.items()}
    out = nc.dram_tensor("out", (B, S, D), F32, kind="ExternalOutput").ap()
    build(nc, t, out)
    return run_bass_kernel_spmd(nc, [{"in_" + k: v for k, v in laid.items()}], core_ids=[0]).results[0]["out"]
```

```python
from contextlib import ExitStack

import numpy as np

import concourse.bass as bass
from concourse import mybir

F32 = mybir.dt.float32
ALU = mybir.AluOpType
ACT = mybir.ActivationFunctionType
AX = mybir.AxisListType

B, S, D, C = 32, 128, 128, 96
G = 4
GROUPS = B // G
PAIRS = GROUPS // 2
N = G * S
LN_EPS = 1e-5
BIG = 3.0e38


class Core:

    def __init__(self, nc, ctx):
        self.nc, self.ctx, self.layer_semaphores = nc, ctx, []
        self.X = self.sbuf("x_resident", [S, B, D])
        self.ident = self.sbuf("ident", [128, 128])
        self.ones = self.sbuf("ones", [128, 128])
        self.gates = self.sbuf("gates", [128, 8])
        self.eps = self.sbuf("eps", [128, B])
        self.minus_half = self.sbuf("minus_half", [128, B])
        self.X_groups = self.X[:, :, :].rearrange("p (i s j) d -> p i s j d", s=2, j=G)

    def sbuf(self, name, shape, dt=F32, ctx=None):
        return (ctx or self.ctx).enter_context(self.nc.sbuf_tensor(name, shape, dt))

    def psum(self, ctx, name, shape):
        return ctx.enter_context(self.nc.psum_tensor(name, shape, F32))

    def sem(self, ctx, name):
        handle = self.nc.alloc_semaphore(name)
        self.layer_semaphores.append(handle)
        return handle

    def end_layer(self):
        self.nc.clear_and_free_semaphores(self.layer_semaphores)
        self.layer_semaphores = []
        self.nc.all_engine_barrier()


def turns(eng, body):
    with eng.Fori(0, PAIRS - 1) as i:
        body(i, 0, i * 2, (i, 1, i * 2 + 1))
        body(i, 1, i * 2 + 1, (i + 1, 0, i * 2 + 2))
    i = PAIRS - 1
    body(i, 0, i * 2, (i, 1, i * 2 + 1))
    body(i, 1, i * 2 + 1, None)


def settled(eng, sem, value, passed):
    eng.wait_ge(sem, value)
    eng.sem_inc(passed, 1)


class Norm:

    def __init__(self, core, ctx, layer, bank, width=D, slots=2, source=None):
        self.core, self.nc, self.bank, self.width = core, core.nc, bank, width
        self.source = source or (lambda i, s: core.X_groups[:, i, s])
        sb = lambda name, shape: core.sbuf(f"{layer}_{name}", shape, ctx=ctx)
        self.stats = sb("stats", [S, slots, G, 6])
        self.mv = sb("mean_var", [S, slots, G, 2])
        self.veps = sb("var_eps", [S, slots, G])
        self.rstd = sb("rstd", [S, slots, G])
        self.xn = sb("xn", [S, slots, G, width])
        self.xT = sb("xT", [width, slots, N])
        sem = lambda name: core.sem(ctx, f"{layer}_{name}")
        self.stats_done, self.mv_done, self.veps_done = sem("stats_done"), sem("mv_done"), sem("veps_done")
        self.rstd_done, self.xn_done = sem("rstd_done"), sem("xn_done")
        self.turned, self.xT_ready = sem("turned"), sem("xT_ready")
        self.passed = sem("passed")

    def vector_stats(self, dve, i, s, it):
        x = self.source(i, s)
        for j in range(G):
            last = self.nc.vector.bn_stats(self.stats[:, s, j, :], x[:, j, :])
        last.then_inc(self.stats_done, 1)
        settled(dve, self.stats_done, it + 1, self.passed)
        for j in range(G):
            last = self.nc.vector.bn_aggr(self.mv[:, s, j, :], self.stats[:, s, j, :])
        last.then_inc(self.mv_done, 1)

    def gpsimd_rstd(self, pool, i, s, it):
        core = self.core
        pool.wait_ge(self.mv_done, it + 1)
        self.nc.gpsimd.tensor_tensor(self.veps[:, s, :], self.mv[:, s, :, 1], core.eps[:, 0:G],
                                     ALU.add).then_inc(self.veps_done, 1)
        pool.wait_ge(self.veps_done, it + 1)
        self.nc.gpsimd.tensor_tensor(self.rstd[:, s, :], self.veps[:, s, :], core.minus_half[:, 0:G],
                                     ALU.pow).then_inc(self.rstd_done, 1)

    def vector_normalise(self, dve, i, s, it):
        x = self.source(i, s)
        dve.wait_ge(self.rstd_done, it + 1)
        for j in range(G):
            last = self.nc.vector.tensor_scalar(self.xn[:, s, j, :], x[:, j, :], self.mv[:, s, j, 0:1],
                                                self.rstd[:, s, j:j + 1], ALU.subtract, ALU.mult)
        last.then_inc(self.xn_done, 1)

    def vector(self, dve, i, s, it):
        self.vector_stats(dve, i, s, it)
        self.vector_normalise(dve, i, s, it)

    def tensor_turn(self, pe, i, s, it):
        pe.wait_ge(self.xn_done, it + 1)
        for j in range(G):
            last = self.nc.tensor.transpose(self.bank[0:self.width, j * S:(j + 1) * S],
                                            self.xn[:, s, j, :], self.core.ident[:, :])
        last.then_inc(self.turned, 1)

    def scalar_copy(self, act, i, s, it):
        act.wait_ge(self.turned, it + 1)
        self.nc.scalar.activation(self.xT[:, s, :], self.bank[0:self.width, :],
                                  ACT.Copy).then_inc(self.xT_ready, 1)


def load(eng, sem, pairs):
    for to, source in pairs:
        eng.dma_start(to, source).then_inc(sem, 16)
    return 16 * len(pairs)


def setup(core, x, gates):
    nc, X = core.nc, core.X
    with ExitStack() as ctx:
        raw = core.sbuf("raw_gates", [128, 8], ctx=ctx)
        landed, made = core.sem(ctx, "inputs_landed"), core.sem(ctx, "constants_made")
        with nc.Block() as block:
            @block.sync
            def _(sp):
                sp.dma_start(raw[:, :], gates).then_inc(landed, 16)
                sp.dma_start(X[:, :, :], x.rearrange("b s d -> s b d")).then_inc(landed, 16)
                sp.wait_ge(landed, 32)

            @block.gpsimd
            def _(pool):
                nc.gpsimd.memset(core.ones[:, :], 1.0)
                nc.gpsimd.memset(core.eps[:, :], LN_EPS)
                nc.gpsimd.memset(core.minus_half[:, :], -0.5)
                nc.gpsimd.memset(core.ident[:, :], 0.0).then_inc(made, 1)
                pool.wait_ge(made, 1)
                nc.gpsimd.affine_select(out=core.ident[:, :], in_=core.ident[:, :], compare_op=ALU.not_equal,
                                        fill=1.0, base=0, pattern=[[-1, 128]], channel_multiplier=1)

            @block.scalar
            def _(act):
                act.wait_ge(landed, 32)
                nc.scalar.activation(core.gates[:, :], raw[:, :], ACT.Tanh)


def layer0_cosine(core, ctxT, wvT, bv, wtT, bt):
    nc, H, EPS = core.nc, 64, 1e-8
    with ExitStack() as ctx:
        sb = lambda name, shape: core.sbuf("c0_" + name, shape, ctx=ctx)
        sem = lambda name: core.sem(ctx, "c0_" + name)
        bank = [core.psum(ctx, f"c0_bank{k}", [128, 512]) for k in range(8)]
        norm = Norm(core, ctx, "c0", bank[0])
        wv, wt, bvc, btc = sb("wv", [D, H]), sb("wt", [C, H]), sb("bv", [H, 1]), sb("bt", [H, 1])
        cT = sb("cT", [C, 2, N])
        vT, tT, v2, t2 = (sb(n, [H, 2, N]) for n in ("vT", "tT", "v2", "t2"))
        tn, vn = sb("tn", [S, 2, N]), sb("vn", [S, 2, G])
        den, rden, cosine = sb("den", [S, 2, N]), sb("rden", [S, 2, N]), sb("cosine", [S, 2, N])
        vps, tps = bank[1], bank[2]
        dots, tn2 = bank[3:5], bank[5:7]
        vn2 = bank[7]
        weights, ctx_landed = sem("weights"), [sem("ctx_landed0"), sem("ctx_landed1")]
        projected, squared, summed, rooted = (sem(n) for n in ("projected", "squared", "summed", "rooted"))
        den_done, rden_done, cosine_done, updated = (
            sem(n) for n in ("den_done", "rden_done", "cosine_done", "updated"))
        ctx_groups = ctxT.rearrange("c (i s n) -> c i s n", s=2, n=N)
        with nc.Block() as block:
            @block.sync
            def _(sp):
                load(sp, weights, [(wv[:, :], wvT), (wt[:, :], wtT), (bvc[:, :], bv), (btc[:, :], bt)])

                def group(i, s, it, nxt):
                    sp.wait_ge(updated, it + 1)
                    sp.dma_start(cT[:, s, :], ctx_groups[:, i, s, :]).then_inc(ctx_landed[s], 16)
                turns(sp, group)

            @block.gpsimd
            def _(pool):
                turns(pool, lambda i, s, it, nxt: norm.gpsimd_rstd(pool, i, s, it))

            @block.vector
            def _(dve):
                dve.sem_inc(updated, 2)
                norm.vector(dve, 0, 0, 0)

                def group(i, s, it, nxt):
                    x = core.X_groups[:, i, s]
                    if nxt:
                        norm.vector(dve, *nxt)
                    dve.wait_ge(rooted, it + 1)
                    for j in range(G):
                        js = slice(j * S, (j + 1) * S)
                        last = nc.vector.tensor_scalar(den[:, s, js], tn[:, s, js], vn[:, s, j:j + 1], EPS,
                                                       ALU.mult, ALU.max)
                    last.then_inc(den_done, 1)
                    dve.wait_ge(den_done, it + 1)
                    nc.vector.reciprocal(rden[:, s, :], den[:, s, :]).then_inc(rden_done, 1)
                    dve.wait_ge(rden_done, it + 1)
                    nc.vector.tensor_tensor(cosine[:, s, :], dots[s][:, :], rden[:, s, :],
                                            ALU.mult).then_inc(cosine_done, 1)
                    dve.wait_ge(cosine_done, it + 1)
                    nc.vector.scalar_tensor_tensor(
                        out=x, in0=cosine[:, s, :].rearrange("p (j d) -> p j d", j=G), scalar=core.gates[:, 0:1],
                        in1=x, op0=ALU.mult, op1=ALU.add).then_inc(updated, 1)
                turns(dve, group)

            @block.scalar
            def _(act):
                act.wait_ge(weights, 64)
                norm.scalar_copy(act, 0, 0, 0)

                def group(i, s, it, nxt):
                    act.wait_ge(projected, it + 1)
                    for out, ps, bias, func in ((vT, vps, bvc, ACT.Identity), (v2, vps, bvc, ACT.Square),
                                                (tT, tps, btc, ACT.Identity), (t2, tps, btc, ACT.Square)):
                        last = nc.scalar.activation(out[:, s, :], ps[0:H, :], func, bias=bias[:, 0:1])
                    last.then_inc(squared, 1)
                    if nxt:
                        norm.scalar_copy(act, *nxt)
                    act.wait_ge(summed, it + 1)
                    nc.scalar.activation(tn[:, s, :], tn2[s][:, :], ACT.Sqrt)
                    nc.scalar.activation(vn[:, s, :], vn2[:, 8 * s:8 * s + G], ACT.Sqrt).then_inc(rooted, 1)
                turns(act, group)

            @block.tensor
            def _(pe):
                pe.wait_ge(weights, 64)
                norm.tensor_turn(pe, 0, 0, 0)

                def group(i, s, it, nxt):
                    pe.wait_ge(ctx_landed[s], i * 16 + 16)
                    nc.tensor.matmul(tps[0:H, :], wt[:, :], cT[:, s, :], start=True, stop=True)
                    pe.wait_ge(norm.xT_ready, it + 1)
                    nc.tensor.matmul(vps[0:H, :], wv[:, :], norm.xT[:, s, :], start=True,
                                     stop=True).then_inc(projected, 1)
                    if nxt:
                        norm.tensor_turn(pe, *nxt)
                    pe.wait_ge(squared, it + 1)
                    for j in range(G):
                        js = slice(j * S, (j + 1) * S)
                        nc.tensor.matmul(dots[s][:, js], vT[:, s, js], tT[:, s, js], start=True, stop=True)
                        nc.tensor.matmul(vn2[:, 8 * s + j:8 * s + j + 1], v2[:, s, js], core.ones[0:H, 0:1],
                                         start=True, stop=True)
                    nc.tensor.matmul(tn2[s][:, :], core.ones[0:H, :], t2[:, s, :], start=True,
                                     stop=True).then_inc(summed, 1)
                turns(pe, group)


QUADS = 4
UNITS = G * QUADS


class Attention:

    def __init__(self, core, ctx, layer, score_banks, turn_banks, scale):
        self.core, self.nc, self.scale = core, core.nc, scale
        self.score_banks, self.turn_banks = score_banks, turn_banks
        sb = lambda name, shape: core.sbuf(f"{layer}_{name}", shape, ctx=ctx)
        sem = lambda name: core.sem(ctx, f"{layer}_{name}")
        self.negmax = sb("negmax", [S, 2, 4])
        self.shifted = sb("shifted", [S, 2, 4, S])
        self.weights = sb("probs", [S, 2, 4, S])
        self.turned = sb("probsT", [S, 2, 4, S])
        self.scored, self.maxed, self.shifts = sem("scored"), sem("maxed"), sem("shifts")
        self.exps, self.flips, self.copies, self.weighed = sem("exps"), sem("flips"), sem("copies"), sem("weighed")

    def tensor_scores(self, pe, it, u, matmuls):
        pe.wait_ge(self.shifts, it * UNITS + u + 1)
        matmuls(self.score_banks[u % 2], u // QUADS, u % QUADS).then_inc(self.scored, 1)

    def vector_shift(self, dve, it, u):
        scores = self.score_banks[u % 2][:, :].rearrange("p (h k) -> p h k", h=4)
        negmax = self.negmax[:, u % 2, :]
        dve.wait_ge(self.scored, it * UNITS + u + 1)
        self.nc.vector.tensor_reduce(negmax, scores, AX.X, ALU.max, negate=True).then_inc(self.maxed, 1)
        dve.wait_ge(self.exps, it * UNITS + u + 1)
        dve.wait_ge(self.maxed, it * UNITS + u + 1)
        self.nc.vector.tensor_tensor(self.shifted[:, u % 2], scores,
                                     negmax.unsqueeze(2).to_broadcast([S, 4, S]), ALU.add).then_inc(self.shifts, 1)

    def scalar_exp(self, act, it, u):
        act.wait_ge(self.flips, it * UNITS + u + 1)
        act.wait_ge(self.shifts, it * UNITS + u + 3)
        self.nc.scalar.activation(self.weights[:, u % 2], self.shifted[:, u % 2], ACT.Exp,
                                  scale=self.scale).then_inc(self.exps, 1)

    def tensor_turn(self, pe, it, u):
        pe.wait_ge(self.copies, it * UNITS + u + 1)
        pe.wait_ge(self.exps, it * UNITS + u + 3)
        for h in range(4):
            last = self.nc.tensor.transpose(self.turn_banks[u % 2][:, h * S:(h + 1) * S],
                                            self.weights[:, u % 2, h, :], self.core.ident[:, :])
        last.then_inc(self.flips, 1)

    def scalar_copy(self, act, it, u):
        act.wait_ge(self.weighed, it * UNITS + u + 1)
        act.wait_ge(self.flips, it * UNITS + u + 3)
        self.nc.scalar.activation(self.turned[:, u % 2], self.turn_banks[u % 2][:, :], ACT.Copy).then_inc(self.copies, 1)

    def tensor_weigh(self, pe, it, u, out, values):
        pe.wait_ge(self.copies, it * UNITS + u + 3)
        for k in range(4):
            last = self.nc.tensor.matmul(out(u // QUADS, u % QUADS * 4 + k), self.turned[:, u % 2, k, :],
                                         values(u // QUADS, u % QUADS * 4 + k), start=True, stop=True)
        last.then_inc(self.weighed, 1)

    def vector_start(self, dve):
        dve.sem_inc(self.shifts, 2)

    def scalar_start(self, act):
        act.sem_inc(self.exps, 2)
        act.sem_inc(self.copies, 2)

    def tensor_start(self, pe):
        pe.sem_inc(self.flips, 2)
        pe.sem_inc(self.weighed, 2)


def stream(eng, body):
    place = lambda i, s: (i, s, i * 2 + s)

    def turn(i, first=False, last=False):
        body(place(i, 0), None if first else place(i - 1, 1), place(i, 1), None if last else place(i + 1, 0))
        body(place(i, 1), place(i, 0), None if last else place(i + 1, 0), None if last else place(i + 1, 1))
    turn(0, first=True)
    with eng.Fori(1, PAIRS - 1) as i:
        turn(i)
    turn(PAIRS - 1, last=True)


def unit_at(at, after, u):
    return (at, u) if u < UNITS else (after, u - UNITS) if after else None


def layer2_attention(core, ctxT, wq, bq, wk, bk, wv, bv_rows, w1, b1, w2, b2_row, head_mask):
    nc, HEADS, DH, FF = core.nc, 16, 8, 2 * D
    with ExitStack() as ctx:
        sb = lambda name, shape: core.sbuf("a1_" + name, shape, ctx=ctx)
        sem = lambda name: core.sem(ctx, "a1_" + name)
        bank = [core.psum(ctx, f"a1_bank{k}", [128, 512]) for k in range(8)]
        norm = Norm(core, ctx, "a1", bank[0])
        att = Attention(core, ctx, "a1", bank[1:3], bank[3:5], DH ** -0.5)
        out_banks, mlp_bank = bank[5:7], bank[7]
        wq_s, wk_s, wv_s = sb("wq", [D, D]), sb("wk", [C, D]), sb("wv", [C, D])
        bq_s, bk_s, bv_s = sb("bq", [D, 1]), sb("bk", [D, 1]), sb("bv", [S, D])
        w1_s, b1_s = sb("w1", [D, FF]), sb("b1", [128, 2])
        w2_s, b2_s = sb("w2", [128, 2, D]), sb("b2", [1, D])
        mask = sb("mask", [D, HEADS])
        cT = sb("cT", [C, 2, N])
        qT, kT = sb("qT", [D, 2, N]), sb("kT", [D, 2, N])
        km = sb("k_masked", [D, 2, HEADS, G, S])
        v = sb("v_ones", [S, 2, G, HEADS, DH + 1])
        rsum, o = sb("rsum", [S, 2, HEADS]), sb("o", [S, 2, G, D])
        oT, hT = sb("oT", [D, N]), sb("hT", [128, 2, N])
        weights, ctx_landed, ones_set = sem("weights"), [sem("ctx_landed0"), sem("ctx_landed1")], sem("ones_set")
        k_projected, q_projected, v_projected = sem("k_projected"), sem("q_projected"), sem("v_projected")
        k_ready, q_ready, v_ready = sem("k_ready"), sem("q_ready"), sem("v_ready")
        masked_dve, masked_pool = sem("k_masked_by_vector"), sem("k_masked_by_gpsimd")
        sums_inverted, normalised, passed = sem("sums_inverted"), sem("normalised"), sem("masks_passed")
        o_turned, oT_ready, hidden, h_ready, mixed, updated = (
            sem(n) for n in ("o_turned", "oT_ready", "hidden", "h_ready", "mixed", "updated"))
        ctx_groups = ctxT.rearrange("c (i s n) -> c i s n", s=2, n=N)
        loads = [(wq_s[:, :], wq), (wk_s[:, :], wk), (wv_s[:, :], wv), (bq_s[:, :], bq), (bk_s[:, :], bk),
                 (bv_s[:, :], bv_rows), (w1_s[:, :], w1), (b1_s[:, :], b1), (w2_s[:, :, :], w2), (b2_s[:, :], b2_row),
                 (mask[:, :], head_mask)]
        LOADED = 16 * len(loads)
        BY_VECTOR = 11
        BY_POOL = HEADS - BY_VECTOR
        FIRST, LAST = (0, 0, 0), (PAIRS - 1, 1, GROUPS - 1)
        K_AT, Q_AT, V_AT, TURN_AT, HIDDEN_AT, MIX_AT = 0, 2, 4, 1, (3, 5), 7

        with nc.Block() as block:
            @block.sync
            def _(sp):
                for s in range(2):
                    sp.dma_start(cT[:, s, :], ctx_groups[:, 0, s, :]).then_inc(ctx_landed[s], 16)
                load(sp, weights, loads)
                with sp.Fori(1, PAIRS) as i:
                    for s in range(2):
                        sp.wait_ge(k_projected, i * 2 + s - 1)
                        sp.wait_ge(v_projected, i * 2 + s - 1)
                        sp.dma_start(cT[:, s, :], ctx_groups[:, i, s, :]).then_inc(ctx_landed[s], 16)

            @block.gpsimd
            def _(pool):
                nc.gpsimd.memset(v[:, :, :, :, :], 1.0).then_inc(ones_set, 1)
                for it in range(2):
                    norm.gpsimd_rstd(pool, 0, it, it)
                pool.wait_ge(weights, LOADED)

                def mask_keys(at):
                    i, s, it = at
                    settled(pool, k_ready, it + 1, passed)
                    for h in range(BY_VECTOR, HEADS):
                        nc.gpsimd.tensor_scalar(km[:, s, h, :, :], kT[:, s, :].rearrange("p (b k) -> p b k", b=G),
                                                mask[:, h:h + 1], None, ALU.mult).then_inc(masked_pool, 1)
                mask_keys(FIRST)

                def group(at, before, after, after2):
                    if after:
                        mask_keys(after)
                    if after2:
                        norm.gpsimd_rstd(pool, *after2)
                stream(pool, group)

            @block.vector
            def _(dve):
                dve.sem_inc(normalised, 2)
                att.vector_start(dve)
                norm.vector(dve, 0, 0, 0)
                norm.vector(dve, 0, 1, 1)
                dve.wait_ge(weights, LOADED)
                dve.wait_ge(ones_set, 1)

                def bias_values(at, ps):
                    i, s, it = at
                    dve.wait_ge(v_projected, it + 1)
                    nc.vector.tensor_tensor(
                        v[:, s, :, :, 0:DH], ps[:, :].rearrange("p (b h e) -> p b h e", b=G, h=HEADS),
                        bv_s[:, :].rearrange("p (h e) -> p h e", h=HEADS).unsqueeze(1).to_broadcast([S, G, HEADS, DH]),
                        ALU.add).then_inc(v_ready, 1)

                def normalise(at, b):
                    i, s, it = at
                    heads = out_banks[b % 2][:, 0:HEADS * (DH + 1)].rearrange("p (h e) -> p h e", h=HEADS)
                    dve.wait_ge(att.weighed, it * UNITS + 4 * b + 4 + 2)
                    nc.vector.reciprocal(rsum[:, b % 2, :], heads[:, :, DH]).then_inc(sums_inverted, 1)
                    dve.wait_ge(sums_inverted, it * G + b + 1)
                    nc.vector.tensor_tensor(o[:, s, b, :].rearrange("p (h e) -> p h e", h=HEADS), heads[:, :, 0:DH],
                                            rsum[:, b % 2, :].unsqueeze(2).to_broadcast([S, HEADS, DH]),
                                            ALU.mult).then_inc(normalised, 1)

                def update(at):
                    i, s, it = at
                    x = core.X_groups[:, i, s]
                    dve.wait_ge(mixed, it + 1)
                    nc.vector.scalar_tensor_tensor(
                        out=x, in0=mlp_bank[:, :].rearrange("p (j d) -> p j d", j=G), scalar=core.gates[:, 1:2],
                        in1=x, op0=ALU.mult, op1=ALU.add).then_inc(updated, 1)

                def mask_keys(at, h):
                    i, s, it = at
                    dve.wait_ge(k_ready, it + 1)
                    nc.vector.tensor_scalar(km[:, s, h, :, :], kT[:, s, :].rearrange("p (b k) -> p b k", b=G),
                                            mask[:, h:h + 1], None, ALU.mult).then_inc(masked_dve, 1)

                for h in range(BY_VECTOR):
                    mask_keys(FIRST, h)
                bias_values(FIRST, bank[5])
                for u in range(3):
                    att.vector_shift(dve, 0, u)

                def group(at, before, after, after2):
                    for u in range(UNITS):
                        unit = unit_at(at, after, u + 3)
                        if unit:
                            att.vector_shift(dve, unit[0][2], unit[1])
                        if after and u == V_AT:
                            bias_values(after, bank[0])
                        if after and 1 <= u <= BY_VECTOR:
                            mask_keys(after, u - 1)
                        if before and u == MIX_AT:
                            update(before)
                        if u % 4 == 3:
                            normalise(at, u // 4)
                        if after2 and u == 5:
                            norm.vector_stats(dve, *after2)
                        if after2 and u == 11:
                            norm.vector_normalise(dve, *after2)
                stream(dve, group)
                update(LAST)

            @block.scalar
            def _(act):
                att.scalar_start(act)
                act.wait_ge(weights, LOADED)

                def bias_keys(at, ps):
                    act.wait_ge(k_projected, at[2] + 1)
                    nc.scalar.activation(kT[:, at[1], :], ps[:, :], ACT.Identity, bias=bk_s[:, 0:1]).then_inc(k_ready, 1)

                def bias_queries(at, ps):
                    act.wait_ge(q_projected, at[2] + 1)
                    nc.scalar.activation(qT[:, at[1], :], ps[:, :], ACT.Identity, bias=bq_s[:, 0:1]).then_inc(q_ready, 1)

                def copy_turned(at):
                    act.wait_ge(o_turned, at[2] + 1)
                    nc.scalar.activation(oT[:, :], mlp_bank[:, :], ACT.Copy).then_inc(oT_ready, 1)

                def rectify(at, f):
                    act.wait_ge(hidden, at[2] * 2 + f + 1)
                    nc.scalar.activation(hT[:, f, :], mlp_bank[:, :], ACT.Relu, bias=b1_s[:, f:f + 1]).then_inc(h_ready, 1)

                bias_keys(FIRST, bank[3])
                norm.scalar_copy(act, 0, 0, 0)
                bias_queries(FIRST, bank[4])
                norm.scalar_copy(act, 0, 1, 1)
                att.scalar_exp(act, 0, 0)
                att.scalar_copy(act, 0, 0)
                att.scalar_exp(act, 0, 1)
                att.scalar_exp(act, 0, 2)

                def group(at, before, after, after2):
                    for u in range(UNITS):
                        if after and u == K_AT:
                            bias_keys(after, bank[0])
                        if after and u == Q_AT:
                            bias_queries(after, bank[0])
                        for ahead, step in ((1, att.scalar_copy), (3, att.scalar_exp)):
                            unit = unit_at(at, after, u + ahead)
                            if unit:
                                step(act, unit[0][2], unit[1])
                        if before and u == TURN_AT:
                            copy_turned(before)
                        if before and u in HIDDEN_AT:
                            rectify(before, HIDDEN_AT.index(u))
                        if after2 and u == 14:
                            norm.scalar_copy(act, *after2)
                stream(act, group)
                copy_turned(LAST)
                for f in range(2):
                    rectify(LAST, f)

            @block.tensor
            def _(pe):
                att.tensor_start(pe)
                pe.sem_inc(updated, 1)
                pe.wait_ge(weights, LOADED)

                def project_keys(at, ps):
                    i, s, it = at
                    pe.wait_ge(ctx_landed[s], i * 16 + 16)
                    nc.tensor.matmul(ps[:, :], wk_s[:, :], cT[:, s, :], start=True, stop=True).then_inc(k_projected, 1)

                def project_queries(at, ps):
                    pe.wait_ge(norm.xT_ready, at[2] + 1)
                    nc.tensor.matmul(ps[:, :], wq_s[:, :], norm.xT[:, at[1], :], start=True,
                                     stop=True).then_inc(q_projected, 1)

                def project_values(at, ps):
                    for b in range(G):
                        last = nc.tensor.matmul(ps[:, b * S:(b + 1) * S], cT[:, at[1], b * S:(b + 1) * S], wv_s[:, :],
                                                start=True, stop=True)
                    last.then_inc(v_projected, 1)

                def scores(at, u):
                    i, s, it = at

                    def quad_scores(ps, b, quad):
                        if b == 0:
                            pe.wait_ge(masked_dve, it * BY_VECTOR + min(4 * quad + 4, BY_VECTOR))
                            if 4 * quad + 4 > BY_VECTOR:
                                pe.wait_ge(masked_pool, it * BY_POOL + 4 * quad + 4 - BY_VECTOR)
                        return nc.tensor.matmul(ps[:, :], qT[:, s, b * S:(b + 1) * S],
                                                km[:, s, 4 * quad:4 * quad + 4, b, :], start=True, stop=True)
                    att.tensor_scores(pe, it, u, quad_scores)

                def turn_outputs(at):
                    i, s, it = at
                    pe.wait_ge(normalised, it * G + G + 2)
                    pe.wait_ge(updated, it + 1)
                    for b in range(G):
                        last = nc.tensor.transpose(mlp_bank[:, b * S:(b + 1) * S], o[:, s, b, :], core.ident[:, :])
                    last.then_inc(o_turned, 1)

                def hide(at, f):
                    if f == 0:
                        pe.wait_ge(oT_ready, at[2] + 1)
                    else:
                        pe.wait_ge(h_ready, at[2] * 2 + 1)
                    nc.tensor.matmul(mlp_bank[:, :], w1_s[:, f * 128:(f + 1) * 128], oT[:, :], start=True,
                                     stop=True).then_inc(hidden, 1)

                def mix(at):
                    pe.wait_ge(h_ready, at[2] * 2 + 2)
                    for b in range(G):
                        bs = slice(b * S, (b + 1) * S)
                        nc.tensor.matmul(mlp_bank[:, bs], core.ones[0:1, :], b2_s[0:1, :], start=True, stop=False)
                        for f in range(2):
                            last = nc.tensor.matmul(mlp_bank[:, bs], hT[:, f, bs], w2_s[:, f, :], start=False,
                                                    stop=f == 1)
                    last.then_inc(mixed, 1)

                project_keys(FIRST, bank[3])
                norm.tensor_turn(pe, 0, 0, 0)
                project_queries(FIRST, bank[4])
                project_values(FIRST, bank[5])
                norm.tensor_turn(pe, 0, 1, 1)
                pe.wait_ge(q_ready, 1)
                pe.wait_ge(v_ready, 1)
                for u in range(3):
                    scores(FIRST, u)
                att.tensor_turn(pe, 0, 0)

                def group(at, before, after, after2):
                    i, s, it = at
                    for u in range(UNITS):
                        if after and u == K_AT:
                            pe.wait_ge(norm.xT_ready, after[2] + 1)
                            project_keys(after, bank[0])
                        if after and u == Q_AT:
                            pe.wait_ge(k_ready, after[2] + 1)
                            project_queries(after, bank[0])
                        if after and u == V_AT:
                            pe.wait_ge(q_ready, after[2] + 1)
                            project_values(after, bank[0])
                        if after and u == UNITS - 3:
                            pe.wait_ge(v_ready, after[2] + 1)
                        unit = unit_at(at, after, u + 3)
                        if unit:
                            scores(*unit)
                        unit = unit_at(at, after, u + 1)
                        if unit:
                            att.tensor_turn(pe, unit[0][2], unit[1])
                        if before and u == TURN_AT:
                            turn_outputs(before)
                        if before and u in HIDDEN_AT:
                            hide(before, HIDDEN_AT.index(u))
                        if before and u == MIX_AT:
                            mix(before)
                        if u % 4 == 0:
                            pe.wait_ge(normalised, it * G + u // 4 + 1)
                        att.tensor_weigh(pe, it, u,
                                         lambda b, h: out_banks[b % 2][:, h * (DH + 1):(h + 1) * (DH + 1)],
                                         lambda b, h: v[:, s, b, h, :])
                        if after2 and u == 13:
                            norm.tensor_turn(pe, *after2)
                stream(pe, group)
                turn_outputs(LAST)
                for f in range(2):
                    hide(LAST, f)
                mix(LAST)


def layer6_attention(core, ctxT, wq, wk, wv, wo, bo_row):
    nc, HEADS, DH = core.nc, 16, 64
    TILES = HEADS * DH // 128
    PROJECTIONS = 3 * TILES
    with ExitStack() as ctx:
        sb = lambda name, shape: core.sbuf("a3_" + name, shape, ctx=ctx)
        sem = lambda name: core.sem(ctx, "a3_" + name)
        bank = [core.psum(ctx, f"a3_bank{k}", [128, 512]) for k in range(8)]
        norm = Norm(core, ctx, "a3", bank[0])
        att = Attention(core, ctx, "a3", bank[1:3], bank[3:5], DH ** -0.5)
        out_banks, mix_bank = bank[5:7], bank[7]
        start_banks = bank[3:7]
        wq_s, wk_s, wv_s = sb("wq", [D, HEADS * DH]), sb("wk", [C, HEADS * DH]), sb("wv", [C, HEADS * DH])
        wo_s, bo_s = sb("wo", [128, TILES, D]), sb("bo", [1, D])
        cT = sb("cT", [C, 2, N])
        qT, kT = sb("qT", [128, 2, TILES, N]), sb("kT", [128, 2, TILES, N])
        v = sb("v_ones", [S, 2, G, HEADS, DH + 1])
        rsum, o, oT = sb("rsum", [S, 2, 4]), sb("o", [S, 2, HEADS * DH]), sb("oT", [128, TILES, S])
        weights, ctx_landed, ones_set = sem("weights"), [sem("ctx_landed0"), sem("ctx_landed1")], sem("ones_set")
        projected, emptied = [sem("projected_even"), sem("projected_odd")], [sem("emptied_by_scalar"), sem("emptied_by_vector")]
        sums_inverted, normalised = sem("sums_inverted"), sem("normalised")
        o_turned, oT_ready, mixed, updated = (sem(n) for n in ("o_turned", "oT_ready", "mixed", "updated"))
        ctx_groups = ctxT.rearrange("c (i s n) -> c i s n", s=2, n=N)
        loads = [(wq_s[:, :], wq), (wk_s[:, :], wk), (wv_s[:, :], wv), (wo_s[:, :, :], wo), (bo_s[:, :], bo_row)]
        LOADED = 16 * len(loads)
        HALF = PROJECTIONS // 2

        def projection_out(s, n):
            if n < TILES:
                return qT[:, s, n, :]
            if n < 2 * TILES:
                return kT[:, s, n - TILES, :]
            b, half = divmod(n - 2 * TILES, 2)
            return v[:, s, b, 8 * half:8 * half + 8, 0:DH]

        def projection_in(bank_of, n):
            return bank_of[:, :] if n < 2 * TILES else bank_of[:, :].rearrange("p (h e) -> p h e", e=DH)

        def tail_of(at, before, u):
            b, phase = divmod(u - 4, 4)
            return (at, b, phase) if b >= 0 else (before, G - 1, phase) if before else (None, 0, 3)

        with nc.Block() as block:
            @block.sync
            def _(sp):
                for s in range(2):
                    sp.dma_start(cT[:, s, :], ctx_groups[:, 0, s, :]).then_inc(ctx_landed[s], 16)
                load(sp, weights, loads)
                with sp.Fori(1, PAIRS) as i:
                    for s in range(2):
                        for k in range(2):
                            sp.wait_ge(projected[k], (i * 2 + s - 1) * HALF)
                        sp.dma_start(cT[:, s, :], ctx_groups[:, i, s, :]).then_inc(ctx_landed[s], 16)

            @block.gpsimd
            def _(pool):
                nc.gpsimd.memset(v[:, :, :, :, :], 1.0).then_inc(ones_set, 1)
                for it in range(2):
                    norm.gpsimd_rstd(pool, 0, it, it)

                def group(at, before, after, after2):
                    if after2:
                        norm.gpsimd_rstd(pool, *after2)
                stream(pool, group)

            @block.vector
            def _(dve):
                dve.sem_inc(normalised, 2)
                dve.sem_inc(updated, 1)
                att.vector_start(dve)
                norm.vector(dve, 0, 0, 0)
                norm.vector(dve, 0, 1, 1)
                dve.wait_ge(ones_set, 1)

                def empty(at, n, bank_of):
                    i, s, it = at
                    dve.wait_ge(projected[1], it * HALF + n // 2 + 1)
                    nc.vector.tensor_copy(projection_out(s, n), projection_in(bank_of, n)).then_inc(emptied[1], 1)

                def normalise(it, u):
                    heads = out_banks[u % 2][:, 0:4 * (DH + 1)].rearrange("p (h e) -> p h e", h=4)
                    dve.wait_ge(att.weighed, it * UNITS + u + 3)
                    nc.vector.reciprocal(rsum[:, u % 2, :], heads[:, :, DH]).then_inc(sums_inverted, 1)
                    dve.wait_ge(sums_inverted, it * UNITS + u + 1)
                    b, quad = divmod(u, 4)
                    nc.vector.tensor_tensor(
                        o[:, b % 2, quad * 4 * DH:(quad + 1) * 4 * DH].rearrange("p (h e) -> p h e", h=4),
                        heads[:, :, 0:DH], rsum[:, u % 2, :].unsqueeze(2).to_broadcast([S, 4, DH]),
                        ALU.mult).then_inc(normalised, 1)

                def update(at, b):
                    i, s, it = at
                    x = core.X_groups[:, i, s, b, :]
                    dve.wait_ge(mixed, it * G + b + 1)
                    nc.vector.scalar_tensor_tensor(out=x, in0=mix_bank[:, 0:D], scalar=core.gates[:, 3:4],
                                                   in1=x, op0=ALU.mult, op1=ALU.add).then_inc(updated, 1)

                for n in range(1, PROJECTIONS, 2):
                    empty((0, 0, 0), n, start_banks[n % 4])
                for u in range(3):
                    att.vector_shift(dve, 0, u)

                def group(at, before, after, after2):
                    for u in range(UNITS):
                        ahead = unit_at(at, after, u + 3)
                        if ahead:
                            att.vector_shift(dve, ahead[0][2], ahead[1])
                        if after and u < HALF:
                            empty(after, 2 * u + 1, bank[0])
                        place, b, phase = tail_of(at, before, u)
                        if phase == 2 and place:
                            update(place, b)
                        normalise(at[2], u)
                        if after2 and u == 5:
                            norm.vector_stats(dve, *after2)
                        if after2 and u == 9:
                            norm.vector_normalise(dve, *after2)
                stream(dve, group)
                update((PAIRS - 1, 1, GROUPS - 1), G - 1)

            @block.scalar
            def _(act):
                att.scalar_start(act)
                norm.scalar_copy(act, 0, 0, 0)
                act.wait_ge(ones_set, 1)

                def empty(at, n, bank_of):
                    i, s, it = at
                    act.wait_ge(projected[0], it * HALF + n // 2 + 1)
                    nc.scalar.activation(projection_out(s, n), projection_in(bank_of, n), ACT.Copy)\
                        .then_inc(emptied[0], 1)

                def copy_turned(at, b, half):
                    act.wait_ge(o_turned, at[2] * 2 * G + 2 * b + half + 1)
                    nc.scalar.activation(oT[:, 4 * half:4 * half + 4, :],
                                         mix_bank[:, :].rearrange("p (t n) -> p t n", t=4), ACT.Copy).then_inc(oT_ready, 1)

                for n in range(0, PROJECTIONS, 2):
                    empty((0, 0, 0), n, start_banks[n % 4])
                norm.scalar_copy(act, 0, 1, 1)
                att.scalar_exp(act, 0, 0)
                att.scalar_copy(act, 0, 0)
                att.scalar_exp(act, 0, 1)
                att.scalar_exp(act, 0, 2)

                def group(at, before, after, after2):
                    for u in range(UNITS):
                        if after and u < HALF:
                            empty(after, 2 * u, bank[0])
                        for ahead, step in ((1, att.scalar_copy), (3, att.scalar_exp)):
                            unit = unit_at(at, after, u + ahead)
                            if unit:
                                step(act, unit[0][2], unit[1])
                        place, b, phase = tail_of(at, before, u)
                        if phase < 2 and place:
                            copy_turned(place, b, phase)
                        if after2 and u == 14:
                            norm.scalar_copy(act, *after2)
                stream(act, group)
                for half in range(2):
                    copy_turned((PAIRS - 1, 1, GROUPS - 1), G - 1, half)

            @block.tensor
            def _(pe):
                att.tensor_start(pe)
                pe.wait_ge(weights, LOADED)

                def project(at, n, ps):
                    i, s, it = at
                    kind, t = divmod(n, TILES)
                    if kind < 2:
                        w, tokens = ((wq_s, norm.xT), (wk_s, cT))[kind]
                        mm = nc.tensor.matmul(ps[:, :], w[:, t * 128:(t + 1) * 128], tokens[:, s, :],
                                              start=True, stop=True)
                    else:
                        b, half = divmod(t, 2)
                        mm = nc.tensor.matmul(ps[:, :], cT[:, s, b * S:(b + 1) * S],
                                              wv_s[:, half * 512:half * 512 + 512], start=True, stop=True)
                    mm.then_inc(projected[n % 2], 1)

                def project_ahead(at, n):
                    i, s, it = at
                    if n == 0:
                        pe.wait_ge(ctx_landed[s], i * 16 + 16)
                        pe.wait_ge(norm.xT_ready, it + 1)
                    else:
                        pe.wait_ge(emptied[(n - 1) % 2], it * HALF + (n - 1) // 2 + 1)
                    project(at, n, bank[0])

                def wait_emptied(it):
                    for k in range(2):
                        pe.wait_ge(emptied[k], it * HALF + HALF)

                def scores(at, u):
                    i, s, it = at

                    def quad_scores(ps, b, quad):
                        r = 64 * (quad % 2)
                        for k in range(4):
                            t = 4 * (quad // 2) + k
                            last = nc.tensor.matmul(ps[:, k * S:(k + 1) * S], qT[r:r + 64, s, t, b * S:(b + 1) * S],
                                                    kT[r:r + 64, s, t, b * S:(b + 1) * S], start=True, stop=True)
                        return last
                    att.tensor_scores(pe, it, u, quad_scores)

                def tail(at, b, phase):
                    it = at[2]
                    if phase < 2:
                        if phase == 0:
                            pe.wait_ge(normalised, it * UNITS + 4 * b + 4 + 2)
                            pe.wait_ge(updated, it * G + b + 1)
                        else:
                            pe.wait_ge(oT_ready, it * 2 * G + 2 * b + 1)
                        for k in range(4):
                            t = 4 * phase + k
                            last = nc.tensor.transpose(mix_bank[:, k * S:(k + 1) * S], o[:, b % 2, t * 128:(t + 1) * 128],
                                                       core.ident[:, :])
                        last.then_inc(o_turned, 1)
                    elif phase == 2:
                        pe.wait_ge(oT_ready, it * 2 * G + 2 * b + 2)
                        nc.tensor.matmul(mix_bank[:, 0:D], core.ones[0:1, :], bo_s[0:1, :], start=True, stop=False)
                        for t in range(TILES):
                            last = nc.tensor.matmul(mix_bank[:, 0:D], oT[:, t, :], wo_s[:, t, :], start=False,
                                                    stop=t == TILES - 1)
                        last.then_inc(mixed, 1)

                norm.tensor_turn(pe, 0, 0, 0)
                pe.wait_ge(ctx_landed[0], 16)
                pe.wait_ge(norm.xT_ready, 1)
                for n in range(PROJECTIONS):
                    if n >= 4:
                        pe.wait_ge(emptied[n % 2], (n - 4) // 2 + 1)
                    project((0, 0, 0), n, start_banks[n % 4])
                norm.tensor_turn(pe, 0, 1, 1)
                wait_emptied(0)
                for u in range(3):
                    scores((0, 0, 0), u)
                att.tensor_turn(pe, 0, 0)

                def group(at, before, after, after2):
                    i, s, it = at
                    for u in range(UNITS):
                        if after and u < HALF:
                            project_ahead(after, 2 * u)
                        if after and u == UNITS - 3:
                            wait_emptied(after[2])
                        unit = unit_at(at, after, u + 3)
                        if unit:
                            scores(*unit)
                        unit = unit_at(at, after, u + 1)
                        if unit:
                            att.tensor_turn(pe, unit[0][2], unit[1])
                        if after and u < HALF:
                            project_ahead(after, 2 * u + 1)
                        place, b, phase = tail_of(at, before, u)
                        if place:
                            tail(place, b, phase)
                        pe.wait_ge(normalised, it * UNITS + u + 1)
                        att.tensor_weigh(pe, it, u,
                                         lambda b, h: out_banks[u % 2][:, h % 4 * (DH + 1):(h % 4 + 1) * (DH + 1)],
                                         lambda b, h: v[:, s, b, h, :])
                        if after2 and u == 13:
                            norm.tensor_turn(pe, *after2)
                stream(pe, group)
                for phase in range(3):
                    tail((PAIRS - 1, 1, GROUPS - 1), G - 1, phase)


def layer7_selected_gelu(core, w_router, w_block):
    nc, SELECTED = core.nc, S * 3 // 4
    ROUNDS = SELECTED // 8
    with ExitStack() as ctx:
        sb = lambda name, shape: core.sbuf("f3_" + name, shape, ctx=ctx)
        sem = lambda name: core.sem(ctx, "f3_" + name)
        bank = [core.psum(ctx, f"f3_bank{k}", [128, 512]) for k in range(8)]
        norm = Norm(core, ctx, "f3", bank[0])
        wr, wb = sb("wr", [D, 1]), sb("wb", [D, D])
        scores = sb("scores", [S, B])
        scores_v = scores[:, :].rearrange("p (i s j) -> p i s j", s=2, j=G)
        gelu, diff = sb("gelu", [S, 2, G, D]), sb("diff", [S, B, D])
        diff_v = diff[:, :, :].rearrange("p (i s j) d -> p i s j d", s=2, j=G)
        cand, top8, selected, pick = sb("cand", [B, 2, S]), sb("top8", [B, 8]), sb("selected", [B, S]), sb("pick", [S, B])
        weights, scored, score_kept, gelu_done, diff_done, updated = (
            sem(n) for n in ("weights", "scored", "score_kept", "gelu_done", "diff_done", "updated"))
        turned, chain, selected_done, selected_turned, pick_done = (
            sem(n) for n in ("scores_turned", "ranking", "selected_done", "selected_turned", "pick_done"))
        with nc.Block() as block:
            @block.sync
            def _(sp):
                load(sp, weights, [(wr[:, :], w_router), (wb[:, :], w_block)])

            @block.gpsimd
            def _(pool):
                turns(pool, lambda i, s, it, nxt: norm.gpsimd_rstd(pool, i, s, it))

            @block.vector
            def _(dve):
                dve.sem_inc(diff_done, 2)
                norm.vector(dve, 0, 0, 0)

                def group(i, s, it, nxt):
                    if nxt:
                        norm.vector(dve, *nxt)
                    x = core.X_groups[:, i, s]
                    dve.wait_ge(scored, it + 1)
                    nc.vector.tensor_copy(scores_v[:, i, s, :], bank[4 + s][:, 0:G]).then_inc(score_kept, 1)
                    dve.wait_ge(gelu_done, it + 1)
                    nc.vector.tensor_tensor(diff_v[:, i, s], gelu[:, s], norm.xn[:, s], ALU.subtract)\
                        .then_inc(diff_done, 1)
                    nc.vector.scalar_tensor_tensor(out=x, in0=norm.xn[:, s], scalar=core.gates[:, 7:8], in1=x,
                                                   op0=ALU.mult, op1=ALU.add).then_inc(updated, 1)
                turns(dve, group)
                dve.wait_ge(turned, 1)
                nc.vector.tensor_copy(cand[:, 0, :], bank[6][0:B, 0:S]).then_inc(chain, 1)
                for r in range(ROUNDS):
                    dve.wait_ge(chain, 2 * r + 1)
                    nc.vector.max(top8[:, :], cand[:, r % 2, :]).then_inc(chain, 1)
                    dve.wait_ge(chain, 2 * r + 2)
                    nc.vector.match_replace(cand[:, 1 - r % 2, :], top8[:, :], cand[:, r % 2, :], -BIG)\
                        .then_inc(chain, 1)
                dve.wait_ge(chain, 2 * ROUNDS + 1)
                nc.vector.tensor_scalar(selected[:, :], cand[:, ROUNDS % 2, :], -BIG, None, ALU.is_equal)\
                    .then_inc(selected_done, 1)
                dve.wait_ge(selected_turned, 1)
                nc.vector.tensor_scalar(pick[:, :], bank[7][:, 0:B], core.gates[:, 7:8], None, ALU.mult)\
                    .then_inc(pick_done, 1)
                dve.wait_ge(pick_done, 1)
                dve.wait_ge(updated, GROUPS)
                dve.wait_ge(diff_done, GROUPS + 2)
                for b in range(B):
                    nc.vector.scalar_tensor_tensor(out=core.X[:, b, :], in0=diff[:, b, :], scalar=pick[:, b:b + 1],
                                                   in1=core.X[:, b, :], op0=ALU.mult, op1=ALU.add)

            @block.scalar
            def _(act):
                norm.scalar_copy(act, 0, 0, 0)

                def group(i, s, it, nxt):
                    if nxt:
                        norm.scalar_copy(act, *nxt)
                    act.wait_ge(diff_done, it + 1)
                    act.wait_ge(scored, it + 1)
                    nc.scalar.activation(gelu[:, s].rearrange("p j d -> p (j d)"), bank[2 + s][:, :],
                                         ACT.Gelu_apprx_tanh).then_inc(gelu_done, 1)
                turns(act, group)

            @block.tensor
            def _(pe):
                pe.wait_ge(weights, 32)
                norm.tensor_turn(pe, 0, 0, 0)

                def group(i, s, it, nxt):
                    pe.wait_ge(norm.xT_ready, it + 1)
                    if nxt:
                        norm.tensor_turn(pe, *nxt)
                    pe.wait_ge(diff_done, it + 1)
                    for b in range(G):
                        xT = norm.xT[:, s, b * S:(b + 1) * S]
                        nc.tensor.matmul(bank[2 + s][:, b * S:(b + 1) * S], xT, wb[:, :], start=True, stop=True)
                        last = nc.tensor.matmul(bank[4 + s][:, b:b + 1], xT, wr[:, :], start=True, stop=True)
                    last.then_inc(scored, 1)
                turns(pe, group)
                pe.wait_ge(score_kept, GROUPS)
                nc.tensor.transpose(bank[6][0:B, 0:S], scores[:, :], core.ident[:, :]).then_inc(turned, 1)
                pe.wait_ge(selected_done, 1)
                nc.tensor.transpose(bank[7][:, 0:B], selected[:, :], core.ident[0:B, 0:B]).then_inc(selected_turned, 1)


def layer5_experts(core, gate_wT, w1T, b1, w2T, b2):
    nc, E, TOP = core.nc, 8, 2
    CAPACITY = int(1.25 * B * S / E)
    PAD = 8 - TOP
    with ExitStack() as ctx:
        sb = lambda name, shape: core.sbuf("f2_" + name, shape, ctx=ctx)
        sem = lambda name: core.sem(ctx, "f2_" + name)
        bank = [core.psum(ctx, f"f2_bank{k}", [128, 512]) for k in range(8)]
        norm = Norm(core, ctx, "f2", bank[0])
        gw, w1, b1_s, w2, b2_s = (sb("gw", [D, E]), sb("w1", [D, E, D]), sb("b1", [D, E]), sb("w2", [D, E, D]),
                                  sb("b2", [E, D]))
        xT_all = sb("xT_all", [D, B * S])
        xT_groups = xT_all[:, :].rearrange("d (i s n) -> d i s n", s=2, n=N)
        logits = sb("logits", [S, B, E])
        logits_v = logits[:, :, :].rearrange("p (i s j) e -> p i s (j e)", s=2, j=G)
        negmax, shifted, exps, sums, rsums = (sb("negmax", [S, B]), sb("shifted", [S, B, E]), sb("exps", [S, B, E]),
                                              sb("sums", [S, B]), sb("rsums", [S, B]))
        cand, top8, marked = sb("cand", [S, B, PAD + E]), sb("top8", [S, B, 8]), sb("marked", [S, B, PAD + E])
        chosen, counts, keep = sb("chosen", [S, B, E]), sb("counts", [S, E]), sb("keep", [S, E])
        w, wk, wg = sb("w", [S, B, E]), sb("w_kept", [S, B, E]), sb("w_gated", [S, B, E])
        wg_v = wg[:, :, :].rearrange("p (i s j) e -> p i s j e", s=2, j=G)
        wT = sb("wT", [E, B * S])
        h = sb("h", [D, 2, N])
        weights, scored, kept, all_turned = sem("weights"), sem("scored"), sem("logits_kept"), sem("xT_kept")
        chain, exp_done, ready, counts_in, counted, wg_done = (
            sem(n) for n in ("weighting", "exp_done", "ready_for_exp", "counts_in", "counted", "wg_done"))
        wT_turned, wT_kept, biased, bias_added = (sem(n) for n in ("wT_turned", "wT_kept", "biased", "bias_added"))
        hidden, activated, mixed, added = (sem(n) for n in ("hidden", "activated", "mixed", "added"))
        loads = [(gw[:, :], gate_wT), (w1[:, :, :], w1T), (b1_s[:, :], b1), (w2[:, :, :], w2T), (b2_s[:, :], b2)]
        LOADED = 16 * len(loads)
        with nc.Block() as block:
            @block.sync
            def _(sp):
                load(sp, weights, loads)

            @block.gpsimd
            def _(pool):
                turns(pool, lambda i, s, it, nxt: norm.gpsimd_rstd(pool, i, s, it))

            @block.scalar
            def _(act):
                norm.scalar_copy(act, 0, 0, 0)

                def group(i, s, it, nxt):
                    act.wait_ge(norm.xT_ready, it + 1)
                    nc.scalar.activation(xT_groups[:, i, s, :], norm.xT[:, s, :], ACT.Copy).then_inc(all_turned, 1)
                    if nxt:
                        norm.scalar_copy(act, *nxt)
                turns(act, group)
                act.wait_ge(ready, 1)
                nc.scalar.activation(exps[:, :, :], shifted[:, :, :], ACT.Exp).then_inc(exp_done, 1)
                for g in range(GROUPS):
                    act.wait_ge(wT_turned, g + 1)
                    nc.scalar.activation(wT[:, g * N:(g + 1) * N], bank[2 + g % 2][0:E, :], ACT.Copy).then_inc(wT_kept, 1)

            @block.vector
            def _(dve):
                norm.vector(dve, 0, 0, 0)

                def group(i, s, it, nxt):
                    if nxt:
                        norm.vector(dve, *nxt)
                    dve.wait_ge(scored, it + 1)
                    nc.vector.tensor_copy(logits_v[:, i, s, :], bank[4 + s][:, 0:G * E]).then_inc(kept, 1)
                turns(dve, group)
                wide = lambda a: a.unsqueeze(2).to_broadcast([S, B, E])
                dve.wait_ge(kept, GROUPS)
                nc.vector.tensor_reduce(negmax[:, :], logits[:, :, :], AX.X, ALU.max, negate=True).then_inc(chain, 1)
                dve.wait_ge(chain, 1)
                nc.vector.tensor_tensor(shifted[:, :, :], logits[:, :, :], wide(negmax[:, :]), ALU.add).then_inc(ready, 1)
                nc.vector.memset(cand[:, :, :], BIG).then_inc(chain, 1)
                dve.wait_ge(exp_done, 1)
                nc.vector.tensor_reduce(sums[:, :], exps[:, :, :], AX.X, ALU.add).then_inc(chain, 1)
                dve.wait_ge(chain, 3)
                nc.vector.reciprocal(rsums[:, :], sums[:, :]).then_inc(chain, 1)
                dve.wait_ge(chain, 4)
                nc.vector.tensor_tensor(cand[:, :, PAD:], exps[:, :, :], wide(rsums[:, :]), ALU.mult).then_inc(chain, 1)
                dve.wait_ge(chain, 5)
                for b in range(B):
                    nc.vector.max(top8[:, b, :], cand[:, b, :]).then_inc(chain, 1)
                dve.wait_ge(chain, 5 + B)
                for b in range(B):
                    nc.vector.match_replace(marked[:, b, :], top8[:, b, :], cand[:, b, :], -BIG).then_inc(chain, 1)
                dve.wait_ge(chain, 5 + 2 * B)
                nc.vector.tensor_scalar(chosen[:, :, :], marked[:, :, PAD:], -BIG, None, ALU.is_equal).then_inc(chain, 1)
                dve.wait_ge(chain, 6 + 2 * B)
                nc.vector.tensor_reduce(counts[:, :], chosen[:, :, :].rearrange("p b e -> p e b"), AX.X,
                                        ALU.add).then_inc(counts_in, 1)
                nc.vector.tensor_tensor(w[:, :, :], chosen[:, :, :], cand[:, :, PAD:], ALU.mult).then_inc(chain, 1)
                dve.wait_ge(counted, 1)
                nc.vector.tensor_scalar(keep[:, :], bank[6][:, 0:E], float(CAPACITY), None, ALU.is_le).then_inc(chain, 1)
                dve.wait_ge(chain, 8 + 2 * B)
                nc.vector.tensor_tensor(wk[:, :, :], w[:, :, :], keep[:, :].unsqueeze(1).to_broadcast([S, B, E]),
                                        ALU.mult).then_inc(chain, 1)
                dve.wait_ge(chain, 9 + 2 * B)
                nc.vector.tensor_scalar(wg[:, :, :], wk[:, :, :], core.gates[:, 6:7], None, ALU.mult).then_inc(wg_done, 1)
                for g in range(GROUPS):
                    x = core.X[:, g * G:(g + 1) * G, :]
                    dve.wait_ge(biased, g + 1)
                    nc.vector.tensor_tensor(x, bank[4 + g % 2][:, :].rearrange("p (j d) -> p j d", j=G), x,
                                            ALU.add).then_inc(bias_added, 1)

            @block.tensor
            def _(pe):
                pe.wait_ge(weights, LOADED)
                norm.tensor_turn(pe, 0, 0, 0)

                def group(i, s, it, nxt):
                    pe.wait_ge(norm.xT_ready, it + 1)
                    for b in range(G):
                        last = nc.tensor.matmul(bank[4 + s][:, b * E:(b + 1) * E], norm.xT[:, s, b * S:(b + 1) * S],
                                                gw[:, :], start=True, stop=True)
                    last.then_inc(scored, 1)
                    if nxt:
                        pe.wait_ge(kept, it + 1)
                        pe.wait_ge(all_turned, it + 1)
                        norm.tensor_turn(pe, *nxt)
                turns(pe, group)
                pe.wait_ge(counts_in, 1)
                nc.tensor.matmul(bank[6][:, 0:E], core.ones[:, :], counts[:, :], start=True, stop=True)\
                    .then_inc(counted, 1)
                pe.wait_ge(wg_done, 1)

                def turn(g):
                    if g >= 2:
                        pe.wait_ge(wT_kept, g - 1)
                    for j in range(G):
                        last = nc.tensor.transpose(bank[2 + g % 2][0:E, j * S:(j + 1) * S], wg[:, g * G + j, :],
                                                   core.ident[:, :])
                    last.then_inc(wT_turned, 1)

                turn(0)
                for g in range(GROUPS):
                    if g + 1 < GROUPS:
                        turn(g + 1)
                    pe.wait_ge(wT_kept, g + 1)
                    if g >= 2:
                        pe.wait_ge(bias_added, g - 1)
                    for j in range(G):
                        b = g * G + j
                        last = nc.tensor.matmul(bank[4 + g % 2][:, j * S:(j + 1) * S], wT[:, b * S:(b + 1) * S],
                                                b2_s[:, :], start=True, stop=True)
                    last.then_inc(biased, 1)

        with nc.Block() as block:
            @block.tensor
            def _(pe):
                pe.sem_inc(mixed, 2)

                def expand(i, s, it, e):
                    pe.wait_ge(activated, it * E + e + 1)
                    nc.tensor.matmul(bank[e % 2][:, :], w1[:, e, :], xT_groups[:, i, s, :], start=True,
                                     stop=True).then_inc(hidden, 1)

                expand(0, 0, 0, 0)

                def group(i, s, it, nxt):
                    for e in range(E):
                        if e + 1 < E:
                            expand(i, s, it, e + 1)
                        elif nxt:
                            expand(nxt[0], nxt[1], nxt[2], 0)
                        pe.wait_ge(activated, it * E + e + 3)
                        pe.wait_ge(added, it * E + e + 1)
                        for j in range(G):
                            last = nc.tensor.matmul(bank[2 + e % 2][:, j * S:(j + 1) * S],
                                                    h[:, e % 2, j * S:(j + 1) * S], w2[:, e, :], start=True, stop=True)
                        last.then_inc(mixed, 1)
                turns(pe, group)

            @block.scalar
            def _(act):
                act.sem_inc(activated, 2)

                def group(i, s, it, nxt):
                    for e in range(E):
                        act.wait_ge(mixed, it * E + e + 1)
                        act.wait_ge(hidden, it * E + e + 1)
                        nc.scalar.activation(h[:, e % 2, :], bank[e % 2][:, :], ACT.Silu,
                                             bias=b1_s[:, e:e + 1]).then_inc(activated, 1)
                turns(act, group)

            @block.vector
            def _(dve):
                dve.sem_inc(added, 2)

                def group(i, s, it, nxt):
                    x = core.X_groups[:, i, s]
                    for e in range(E):
                        dve.wait_ge(mixed, it * E + e + 3)
                        if e >= 1:
                            dve.wait_ge(added, it * E + e + 2)
                        for j in range(G):
                            last = nc.vector.scalar_tensor_tensor(
                                out=x[:, j, :], in0=bank[2 + e % 2][:, j * S:(j + 1) * S],
                                scalar=wg_v[:, i, s, j, e:e + 1], in1=x[:, j, :], op0=ALU.mult, op1=ALU.add)
                        last.then_inc(added, 1)
                turns(dve, group)


def layer3_experts(core, routerT, bias_rows, guT, downT):
    nc, ER, EZ, TOP, I, SCALE = core.nc, 32, 8, 6, 64, 2.5
    E, OCT, PAD = ER + EZ, 8, 8 - TOP
    PER = ER // OCT
    LAG, DOWN_LAG = 3, 4
    with ExitStack() as ctx:
        sb = lambda name, shape: core.sbuf("f1_" + name, shape, ctx=ctx)
        sem = lambda name: core.sem(ctx, "f1_" + name)
        norm_bank = core.psum(ctx, "f1_norm_bank", [128, 512])
        acc = core.psum(ctx, "f1_acc", [128, 512])
        turn_banks = [core.psum(ctx, f"f1_turn{k}", [128, 512]) for k in range(2)]
        gu_ps = [core.psum(ctx, f"f1_gu{k}", [128, 1024]) for k in range(2)]
        norm = Norm(core, ctx, "f1", norm_bank)
        rw, bias, gu_w, down_w = (sb("router", [D, E]), sb("bias", [S, E]), sb("gate_up", [D, ER, 2 * I]),
                                  sb("down", [2 * I, ER // 2, D]))
        gscale = sb("gate_scale", [128, 1])
        negmax, shifted, exps = sb("negmax", [S, G]), sb("shifted", [S, G, E]), sb("exps", [S, G, E])
        sums, rsums, probs = sb("sums", [S, G]), sb("rsums", [S, G]), sb("probs", [S, G, E])
        cand, top8, marked = sb("cand", [S, G, PAD + E]), sb("top8", [S, G, 8]), sb("marked", [S, G, PAD + E])
        chosen, w, wz = sb("chosen", [S, G, E]), sb("w", [S, 2, G, E]), sb("w_identity", [S, 2, G])
        silu, gated, h, hT = (sb("silu", [S, 2, OCT, I]), sb("gated", [S, 2, OCT, I]), sb("h", [S, 2, OCT, I]),
                              sb("hT", [2 * I, 2, OCT // 2, S]))
        weights, logits_in, shift_done, exp_done, routed, chain = (
            sem(n) for n in ("weights", "logits_in", "shift_done", "exp_done", "routed", "routing"))
        gu_done, silus, gateds, weighted, flips, copies, downs = (
            sem(n) for n in ("gate_up_done", "silus", "gateds", "weighteds", "flips", "copies", "downs"))
        identity_added, updated, passed = (sem(n) for n in ("identity_added", "updated", "passed_routing"))
        CHAIN = 15
        loads = [(rw[:, :], routerT), (bias[:, :], bias_rows), (gu_w[:, :, :], guT), (down_w[:, :, :], downT)]
        LOADED = 16 * len(loads)
        with nc.Block() as block:
            @block.sync
            def _(sp):
                load(sp, weights, loads)

            @block.gpsimd
            def _(pool):
                pool.sem_inc(weighted, 2)
                norm.gpsimd_rstd(pool, 0, 0, 0)

                def group(i, s, it, nxt):
                    for u in range(G * PER):
                        if u == 4 and nxt:
                            norm.gpsimd_rstd(pool, *nxt)
                        b, o = divmod(u, PER)
                        unit = it * G * PER + u
                        pool.wait_ge(flips, unit + 1)
                        if u == 0:
                            pool.wait_ge(routed, it + 1)
                        pool.wait_ge(gateds, unit + 3)
                        nc.gpsimd.tensor_tensor(
                            h[:, u % 2], gated[:, u % 2],
                            w[:, s, b, o * OCT:(o + 1) * OCT].unsqueeze(2).to_broadcast([S, OCT, I]),
                            ALU.mult).then_inc(weighted, 1)
                turns(pool, group)

            @block.vector
            def _(dve):
                dve.sem_inc(gateds, 2)
                dve.sem_inc(updated, 2)
                nc.vector.memset(cand[:, :, :], BIG).then_inc(chain, 1)
                nc.vector.tensor_scalar(gscale[:, :], core.gates[:, 5:6], SCALE, None, ALU.mult).then_inc(chain, 1)
                dve.wait_ge(weights, LOADED)
                wide = lambda a: a.unsqueeze(2).to_broadcast([S, G, E])

                def route(s, it):
                    step = lambda n: it * CHAIN + n + 2
                    logits = norm_bank[:, 0:G * E].rearrange("p (j e) -> p j e", j=G)
                    dve.wait_ge(logits_in, it + 1)
                    nc.vector.tensor_reduce(negmax[:, :], logits, AX.X, ALU.max, negate=True).then_inc(chain, 1)
                    dve.wait_ge(chain, step(1))
                    nc.vector.tensor_tensor(shifted[:, :, :], logits, wide(negmax[:, :]), ALU.add).then_inc(shift_done, 1)
                    dve.wait_ge(exp_done, it + 1)
                    nc.vector.tensor_reduce(sums[:, :], exps[:, :, :], AX.X, ALU.add).then_inc(chain, 1)
                    dve.wait_ge(chain, step(2))
                    nc.vector.reciprocal(rsums[:, :], sums[:, :]).then_inc(chain, 1)
                    dve.wait_ge(chain, step(3))
                    nc.vector.tensor_tensor(probs[:, :, :], exps[:, :, :], wide(rsums[:, :]), ALU.mult).then_inc(chain, 1)
                    dve.wait_ge(chain, step(4))
                    nc.vector.tensor_tensor(cand[:, :, PAD:], probs[:, :, :],
                                            bias[:, :].unsqueeze(1).to_broadcast([S, G, E]), ALU.add).then_inc(chain, 1)
                    settled(dve, chain, step(5), passed)
                    for j in range(G):
                        nc.vector.max(top8[:, j, :], cand[:, j, :]).then_inc(chain, 1)
                    settled(dve, chain, step(5 + G), passed)
                    for j in range(G):
                        nc.vector.match_replace(marked[:, j, :], top8[:, j, :], cand[:, j, :], -BIG).then_inc(chain, 1)
                    dve.wait_ge(chain, step(5 + 2 * G))
                    nc.vector.tensor_scalar(chosen[:, :, :], marked[:, :, PAD:], -BIG, gscale[:, 0:1], ALU.is_equal,
                                            ALU.mult).then_inc(chain, 1)
                    dve.wait_ge(chain, step(6 + 2 * G))
                    nc.vector.tensor_tensor(w[:, s], chosen[:, :, :], probs[:, :, :], ALU.mult).then_inc(chain, 1)
                    dve.wait_ge(chain, step(7 + 2 * G))
                    nc.vector.tensor_reduce(wz[:, s, :], w[:, s, :, ER:], AX.X, ALU.add).then_inc(routed, 1)

                norm.vector(dve, 0, 0, 0)
                route(0, 0)

                def group(i, s, it, nxt):
                    x = core.X_groups[:, i, s]
                    for u in range(G * PER):
                        unit = it * G * PER + u
                        up = gu_ps[u % 2][:, :].rearrange("p (e c) -> p e c", e=OCT)[:, :, I:]
                        dve.wait_ge(weighted, unit + 1)
                        dve.wait_ge(silus, unit + 1)
                        nc.vector.tensor_tensor(gated[:, u % 2], silu[:, u % 2], up, ALU.mult).then_inc(gateds, 1)
                        if nxt and u == 2:
                            norm.vector_stats(dve, *nxt)
                        if nxt and u == 5:
                            norm.vector_normalise(dve, *nxt)
                        if nxt and u == 12:
                            route(nxt[1], nxt[2])
                    dve.wait_ge(routed, it + 1)
                    for j in range(G):
                        last = nc.vector.scalar_tensor_tensor(out=x[:, j, :], in0=norm.xn[:, s, j, :],
                                                              scalar=wz[:, s, j:j + 1], in1=x[:, j, :],
                                                              op0=ALU.mult, op1=ALU.add)
                    last.then_inc(identity_added, 1)
                    dve.wait_ge(identity_added, it + 1)
                    dve.wait_ge(downs, (it + 1) * G * PER + 2)
                    nc.vector.tensor_tensor(x, acc[:, :].rearrange("p (j d) -> p j d", j=G), x, ALU.add)\
                        .then_inc(updated, 1)
                turns(dve, group)

            @block.scalar
            def _(act):
                act.sem_inc(copies, 2)

                def exp_of(it):
                    act.wait_ge(shift_done, it + 1)
                    nc.scalar.activation(exps[:, :, :], shifted[:, :, :], ACT.Exp).then_inc(exp_done, 1)

                norm.scalar_copy(act, 0, 0, 0)
                exp_of(0)

                def group(i, s, it, nxt):
                    for step in range(G * PER + LAG + 1):
                        if step < G * PER:
                            unit = it * G * PER + step
                            gate = gu_ps[step % 2][:, :].rearrange("p (e c) -> p e c", e=OCT)[:, :, 0:I]
                            act.wait_ge(gateds, unit + 1)
                            act.wait_ge(gu_done, unit + 1)
                            nc.scalar.activation(silu[:, step % 2], gate, ACT.Silu).then_inc(silus, 1)
                        if nxt and step == 8:
                            norm.scalar_copy(act, *nxt)
                        if nxt and step == 12:
                            exp_of(nxt[2])
                        if 0 <= step - LAG < G * PER:
                            u = step - LAG
                            unit = it * G * PER + u
                            act.wait_ge(downs, unit + 1)
                            act.wait_ge(flips, unit + 3)
                            nc.scalar.activation(hT[:, u % 2].rearrange("p e t -> p (e t)"), turn_banks[u % 2][:, :],
                                                 ACT.Copy).then_inc(copies, 1)
                turns(act, group)

            @block.tensor
            def _(pe):
                pe.sem_inc(flips, 2)
                pe.sem_inc(downs, 2)
                pe.wait_ge(weights, LOADED)

                def router(s, it):
                    pe.wait_ge(norm.xT_ready, it + 1)
                    for j in range(G):
                        last = nc.tensor.matmul(norm_bank[:, j * E:(j + 1) * E], norm.xT[:, s, j * S:(j + 1) * S],
                                                rw[:, :], start=True, stop=True)
                    last.then_inc(logits_in, 1)

                norm.tensor_turn(pe, 0, 0, 0)
                router(0, 0)

                def group(i, s, it, nxt):
                    for step in range(G * PER + DOWN_LAG):
                        if step < G * PER:
                            b, o = divmod(step, PER)
                            unit = it * G * PER + step
                            pe.wait_ge(gateds, unit + 1)
                            for k in range(2):
                                last = nc.tensor.matmul(
                                    gu_ps[step % 2][:, k * 512:(k + 1) * 512], norm.xT[:, s, b * S:(b + 1) * S],
                                    gu_w[:, o * OCT + 4 * k:o * OCT + 4 * k + 4, :], start=True, stop=True)
                            last.then_inc(gu_done, 1)
                        if nxt and step == 7:
                            pe.wait_ge(routed, it + 1)
                            norm.tensor_turn(pe, *nxt)
                        if nxt and step == 10:
                            router(nxt[1], nxt[2])
                        if 0 <= step - LAG < G * PER:
                            u = step - LAG
                            unit = it * G * PER + u
                            pe.wait_ge(copies, unit + 1)
                            pe.wait_ge(weighted, unit + 3)
                            hw = h[:, u % 2].rearrange("p e c -> p (e c)")
                            for k in range(OCT // 2):
                                last = nc.tensor.transpose(turn_banks[u % 2][:, k * S:(k + 1) * S],
                                                           hw[:, k * 2 * I:(k + 1) * 2 * I], core.ident[:, :])
                            last.then_inc(flips, 1)
                        if step >= DOWN_LAG:
                            u = step - DOWN_LAG
                            unit = it * G * PER + u
                            b, o = divmod(u, PER)
                            if u == 0:
                                pe.wait_ge(updated, it + 2)
                            pe.wait_ge(copies, unit + 3)
                            for k in range(OCT // 2):
                                p = o * OCT // 2 + k
                                last = nc.tensor.matmul(acc[:, b * S:(b + 1) * S], hT[:, u % 2, k, :], down_w[:, p, :],
                                                        start=p == 0, stop=p == ER // 2 - 1)
                            last.then_inc(downs, 1)
                turns(pe, group)


def layer4_perceiver(core, ctx_nat, mask_rows, lnx_g, lnx_b, lnl_g, lnl_b, q_gamma, k_gamma, w_ctx, w_lat, woT, bo_row):
    nc, H, DH = core.nc, 2, 64
    MASKED = 3.4e38
    QK_TINY = 1e-8 ** 2
    with ExitStack() as ctx:
        sb = lambda name, shape, dt=F32: core.sbuf("a2_" + name, shape, dt, ctx=ctx)
        sem = lambda name: core.sem(ctx, "a2_" + name)
        bank = [core.psum(ctx, f"a2_bank{k}", [128, 512]) for k in range(8)]
        c_nat = sb("ctx", [S, 2, G, C])
        n_x = Norm(core, ctx, "a2x", None)
        n_l = Norm(core, ctx, "a2l", bank[0], source=lambda i, s: n_x.xn[:, s])
        n_c = Norm(core, ctx, "a2c", bank[1], width=C, source=lambda i, s: c_nat[:, s])
        q_gain = sb("q_gain", [128, 1])
        vecs = sb("vecs", [128, 6])
        wc, wl, wo, bo = sb("w_ctx", [C, 2 * D]), sb("w_lat", [D, 3 * D]), sb("wo", [D, D]), sb("bo", [1, D])
        mask_u8, neg = sb("mask", [S, B, S], mybir.dt.uint8), sb("neg", [S, B, 2, S])
        neg_v = neg[:, :, :, :].rearrange("p (i s j) c k -> p i s j (c k)", s=2, j=G)
        lT, cT = sb("latT", [D, 2, N]), sb("ctxT", [C, 2, N])
        qk = sb("qk", [S, 2, G, 3, D])
        v = sb("v", [S, 2, G, 2, D])
        sq, ss, ms, rn, qkn = (sb("sq", [S, G * 3 * D]), sb("ss", [S, G * 6]), sb("ms", [S, G * 6]),
                               sb("rn", [S, 2, G * 6]), sb("qkn", [S, 2, G, 3, D]))
        qT, kT = sb("qT", [D, 2, G, S]), sb("kT", [D, 2, G, 2, S])
        sc, negmax = sb("scores", [S, 2, H, G, 2 * S]), sb("negmax", [S, H, G])
        probs, psum_, rsum = sb("probs", [S, 2, H, G, 2 * S]), sb("prob_sums", [S, 2, G, H]), sb("rsum", [S, G, H])
        pT = sb("probsT", [S, 2, 4, 4, S])
        o, oT = sb("o", [S, 2, G, D]), sb("oT", [D, 2, N])
        weights, ctx_landed = sem("weights"), [sem("ctx_landed0"), sem("ctx_landed1")]
        neg_done, gain_done, chain = sem("neg_done"), sem("gain_done"), sem("chain")
        lT_ready, cT_ready, lat_proj, ctx_proj, lat_kept, ctx_kept = (
            sem(n) for n in ("lT_ready", "cT_ready", "lat_projected", "ctx_projected", "lat_kept", "ctx_kept"))
        squares, ms_done, rn_done, qkn_done, qk_turned, qkT_ready = (
            sem(n) for n in ("squares", "ms_done", "rn_done", "qkn_done", "qk_turned", "qkT_ready"))
        scored, masked, shift_ready, exps, flips, pT_act, pT_dve, weighed = (
            sem(n) for n in ("scored", "masked", "shift_ready", "exps", "flips", "pT_by_scalar", "pT_by_vector",
                             "weighed"))
        normalised, o_turned, oT_ready, mixed, updated = (
            sem(n) for n in ("normalised", "o_turned", "oT_ready", "mixed", "updated"))
        CHAIN = 2
        nat_groups = ctx_nat.rearrange("(i s j) t c -> t i s j c", s=2, j=G)
        loads = [(wc[:, :], w_ctx), (wl[:, :], w_lat), (wo[:, :], woT), (bo[:, :], bo_row),
                 (mask_u8[:, :, :], mask_rows), (vecs[0:C, 0:1], lnx_g), (vecs[0:C, 1:2], lnx_b),
                 (vecs[:, 2:3], lnl_g), (vecs[:, 3:4], lnl_b), (vecs[:, 4:5], q_gamma), (vecs[:, 5:6], k_gamma)]
        LOADED = 16 * len(loads)
        with nc.Block() as block:
            @block.sync
            def _(sp):
                load(sp, weights, loads)

                def group(i, s, it, nxt):
                    sp.wait_ge(updated, it + 1)
                    sp.dma_start(c_nat[:, s], nat_groups[:, i, s]).then_inc(ctx_landed[s], 16)
                turns(sp, group)

            @block.gpsimd
            def _(pool):
                nc.gpsimd.memset(neg[:, :, 1, :], 0.0).then_inc(neg_done, 1)

                def norms(i, s, it):
                    n_x.gpsimd_rstd(pool, i, s, it)
                    n_c.gpsimd_rstd(pool, i, s, it)
                    n_l.gpsimd_rstd(pool, i, s, it)
                norms(0, 0, 0)

                def group(i, s, it, nxt):
                    pool.wait_ge(ms_done, it + 1)
                    nc.gpsimd.tensor_tensor(rn[:, s, :], ms[:, :], core.minus_half[:, 0:G * 6], ALU.pow)\
                        .then_inc(rn_done, 1)
                    if nxt:
                        norms(*nxt)
                turns(pool, group)

            @block.vector
            def _(dve):
                dve.sem_inc(updated, 2)
                dve.wait_ge(weights, LOADED)
                nc.vector.tensor_scalar(neg[:, :, 0, :], mask_u8[:, :, :], 1.0, MASKED, ALU.subtract, ALU.mult)\
                    .then_inc(neg_done, 1)
                nc.vector.tensor_scalar(q_gain[:, :], vecs[:, 4:5], DH ** -0.5, None, ALU.mult).then_inc(gain_done, 1)

                def norms(i, s, it):
                    n_x.vector_stats(dve, i, s, it)
                    dve.wait_ge(ctx_landed[s], i * 16 + 16)
                    n_c.vector_stats(dve, i, s, it)
                    n_x.vector_normalise(dve, i, s, it)
                    n_c.vector_normalise(dve, i, s, it)
                    dve.wait_ge(n_x.xn_done, it + 1)
                    n_l.vector_stats(dve, i, s, it)
                    n_l.vector_normalise(dve, i, s, it)

                norms(0, 0, 0)
                dve.wait_ge(neg_done, 2)

                def group(i, s, it, nxt):
                    for b in range(G):
                        dve.wait_ge(ctx_proj, it * G + b + 1)
                        nc.vector.tensor_copy(qk[:, s, b, 2, :], bank[4 + b % 2][:, 0:D])
                        nc.vector.tensor_copy(v[:, s, b, 0, :], bank[4 + b % 2][:, D:2 * D]).then_inc(ctx_kept, 1)
                    dve.wait_ge(squares, it + 1)
                    nc.vector.tensor_reduce(ss[:, :], sq[:, :].rearrange("p (n e) -> p n e", e=DH), AX.X, ALU.add)\
                        .then_inc(chain, 1)
                    dve.wait_ge(chain, it * CHAIN + 1)
                    nc.vector.tensor_scalar(ms[:, :], ss[:, :], 1.0 / DH, QK_TINY, ALU.mult, ALU.max).then_inc(ms_done, 1)
                    dve.wait_ge(rn_done, it + 1)
                    nc.vector.tensor_tensor(
                        qkn[:, s].rearrange("p b c (h e) -> p (b c h) e", h=H),
                        qk[:, s].rearrange("p b c (h e) -> p (b c h) e", h=H),
                        rn[:, s, :].unsqueeze(2).to_broadcast([S, G * 6, DH]), ALU.mult).then_inc(qkn_done, 1)
                    if nxt:
                        norms(*nxt)
                    for h in range(H):
                        for p in range(2):
                            dve.wait_ge(scored, it * 4 + 2 * h + p + 1)
                            last = nc.vector.tensor_tensor(
                                sc[:, s, h, 2 * p:2 * p + 2, :],
                                bank[2 + 2 * h + p][:, :].rearrange("p (b k) -> p b k", b=2),
                                neg_v[:, i, s, 2 * p:2 * p + 2, :], ALU.add)
                    last.then_inc(masked, 1)
                    dve.wait_ge(masked, it + 1)
                    nc.vector.tensor_reduce(negmax[:, :, :].rearrange("p h b -> p (h b)"), sc[:, s].rearrange("p h b k -> p (h b) k"), AX.X, ALU.max,
                                            negate=True).then_inc(shift_ready, 1)
                    for n in (1, 3):
                        dve.wait_ge(flips, it * 4 + n + 1)
                        nc.vector.tensor_copy(pT[:, s, n].rearrange("p a k -> p (a k)"), bank[6 + n % 2][:, :])\
                            .then_inc(pT_dve, 1)
                    dve.wait_ge(exps, it + 1)
                    nc.vector.reciprocal(rsum[:, :, :], psum_[:, s]).then_inc(chain, 1)
                    dve.wait_ge(weighed, it + 1)
                    dve.wait_ge(chain, it * CHAIN + 2)
                    nc.vector.tensor_tensor(o[:, s].rearrange("p b (h e) -> p (b h) e", h=H),
                                            bank[2][:, :].rearrange("p (n e) -> p n e", e=DH),
                                            rsum[:, :, :].rearrange("p b h -> p (b h)").unsqueeze(2)
                                            .to_broadcast([S, G * H, DH]), ALU.mult).then_inc(normalised, 1)
                    dve.wait_ge(mixed, it + 1)
                    x = core.X_groups[:, i, s]
                    nc.vector.scalar_tensor_tensor(
                        out=x, in0=bank[4][:, :].rearrange("p (j d) -> p j d", j=G), scalar=core.gates[:, 2:3],
                        in1=x, op0=ALU.mult, op1=ALU.add).then_inc(updated, 1)
                turns(dve, group)

            @block.scalar
            def _(act):
                act.wait_ge(weights, LOADED)
                act.wait_ge(gain_done, 1)

                def turned(i, s, it):
                    act.wait_ge(n_l.turned, it + 1)
                    nc.scalar.activation(lT[:, s, :], bank[0][:, :], ACT.Identity, bias=vecs[:, 3:4],
                                         scale=vecs[:, 2:3]).then_inc(lT_ready, 1)
                    act.wait_ge(n_c.turned, it + 1)
                    nc.scalar.activation(cT[:, s, :], bank[1][0:C, :], ACT.Identity, bias=vecs[0:C, 1:2],
                                         scale=vecs[0:C, 0:1]).then_inc(cT_ready, 1)
                turned(0, 0, 0)

                def group(i, s, it, nxt):
                    for b in range(G):
                        act.wait_ge(lat_proj, it * G + b + 1)
                        nc.scalar.activation(qk[:, s, b, 0:2, :].rearrange("p c d -> p (c d)"), bank[2 + b % 2][:, 0:2 * D],
                                             ACT.Copy)
                        nc.scalar.activation(v[:, s, b, 1, :], bank[2 + b % 2][:, 2 * D:3 * D], ACT.Copy)\
                            .then_inc(lat_kept, 1)
                    act.wait_ge(lat_kept, it * G + G)
                    act.wait_ge(ctx_kept, it * G + G)
                    nc.scalar.activation(sq[:, :], qk[:, s].rearrange("p b c d -> p (b c d)"), ACT.Square)\
                        .then_inc(squares, 1)
                    for c, (out, gain) in enumerate(((qT[:, s], q_gain[:, 0:1]), (kT[:, s, :, 1, :], vecs[:, 5:6]),
                                                      (kT[:, s, :, 0, :], vecs[:, 5:6]))):
                        act.wait_ge(qk_turned, it * 3 + c + 1)
                        nc.scalar.activation(out, bank[5 + c][:, :].rearrange("p (b k) -> p b k", b=G), ACT.Copy,
                                             scale=gain).then_inc(qkT_ready, 1)
                    if nxt:
                        turned(*nxt)
                    act.wait_ge(shift_ready, it + 1)
                    for b in range(G):
                        for h in range(H):
                            last = nc.scalar.activation(probs[:, s, h, b, :], sc[:, s, h, b, :], ACT.Exp,
                                                        bias=negmax[:, h, b:b + 1], accum_out=psum_[:, s, b, h:h + 1])
                    last.then_inc(exps, 1)
                    for n in (0, 2):
                        act.wait_ge(flips, it * 4 + n + 1)
                        nc.scalar.activation(pT[:, s, n].rearrange("p a k -> p (a k)"), bank[6 + n % 2][:, :], ACT.Copy)\
                            .then_inc(pT_act, 1)
                    act.wait_ge(o_turned, it + 1)
                    nc.scalar.activation(oT[:, s, :], bank[3][:, :], ACT.Copy).then_inc(oT_ready, 1)
                turns(act, group)

            @block.tensor
            def _(pe):
                pe.wait_ge(weights, LOADED)

                def turned(i, s, it):
                    n_c.tensor_turn(pe, i, s, it)
                    n_l.tensor_turn(pe, i, s, it)
                turned(0, 0, 0)

                def group(i, s, it, nxt):
                    pe.wait_ge(lT_ready, it + 1)
                    pe.wait_ge(cT_ready, it + 1)
                    pe.wait_ge(updated, it + 1 + 1)
                    for b in range(G):
                        bs = slice(b * S, (b + 1) * S)
                        if b >= 2:
                            pe.wait_ge(lat_kept, it * G + b - 1)
                        nc.tensor.matmul(bank[2 + b % 2][:, 0:3 * D], lT[:, s, bs], wl[:, :], start=True, stop=True)\
                            .then_inc(lat_proj, 1)
                        if b >= 2:
                            pe.wait_ge(ctx_kept, it * G + b - 1)
                        nc.tensor.matmul(bank[4 + b % 2][:, 0:2 * D], cT[:, s, bs], wc[:, :], start=True, stop=True)\
                            .then_inc(ctx_proj, 1)
                    pe.wait_ge(qkn_done, it + 1)
                    for c in range(3):
                        for b in range(G):
                            last = nc.tensor.transpose(bank[5 + c][:, b * S:(b + 1) * S], qkn[:, s, b, c, :],
                                                       core.ident[:, :])
                        last.then_inc(qk_turned, 1)
                    pe.wait_ge(qkT_ready, it * 3 + 3)
                    for h in range(H):
                        r = slice(DH * h, DH * h + DH)
                        for p in range(2):
                            for b in (2 * p, 2 * p + 1):
                                last = nc.tensor.matmul(bank[2 + 2 * h + p][:, (b % 2) * 256:(b % 2) * 256 + 256],
                                                        qT[r, s, b, :], kT[r, s, b, :, :].rearrange("p c k -> p (c k)"),
                                                        start=True, stop=True)
                            last.then_inc(scored, 1)
                    if nxt:
                        turned(*nxt)
                    pe.wait_ge(exps, it + 1)
                    for n in range(4):
                        if n >= 2:
                            pe.wait_ge((pT_act, pT_dve)[n % 2], it * 2 + 1)
                        for k in range(4):
                            last = nc.tensor.transpose(bank[6 + n % 2][:, k * S:(k + 1) * S],
                                                       probs[:, s, k // 2, n, (k % 2) * S:(k % 2) * S + S],
                                                       core.ident[:, :])
                        last.then_inc(flips, 1)
                    pe.wait_ge(pT_act, it * 2 + 2)
                    pe.wait_ge(pT_dve, it * 2 + 2)
                    for b in range(G):
                        for h in range(H):
                            for half in range(2):
                                last = nc.tensor.matmul(bank[2][:, (b * H + h) * DH:(b * H + h + 1) * DH],
                                                        pT[:, s, b, 2 * h + half, :], v[:, s, b, half, h * DH:(h + 1) * DH],
                                                        start=half == 0, stop=half == 1)
                    last.then_inc(weighed, 1)
                    pe.wait_ge(normalised, it + 1)
                    for b in range(G):
                        last = nc.tensor.transpose(bank[3][:, b * S:(b + 1) * S], o[:, s, b, :], core.ident[:, :])
                    last.then_inc(o_turned, 1)
                    pe.wait_ge(oT_ready, it + 1)
                    for b in range(G):
                        bs = slice(b * S, (b + 1) * S)
                        nc.tensor.matmul(bank[4][:, bs], core.ones[0:1, :], bo[0:1, :], start=True, stop=False)
                        last = nc.tensor.matmul(bank[4][:, bs], oT[:, s, bs], wo[:, :], start=False, stop=True)
                    last.then_inc(mixed, 1)
                turns(pe, group)


def layer1_soft_moe(core, phi, w, bias):
    nc, E, SLOTS = core.nc, 64, 32
    EC = 8
    CH = EC * SLOTS
    CHUNKS = E // EC
    KT = CH // 128
    NB = B // 2
    with ExitStack() as ctx:
        sb = lambda name, shape: core.sbuf("f0_" + name, shape, ctx=ctx)
        sem = lambda name: core.sem(ctx, "f0_" + name)
        xn, xT = sb("xn", [S, B, D]), sb("xT", [D, B, S])
        phi_s = sb("phi", [D, E * SLOTS])
        slot_max = sb("slot_max", [S, E * SLOTS])
        row_parts, neg_row = sb("row_parts", [S, 4, B]), sb("neg_row_max", [S, B])
        row_sum, acc = sb("row_sum", [S, B]), sb("acc", [S, B, D])
        with ExitStack() as c1:
            sb1 = lambda name, shape: core.sbuf("f0_" + name, shape, ctx=c1)
            bank = [core.psum(c1, f"f0_bank{k}", [128, 512]) for k in range(8)]
            stats, mv, veps, rstd = sb1("stats", [S, B, 6]), sb1("mean_var", [S, B, 2]), sb1("var_eps", [S, B]), sb1("rstd", [S, B])
            weights, stats_done, mv_done, veps_done, rstd_done = (
                sem(n) for n in ("phi_landed", "stats_done", "mv_done", "veps_done", "rstd_done"))
            xn_done, turned, xT_ready, l_done, l_used, row_done, passed = (
                sem(n) for n in ("xn_done", "turned", "xT_ready", "logits", "logits_used", "row_parts_done", "passed1"))
            slot_seen = sem("slot_seen")
            phi_q = phi_s[:, :].rearrange("d (q n) -> d q n", n=512)
            max_q = slot_max[:, :].rearrange("d (q n) -> d q n", n=512)
            with nc.Block() as block:
                @block.sync
                def _(sp):
                    sp.dma_start(phi_s[:, :], phi).then_inc(weights, 16)

                @block.gpsimd
                def _(pool):
                    nc.gpsimd.memset(slot_max[:, :], -BIG).then_inc(slot_seen, 1)
                    nc.gpsimd.memset(acc[:, :, :], 0.0)
                    nc.gpsimd.memset(row_sum[:, :], 0.0)
                    pool.wait_ge(mv_done, 1)
                    nc.gpsimd.tensor_tensor(veps[:, :], mv[:, :, 1], core.eps[:, :], ALU.add).then_inc(veps_done, 1)
                    pool.wait_ge(veps_done, 1)
                    nc.gpsimd.tensor_tensor(rstd[:, :], veps[:, :], core.minus_half[:, :], ALU.pow).then_inc(rstd_done, 1)

                @block.vector
                def _(dve):
                    for b in range(B):
                        last = nc.vector.bn_stats(stats[:, b, :], core.X[:, b, :])
                    last.then_inc(stats_done, 1)
                    dve.wait_ge(stats_done, 1)
                    for b in range(B):
                        last = nc.vector.bn_aggr(mv[:, b, :], stats[:, b, :])
                    last.then_inc(mv_done, 1)
                    dve.wait_ge(rstd_done, 1)
                    for b in range(B):
                        nc.vector.tensor_scalar(xn[:, b, :], core.X[:, b, :], mv[:, b, 0:1], rstd[:, b:b + 1],
                                                ALU.subtract, ALU.mult).then_inc(xn_done, 1)
                    with dve.Fori(0, 4) as q:
                        for b in range(B):
                            ps = bank[2 + b % 6][:, :]
                            dve.wait_ge(l_done, q * B + b + 1)
                            dve.wait_ge(slot_seen, q * B + b + 1)
                            nc.vector.tensor_tensor(max_q[:, q, :], ps, max_q[:, q, :], ALU.max)
                            nc.vector.tensor_reduce(row_parts[:, q, b:b + 1], ps, AX.X, ALU.max).then_inc(slot_seen, 1)
                    dve.wait_ge(slot_seen, 4 * B + 1)
                    nc.vector.tensor_reduce(neg_row[:, :], row_parts[:, :, :].rearrange("p q b -> p b q"), AX.X, ALU.max,
                                            negate=True)

                @block.scalar
                def _(act):
                    for g in range(GROUPS):
                        act.wait_ge(turned, g + 1)
                        nc.scalar.activation(xT[:, g * G:(g + 1) * G, :].rearrange("d b t -> d (b t)"), bank[g % 2][:, :],
                                             ACT.Copy).then_inc(xT_ready, 1)

                @block.tensor
                def _(pe):
                    for g in range(GROUPS):
                        pe.wait_ge(xn_done, g * G + G)
                        if g >= 2:
                            pe.wait_ge(xT_ready, g - 1)
                        for j in range(G):
                            last = nc.tensor.transpose(bank[g % 2][:, j * S:(j + 1) * S], xn[:, g * G + j, :],
                                                       core.ident[:, :])
                        last.then_inc(turned, 1)
                    pe.wait_ge(xT_ready, GROUPS)
                    pe.wait_ge(weights, 16)
                    with pe.Fori(0, 4) as q:
                        for b in range(B):
                            if b < 6:
                                pe.wait_ge(slot_seen, q * B + 1)
                            else:
                                pe.wait_ge(slot_seen, q * B + b - 4)
                            nc.tensor.matmul(bank[2 + b % 6][:, :], xT[:, b, :], phi_q[:, q, :], start=True,
                                             stop=True).then_inc(l_done, 1)

        with ExitStack() as c2:
            sb2 = lambda name, shape: core.sbuf("f0_" + name, shape, ctx=c2)
            bank = [core.psum(c2, f"f0_chunk_bank{k}", [128, 512]) for k in range(8)]
            w_s, bias_s = sb2("w", [D, EC, D]), sb2("bias", [D, EC])
            disp = sb2("dispatch", [S, B, CH])
            y = disp[:, :, :].rearrange("p b n -> p (b n)").rearrange("p (k b d) -> p k b d", k=KT, b=B)
            back = sb2("combine", [S, 4, CH])
            backT = sb2("combineT", [128, KT, B, S])
            part, sums, rsums = sb2("part_sums", [S, 2, CH]), sb2("slot_sums", [S, CH]), sb2("slot_rsums", [S, CH])
            row_part, row_r, row_g = sb2("row_part", [S, B]), sb2("row_r", [S, B]), sb2("row_gate", [S, B])
            slots = sb2("slots", [D, KT, B, 4, SLOTS])
            w_landed, logits, shifts, backs, disps, flips, backTs, pair_sums = (
                sem(n) for n in ("w_landed", "chunk_logits", "shifts", "backs", "disps", "flips", "backTs", "pair_sums"))
            rows_added, sums_done, rsums_done, scaled_dve, scaled_pool = (
                sem(n) for n in ("rows_added", "sums_done", "rsums_done", "scaled_by_vector", "scaled_by_gpsimd"))
            dispatched, slots_act, slots_dve, expanded, biased = (
                sem(n) for n in ("dispatched", "slots_by_scalar", "slots_by_vector", "expanded", "biased"))
            y_flips, y_act, y_dve, returned, added, row_r_done, row_g_done = (
                sem(n) for n in ("y_flips", "y_by_scalar", "y_by_vector", "returned", "added", "row_r_done", "row_g_done"))
            phi_c = phi_s[:, :].rearrange("d (c n) -> d c n", n=CH)
            max_c = slot_max[:, :].rearrange("d (c n) -> d c n", n=CH)
            BY_POOL = (2, 5, 7)
            BY_VECTOR = tuple(g for g in range(GROUPS) if g not in BY_POOL)
            logit_bank = lambda p: bank[(0, 1, 6, 7)[p % 4]]
            pair = lambda p: slice(2 * p, 2 * p + 2)
            half_of_expert = lambda u: slots[:, u // 8, 16 * (u % 2):16 * (u % 2) + 16, u // 2 % 4, :]
            scale_group = lambda g: (disp[:, g * G:(g + 1) * G, :], rsums[:, :].unsqueeze(1).to_broadcast([S, G, CH]))
            with nc.Block() as block:
                @block.sync
                def _(sp):
                    def fetch(c):
                        sp.dma_start(w_s[:, :, :], w[:, c, :, :]).then_inc(w_landed, 16)
                        sp.dma_start(bias_s[:, :], bias[:, c, :]).then_inc(w_landed, 16)
                    fetch(0)
                    with sp.Fori(0, CHUNKS - 1) as c:
                        sp.wait_ge(biased, c * 16 + 16)
                        fetch(c + 1)

                @block.tensor
                def _(pe):
                    with pe.Fori(0, CHUNKS) as c:
                        for step in range(NB + 1):
                            if step < NB:
                                p = step
                                if p >= 4:
                                    pe.wait_ge(shifts, c * NB + p - 3)
                                for k in range(2):
                                    last = nc.tensor.matmul(logit_bank(p)[:, k * CH:(k + 1) * CH], xT[:, 2 * p + k, :],
                                                            phi_c[:, c, :], start=True, stop=True)
                                last.then_inc(logits, 1)
                            if step >= 1:
                                p = step - 1
                                if p >= 2:
                                    pe.wait_ge(backTs, c * NB + p - 1)
                                pe.wait_ge(backs, c * NB + p + 1)
                                for kt in range(KT):
                                    for k in range(2):
                                        at = (kt * 2 + k) * S
                                        last = nc.tensor.transpose(bank[2 + p % 2][:, at:at + S],
                                                                   back[:, 2 * (p % 2) + k, kt * 128:(kt + 1) * 128],
                                                                   core.ident[:, :])
                                last.then_inc(flips, 1)
                        pe.wait_ge(added, c * GROUPS + GROUPS)
                        for p in range(NB):
                            g = p // 2
                            if p % 2 == 0:
                                if g in BY_POOL:
                                    pe.wait_ge(scaled_pool, c * len(BY_POOL) + BY_POOL.index(g) + 1)
                                else:
                                    pe.wait_ge(scaled_dve, c * len(BY_VECTOR) + BY_VECTOR.index(g) + 1)
                            if p >= 2:
                                pe.wait_ge((slots_act, slots_dve)[p % 2], c * (NB // 2) + (p - 2) // 2 + 1)
                            for k in range(2):
                                last = nc.tensor.matmul(bank[4 + p % 2][:, k * CH:(k + 1) * CH], xn[:, 2 * p + k, :],
                                                        disp[:, 2 * p + k, :], start=True, stop=True)
                            last.then_inc(dispatched, 1)
                        pe.wait_ge(slots_act, c * (NB // 2) + NB // 2)
                        pe.wait_ge(slots_dve, c * (NB // 2) + NB // 2)
                        pe.wait_ge(w_landed, c * 32 + 32)

                        def turn_outputs(n):
                            kt, g = divmod(n, GROUPS)
                            if g == 0:
                                pe.wait_ge(biased, c * 16 + 8 * kt + 8)
                            if n == 0:
                                pe.wait_ge(backTs, c * NB + NB)
                            if n >= 2:
                                pe.wait_ge((y_act, y_dve)[n % 2], c * GROUPS + (n - 2) // 2 + 1)
                            for j in range(G):
                                last = nc.tensor.transpose(bank[2 + n % 2][:, j * D:(j + 1) * D],
                                                           slots[:, kt, g * G + j].rearrange("d e s -> d (e s)"), core.ident[:, :])
                            last.then_inc(y_flips, 1)

                        for u in range(16):
                            if u >= 2:
                                pe.wait_ge(biased, c * 16 + u - 1)
                            nc.tensor.matmul(bank[6 + u % 2][:, :], w_s[:, u // 2, :],
                                             half_of_expert(u), start=True,
                                             stop=True).then_inc(expanded, 1)
                            if u >= 9:
                                turn_outputs(u - 9)
                        for n in range(7, 16):
                            turn_outputs(n)
                        pe.wait_ge(y_act, c * GROUPS + GROUPS)
                        pe.wait_ge(y_dve, c * GROUPS + GROUPS)
                        for g in range(GROUPS):
                            if g >= 2:
                                pe.wait_ge(added, c * GROUPS + g - 1 + GROUPS)
                            for j in range(G):
                                for kt in range(KT):
                                    last = nc.tensor.matmul(bank[4 + g % 2][:, j * D:(j + 1) * D],
                                                            backT[:, kt, g * G + j, :], y[:, kt, g * G + j, :],
                                                            start=kt == 0, stop=kt == KT - 1)
                            last.then_inc(returned, 1)

                @block.scalar
                def _(act):
                    with act.Fori(0, CHUNKS) as c:
                        for p in range(NB):
                            if p >= 2:
                                act.wait_ge(flips, c * NB + p - 1)
                            act.wait_ge(logits, c * NB + p + 1)
                            for k in range(2):
                                b = 2 * p + k
                                last = nc.scalar.activation(back[:, b % 4, :], logit_bank(p)[:, k * CH:(k + 1) * CH],
                                                            ACT.Exp, bias=neg_row[:, b:b + 1],
                                                            accum_out=row_part[:, b:b + 1])
                            last.then_inc(backs, 1)
                            act.wait_ge(shifts, c * NB + p + 1)
                            nc.scalar.activation(disp[:, pair(p), :], disp[:, pair(p), :], ACT.Exp).then_inc(disps, 1)
                        for p in range(0, NB, 2):
                            act.wait_ge(dispatched, c * NB + p + 1)
                            nc.scalar.activation(slots[:, :, pair(p)].rearrange("d k b e s -> d b k (e s)"),
                                                 bank[4][:, :].rearrange("d (b k n) -> d b k n", b=2, k=KT),
                                                 ACT.Copy).then_inc(slots_act, 1)
                        act.wait_ge(w_landed, c * 32 + 32)
                        done = 0
                        for u in range(16):
                            act.wait_ge(expanded, c * 16 + u + 1)
                            nc.scalar.activation(half_of_expert(u),
                                                 bank[6 + u % 2][:, :].rearrange("d (b s) -> d b s", b=16), ACT.Identity,
                                                 bias=bias_s[:, u // 2:u // 2 + 1]).then_inc(biased, 1)
                            if u >= 10 and u % 2 == 0:
                                n = u - 10
                                act.wait_ge(y_flips, c * 16 + n + 1)
                                nc.scalar.activation(y[:, 0, n * G:n * G + G, :], bank[2][:, :].rearrange(
                                    "p (j d) -> p j d", j=G), ACT.Copy).then_inc(y_act, 1)
                                done = n + 2
                        for n in range(done, 16, 2):
                            kt, g = divmod(n, GROUPS)
                            act.wait_ge(y_flips, c * 16 + n + 1)
                            nc.scalar.activation(y[:, kt, g * G:g * G + G, :], bank[2][:, :].rearrange(
                                "p (j d) -> p j d", j=G), ACT.Copy).then_inc(y_act, 1)

                @block.gpsimd
                def _(pool):
                    with pool.Fori(0, CHUNKS) as c:
                        for p in range(1, NB):
                            if p >= 2:
                                pool.wait_ge(pair_sums, c * (NB - 1) + p - 1)
                            pool.wait_ge(disps, c * NB + p + 1)
                            nc.gpsimd.tensor_tensor(part[:, :, :], part[:, :, :] if p > 1 else disp[:, pair(0), :],
                                                    disp[:, pair(p), :], ALU.add).then_inc(pair_sums, 1)
                        for g in BY_POOL:
                            pool.wait_ge(rsums_done, c + 1)
                            e, r = scale_group(g)
                            nc.gpsimd.tensor_tensor(e, e, r, ALU.mult).then_inc(scaled_pool, 1)

                @block.vector
                def _(dve):
                    dve.sem_inc(added, GROUPS)
                    dve.sem_inc(rows_added, 1)
                    with dve.Fori(0, CHUNKS) as c:
                        for step in range(NB + 2):
                            if step < NB:
                                p = step
                                dve.wait_ge(backs, c * NB + p + 1)
                                nc.vector.tensor_tensor(disp[:, pair(p), :],
                                                        logit_bank(p)[:, :].rearrange("p (b n) -> p b n", b=2),
                                                        max_c[:, c, :].unsqueeze(1).to_broadcast([S, 2, CH]),
                                                        ALU.subtract).then_inc(shifts, 1)
                            if step >= 2:
                                p = step - 2
                                dve.wait_ge(flips, c * NB + p + 1)
                                nc.vector.tensor_copy(backT[:, :, pair(p), :],
                                                      bank[2 + p % 2][:, :].rearrange("p (k b t) -> p k b t", k=KT, b=2))\
                                    .then_inc(backTs, 1)
                        dve.wait_ge(backs, c * NB + NB)
                        dve.wait_ge(rows_added, c + 1)
                        nc.vector.tensor_tensor(row_sum[:, :], row_sum[:, :], row_part[:, :], ALU.add)\
                            .then_inc(rows_added, 1)
                        dve.wait_ge(pair_sums, (c + 1) * (NB - 1))
                        nc.vector.tensor_tensor(sums[:, :], part[:, 0, :], part[:, 1, :], ALU.add).then_inc(sums_done, 1)
                        dve.wait_ge(sums_done, c + 1)
                        nc.vector.reciprocal(rsums[:, :], sums[:, :]).then_inc(rsums_done, 1)
                        dve.wait_ge(rsums_done, c + 1)
                        for g in BY_VECTOR:
                            e, r = scale_group(g)
                            nc.vector.tensor_tensor(e, e, r, ALU.mult).then_inc(scaled_dve, 1)
                        for p in range(1, NB, 2):
                            dve.wait_ge(dispatched, c * NB + p + 1)
                            nc.vector.tensor_copy(slots[:, :, pair(p)].rearrange("d k b e s -> d b k (e s)"),
                                                  bank[5][:, :].rearrange("d (b k n) -> d b k n", b=2, k=KT))\
                                .then_inc(slots_dve, 1)
                        for n in range(1, 16, 2):
                            kt, g = divmod(n, GROUPS)
                            dve.wait_ge(y_flips, c * 16 + n + 1)
                            nc.vector.tensor_copy(y[:, kt, g * G:g * G + G, :],
                                                  bank[3][:, :].rearrange("p (j d) -> p j d", j=G)).then_inc(y_dve, 1)
                        for g in range(GROUPS):
                            dve.wait_ge(added, c * GROUPS + g + 1)
                            dve.wait_ge(returned, c * GROUPS + g + 1)
                            a = acc[:, g * G:g * G + G, :]
                            nc.vector.tensor_tensor(a, bank[4 + g % 2][:, :].rearrange("p (j d) -> p j d", j=G), a,
                                                    ALU.add).then_inc(added, 1)
                    dve.wait_ge(rows_added, CHUNKS + 1)
                    nc.vector.reciprocal(row_r[:, :], row_sum[:, :]).then_inc(row_r_done, 1)
                    dve.wait_ge(row_r_done, 1)
                    nc.vector.tensor_scalar(row_g[:, :], row_r[:, :], core.gates[:, 4:5], None, ALU.mult)\
                        .then_inc(row_g_done, 1)
                    dve.wait_ge(row_g_done, 1)
                    dve.wait_ge(added, (CHUNKS + 1) * GROUPS)
                    for b in range(B):
                        nc.vector.scalar_tensor_tensor(out=core.X[:, b, :], in0=acc[:, b, :], scalar=row_g[:, b:b + 1],
                                                       in1=core.X[:, b, :], op0=ALU.mult, op1=ALU.add)


def store(core, out):
    nc = core.nc
    with ExitStack() as ctx:
        stored = core.sem(ctx, "stored")
        with nc.Block() as block:
            @block.sync
            def _(sp):
                sp.dma_start(out.rearrange("b s d -> s b d"), core.X[:, :, :]).then_inc(stored, 16)
                sp.wait_ge(stored, 16)


def arrays(inputs):
    a = {k: np.asarray(v) for k, v in inputs.items()}
    col = lambda v: v.reshape(-1, 1)
    rows = lambda v, n=128: np.tile(v.reshape(1, -1), (n, 1))
    in_halves = lambda w: w.reshape(-1, 2, 2, 4, 64).transpose(0, 1, 3, 2, 4).reshape(-1, 1024)
    laid = {
        "x": a["x"],
        "ctxT": a["ctx_768"].transpose(2, 0, 1).reshape(C, B * S),
        "gates": rows(np.concatenate([a["g_xattn"], a["g_ffn"]])),
        "c0_wvT": a["L0_xattn_Wv"].T, "c0_bv": col(a["L0_xattn_bv"]),
        "c0_wtT": a["L0_xattn_Wt"].T, "c0_bt": col(a["L0_xattn_bt"]),
        "a1_wq": a["L1_xattn_Wq"], "a1_bq": col(a["L1_xattn_bq"]),
        "a1_wk": a["L1_xattn_Wk"], "a1_bk": col(a["L1_xattn_bk"]),
        "a1_wv": a["L1_xattn_Wv"], "a1_bv": rows(a["L1_xattn_bv"]),
        "a1_w1": a["L1_xattn_W1"], "a1_b1": a["L1_xattn_b1"].reshape(2, 128).T,
        "a1_w2": a["L1_xattn_W2"].reshape(2, 128, D).transpose(1, 0, 2),
        "a1_b2": a["L1_xattn_b2"].reshape(1, D),
        "a1_mask": np.repeat(np.eye(16, dtype=np.float32), 8, axis=0),
        "f0_phi": a["L0_ffn_phi"].reshape(D, 64 * 32),
        "f0_w": a["L0_ffn_W"].reshape(8, 8, D, D).transpose(2, 0, 1, 3), "f0_bias": a["L0_ffn_b"].reshape(8, 8, D).transpose(2, 0, 1),
        "f1_routerT": a["L1_ffn_classifier_weight"].T, "f1_bias": rows(a["L1_ffn_e_score_correction_bias"]),
        "f1_guT": a["L1_ffn_gate_up_proj"][:32].transpose(2, 0, 1),
        "f1_downT": a["L1_ffn_down_proj"].transpose(0, 2, 1).reshape(16, 128, D).transpose(1, 0, 2),
        "ctx": a["ctx_768"], "a2_mask": np.tile(np.asarray(a["mask_BxS2_bk0"]).reshape(1, B, S), (S, 1, 1)),
        "a2_lnx_g": col(a["L2_xattn_ln_x_g"]), "a2_lnx_b": col(a["L2_xattn_ln_x_b"]),
        "a2_lnl_g": col(a["L2_xattn_ln_l_g"]), "a2_lnl_b": col(a["L2_xattn_ln_l_b"]),
        "a2_qn": col(np.tile(a["L2_xattn_qn_g"], 2)), "a2_kn": col(np.tile(a["L2_xattn_kn_g"], 2)),
        "a2_wc": a["L2_xattn_Wkv"].T, "a2_wl": np.concatenate([a["L2_xattn_Wq"], a["L2_xattn_Wlkv"]]).T,
        "a2_wo": a["L2_xattn_Wo"].T, "a2_bo": a["L2_xattn_bo"].reshape(1, D),
        "f2_gateT": a["L2_ffn_gate_w"].T,
        "f2_w1T": a["L2_ffn_w1"].transpose(2, 0, 1), "f2_b1": a["L2_ffn_b1"].T,
        "f2_w2T": a["L2_ffn_w2"].transpose(2, 0, 1), "f2_b2": a["L2_ffn_b2"],
        "a3_wq": in_halves(a["L3_xattn_w_q"]), "a3_wk": in_halves(a["L3_xattn_w_kv"][:, :1024]),
        "a3_wv": a["L3_xattn_w_kv"][:, 1024:],
        "a3_wo": a["L3_xattn_w_out"].reshape(8, 128, D).transpose(1, 0, 2), "a3_bo": a["L3_xattn_b_out"].reshape(1, D),
        "f3_wr": col(a["L3_ffn_w_router"]), "f3_wb": a["L3_ffn_w_block"],
    }
    return {k: np.ascontiguousarray(v) for k, v in laid.items()}


def build(nc, t, out):
    with ExitStack() as ctx:
        core = Core(nc, ctx)
        setup(core, t["x"], t["gates"])
        core.end_layer()
        layer0_cosine(core, t["ctxT"], t["c0_wvT"], t["c0_bv"], t["c0_wtT"], t["c0_bt"])
        core.end_layer()
        layer1_soft_moe(core, t["f0_phi"], t["f0_w"], t["f0_bias"])
        core.end_layer()
        layer2_attention(core, t["ctxT"], t["a1_wq"], t["a1_bq"], t["a1_wk"], t["a1_bk"], t["a1_wv"], t["a1_bv"],
                         t["a1_w1"], t["a1_b1"], t["a1_w2"], t["a1_b2"], t["a1_mask"])
        core.end_layer()
        layer3_experts(core, t["f1_routerT"], t["f1_bias"], t["f1_guT"], t["f1_downT"])
        core.end_layer()
        layer4_perceiver(core, t["ctx"], t["a2_mask"], t["a2_lnx_g"], t["a2_lnx_b"], t["a2_lnl_g"], t["a2_lnl_b"],
                         t["a2_qn"], t["a2_kn"], t["a2_wc"], t["a2_wl"], t["a2_wo"], t["a2_bo"])
        core.end_layer()
        layer5_experts(core, t["f2_gateT"], t["f2_w1T"], t["f2_b1"], t["f2_w2T"], t["f2_b2"])
        core.end_layer()
        layer6_attention(core, t["ctxT"], t["a3_wq"], t["a3_wk"], t["a3_wv"], t["a3_wo"], t["a3_bo"])
        core.end_layer()
        layer7_selected_gelu(core, t["f3_wr"], t["f3_wb"])
        core.end_layer()
        store(core, out)


def kernel(**inputs):
    import concourse.bacc as bacc
    from concourse.bass_utils import run_bass_kernel_spmd

    nc = bacc.Bacc("TRN2", target_bir_lowering=False, num_devices=1)
    laid = arrays(inputs)
    t = {k: nc.dram_tensor("in_" + k, v.shape, mybir.dt.from_np(v.dtype), kind="ExternalInput").ap() for k, v in laid.items()}
    out = nc.dram_tensor("out", (B, S, D), F32, kind="ExternalOutput").ap()
    build(nc, t, out)
    return run_bass_kernel_spmd(nc, [{"in_" + k: v for k, v in laid.items()}], core_ids=[0]).results[0]["out"]
```

```python
from contextlib import ExitStack

import numpy as np

import concourse.bass as bass
from concourse import mybir

F32 = mybir.dt.float32
ALU = mybir.AluOpType
ACT = mybir.ActivationFunctionType
AX = mybir.AxisListType

B, S, D, C = 32, 128, 128, 96
G = 4
GROUPS = B // G
PAIRS = GROUPS // 2
N = G * S
LN_EPS = 1e-5
BIG = 3.0e38


class Held:
    pass


class Core:

    def __init__(self, nc, ctx):
        self.nc, self.ctx, self.layer_semaphores = nc, ctx, []
        self.X = self.sbuf("x_resident", [S, B, D])
        self.ident = self.sbuf("ident", [128, 128])
        self.ones = self.sbuf("ones", [128, 128])
        self.gates = self.sbuf("gates", [128, 8])
        self.eps = self.sbuf("eps", [128, B])
        self.minus_half = self.sbuf("minus_half", [128, B])
        self.x_landed = [nc.alloc_semaphore("x_first_landed"), nc.alloc_semaphore("x_rest_landed")]
        self.X_groups = self.X[:, :, :].rearrange("p (i s j) d -> p i s j d", s=2, j=G)

    def hold(self, ctx, layer, places):
        held = Held()
        held.tiles = [self.sbuf(f"{layer}_{name}", shape, dt, ctx=ctx) for name, shape, dt, _ in places]
        held.pairs = [(tile[tuple(slice(None) for _ in shape)], source)
                      for tile, (_, shape, _, source) in zip(held.tiles, places)]
        held.landed = self.nc.alloc_semaphore(f"{layer}_held_landed")
        held.all = 16 * len(places)
        return held

    def sbuf(self, name, shape, dt=F32, ctx=None):
        return (ctx or self.ctx).enter_context(self.nc.sbuf_tensor(name, shape, dt))

    def psum(self, ctx, name, shape):
        return ctx.enter_context(self.nc.psum_tensor(name, shape, F32))

    def sem(self, ctx, name):
        handle = self.nc.alloc_semaphore(name)
        self.layer_semaphores.append(handle)
        return handle

    def end_layer(self):
        self.nc.clear_and_free_semaphores(self.layer_semaphores)
        self.layer_semaphores = []
        self.nc.all_engine_barrier()


def turns(eng, body):
    with eng.Fori(0, PAIRS - 1) as i:
        body(i, 0, i * 2, (i, 1, i * 2 + 1))
        body(i, 1, i * 2 + 1, (i + 1, 0, i * 2 + 2))
    i = PAIRS - 1
    body(i, 0, i * 2, (i, 1, i * 2 + 1))
    body(i, 1, i * 2 + 1, None)


def stream(eng, body):
    place = lambda i, s: (i, s, i * 2 + s)

    def turn(i, first=False, last=False):
        body(place(i, 0), None if first else place(i - 1, 1), place(i, 1), None if last else place(i + 1, 0))
        body(place(i, 1), place(i, 0), None if last else place(i + 1, 0), None if last else place(i + 1, 1))
    turn(0, first=True)
    with eng.Fori(1, PAIRS - 1) as i:
        turn(i)
    turn(PAIRS - 1, last=True)


def settled(eng, sem, value, passed):
    eng.wait_ge(sem, value)
    eng.sem_inc(passed, 1)


class Norm:

    def __init__(self, core, ctx, layer, bank, width=D, slots=2, source=None):
        self.core, self.nc, self.bank, self.width = core, core.nc, bank, width
        self.source = source or (lambda i, s: core.X_groups[:, i, s])
        sb = lambda name, shape: core.sbuf(f"{layer}_{name}", shape, ctx=ctx)
        self.stats = sb("stats", [S, slots, G, 6])
        self.mv = sb("mean_var", [S, slots, G, 2])
        self.veps = sb("var_eps", [S, slots, G])
        self.rstd = sb("rstd", [S, slots, G])
        self.xn = sb("xn", [S, slots, G, width])
        self.xT = sb("xT", [width, slots, N])
        sem = lambda name: core.sem(ctx, f"{layer}_{name}")
        self.stats_done, self.mv_done, self.veps_done = sem("stats_done"), sem("mv_done"), sem("veps_done")
        self.rstd_done, self.xn_done = sem("rstd_done"), sem("xn_done")
        self.turned, self.xT_ready = sem("turned"), sem("xT_ready")
        self.passed = sem("passed")

    def vector_stats(self, dve, i, s, it):
        x = self.source(i, s)
        for j in range(G):
            last = self.nc.vector.bn_stats(self.stats[:, s, j, :], x[:, j, :])
        last.then_inc(self.stats_done, 1)
        settled(dve, self.stats_done, it + 1, self.passed)
        for j in range(G):
            last = self.nc.vector.bn_aggr(self.mv[:, s, j, :], self.stats[:, s, j, :])
        last.then_inc(self.mv_done, 1)

    def gpsimd_rstd(self, pool, i, s, it):
        core = self.core
        pool.wait_ge(self.mv_done, it + 1)
        self.nc.gpsimd.tensor_tensor(self.veps[:, s, :], self.mv[:, s, :, 1], core.eps[:, 0:G],
                                     ALU.add).then_inc(self.veps_done, 1)
        pool.wait_ge(self.veps_done, it + 1)
        self.nc.gpsimd.tensor_tensor(self.rstd[:, s, :], self.veps[:, s, :], core.minus_half[:, 0:G],
                                     ALU.pow).then_inc(self.rstd_done, 1)

    def vector_normalise(self, dve, i, s, it):
        x = self.source(i, s)
        dve.wait_ge(self.rstd_done, it + 1)
        for j in range(G):
            last = self.nc.vector.tensor_scalar(self.xn[:, s, j, :], x[:, j, :], self.mv[:, s, j, 0:1],
                                                self.rstd[:, s, j:j + 1], ALU.subtract, ALU.mult)
        last.then_inc(self.xn_done, 1)

    def vector(self, dve, i, s, it):
        self.vector_stats(dve, i, s, it)
        self.vector_normalise(dve, i, s, it)

    def tensor_turn(self, pe, i, s, it):
        pe.wait_ge(self.xn_done, it + 1)
        for j in range(G):
            last = self.nc.tensor.transpose(self.bank[0:self.width, j * S:(j + 1) * S],
                                            self.xn[:, s, j, :], self.core.ident[:, :])
        last.then_inc(self.turned, 1)

    def scalar_copy(self, act, i, s, it):
        act.wait_ge(self.turned, it + 1)
        self.nc.scalar.activation(self.xT[:, s, :], self.bank[0:self.width, :],
                                  ACT.Copy).then_inc(self.xT_ready, 1)


class Bias:

    def __init__(self, core, ctx, layer, row, gate):
        self.core, self.nc, self.row, self.gate = core, core.nc, row, gate
        self.gated = core.sbuf(f"{layer}_gated_bias", [S, D], ctx=ctx)
        self.made, self.added = core.sem(ctx, f"{layer}_bias_gated"), core.sem(ctx, f"{layer}_bias_added")

    def vector_start(self):
        self.nc.vector.tensor_scalar(self.gated[:, :], self.row[:, :], self.core.gates[:, self.gate:self.gate + 1],
                                     None, ALU.mult).then_inc(self.made, 1)

    def gpsimd_start(self, pool):
        pool.wait_ge(self.made, 1)

    def gpsimd_add(self, pool, at, normalised):
        i, s, it = at
        x = self.core.X_groups[:, i, s]
        pool.wait_ge(normalised, it + 1)
        self.nc.gpsimd.tensor_tensor(x, x, self.gated[:, :].unsqueeze(1).to_broadcast([S, G, D]),
                                     ALU.add).then_inc(self.added, 1)

    def vector_wait(self, dve, at):
        dve.wait_ge(self.added, at[2] + 1)


def load_ahead(eng, held):
    for to, source in held.pairs:
        eng.dma_start(to, source).then_inc(held.landed, 16)


def load(eng, sem, pairs):
    for to, source in pairs:
        eng.dma_start(to, source).then_inc(sem, 16)
    return 16 * len(pairs)


def setup(core, x, gates):
    nc, X = core.nc, core.X
    with ExitStack() as ctx:
        raw = core.sbuf("raw_gates", [128, 8], ctx=ctx)
        landed, made = core.sem(ctx, "inputs_landed"), core.sem(ctx, "constants_made")
        with nc.Block() as block:
            @block.sync
            def _(sp):
                sp.dma_start(raw[:, :], gates).then_inc(landed, 16)
                x_rows, first = x.rearrange("b s d -> s b d"), 2 * G
                sp.dma_start(X[:, 0:first, :], x_rows[:, 0:first, :]).then_inc(core.x_landed[0], 16)
                sp.dma_start(X[:, first:, :], x_rows[:, first:, :]).then_inc(core.x_landed[1], 16)

            @block.gpsimd
            def _(pool):
                nc.gpsimd.memset(core.ones[:, :], 1.0)
                nc.gpsimd.memset(core.eps[:, :], LN_EPS)
                nc.gpsimd.memset(core.minus_half[:, :], -0.5)
                nc.gpsimd.memset(core.ident[:, :], 0.0).then_inc(made, 1)
                pool.wait_ge(made, 1)
                nc.gpsimd.affine_select(out=core.ident[:, :], in_=core.ident[:, :], compare_op=ALU.not_equal,
                                        fill=1.0, base=0, pattern=[[-1, 128]], channel_multiplier=1)

            @block.scalar
            def _(act):
                act.wait_ge(landed, 16)
                nc.scalar.activation(core.gates[:, :], raw[:, :], ACT.Tanh)


def layer0_cosine(core, ctxT, wvT, bv, wtT, bt, ahead):
    nc, H, EPS = core.nc, 64, 1e-8
    with ExitStack() as ctx:
        sb = lambda name, shape: core.sbuf("c0_" + name, shape, ctx=ctx)
        sem = lambda name: core.sem(ctx, "c0_" + name)
        bank = [core.psum(ctx, f"c0_bank{k}", [128, 512]) for k in range(8)]
        norm = Norm(core, ctx, "c0", bank[0])
        wv, wt, bvc, btc = sb("wv", [D, H]), sb("wt", [C, H]), sb("bv", [H, 1]), sb("bt", [H, 1])
        cT = sb("cT", [C, 2, N])
        vT, tT, v2, t2 = (sb(n, [H, 2, N]) for n in ("vT", "tT", "v2", "t2"))
        tn, vn = sb("tn", [S, 2, N]), sb("vn", [S, 2, G])
        den, rden, cosine = sb("den", [S, 2, N]), sb("rden", [S, 2, N]), sb("cosine", [S, 2, N])
        vps, tps = bank[1], bank[2]
        dots, tn2 = bank[3:5], bank[5:7]
        vn2 = bank[7]
        weights, ctx_landed = sem("weights"), [sem("ctx_landed0"), sem("ctx_landed1")]
        projected, squared, summed, rooted = (sem(n) for n in ("projected", "squared", "summed", "rooted"))
        den_done, rden_done, cosine_done, updated = (
            sem(n) for n in ("den_done", "rden_done", "cosine_done", "updated"))
        ctx_groups = ctxT.rearrange("c (i s n) -> c i s n", s=2, n=N)
        with nc.Block() as block:
            @block.sync
            def _(sp):
                load(sp, weights, [(wv[:, :], wvT), (wt[:, :], wtT), (bvc[:, :], bv), (btc[:, :], bt)])

                for s in range(2):
                    sp.dma_start(cT[:, s, :], ctx_groups[:, 0, s, :]).then_inc(ctx_landed[s], 16)
                with sp.Fori(1, PAIRS) as i:
                    for s in range(2):
                        sp.wait_ge(projected, i * 2 + s - 1)
                        sp.dma_start(cT[:, s, :], ctx_groups[:, i, s, :]).then_inc(ctx_landed[s], 16)
                load_ahead(sp, ahead)

            @block.gpsimd
            def _(pool):
                for it in range(2):
                    norm.gpsimd_rstd(pool, 0, it, it)
                stream(pool, lambda at, before, after, after2: after2 and norm.gpsimd_rstd(pool, *after2))

            @block.vector
            def _(dve):
                dve.sem_inc(updated, 2)
                dve.wait_ge(core.x_landed[0], 16)
                norm.vector(dve, 0, 0, 0)
                norm.vector(dve, 0, 1, 1)

                def group(at, before, after, after2):
                    i, s, it = at
                    x = core.X_groups[:, i, s]
                    if not before:
                        dve.wait_ge(core.x_landed[1], 16)
                    if after2:
                        norm.vector_stats(dve, *after2)
                    dve.wait_ge(rooted, it + 1)
                    for j in range(G):
                        js = slice(j * S, (j + 1) * S)
                        last = nc.vector.tensor_scalar(den[:, s, js], tn[:, s, js], vn[:, s, j:j + 1], EPS,
                                                       ALU.mult, ALU.max)
                    last.then_inc(den_done, 1)
                    if after2:
                        norm.vector_normalise(dve, *after2)
                    dve.wait_ge(den_done, it + 1)
                    nc.vector.reciprocal(rden[:, s, :], den[:, s, :]).then_inc(rden_done, 1)
                    dve.wait_ge(rden_done, it + 1)
                    nc.vector.tensor_tensor(cosine[:, s, :], dots[s][:, :], rden[:, s, :],
                                            ALU.mult).then_inc(cosine_done, 1)
                    dve.wait_ge(cosine_done, it + 1)
                    nc.vector.scalar_tensor_tensor(
                        out=x, in0=cosine[:, s, :].rearrange("p (j d) -> p j d", j=G), scalar=core.gates[:, 0:1],
                        in1=x, op0=ALU.mult, op1=ALU.add).then_inc(updated, 1)
                stream(dve, group)

            @block.scalar
            def _(act):
                act.wait_ge(weights, 64)

                def square(at):
                    i, s, it = at
                    act.wait_ge(projected, it + 1)
                    for out, ps, bias, func in ((vT, vps, bvc, ACT.Identity), (v2, vps, bvc, ACT.Square),
                                                (tT, tps, btc, ACT.Identity), (t2, tps, btc, ACT.Square)):
                        last = nc.scalar.activation(out[:, s, :], ps[0:H, :], func, bias=bias[:, 0:1])
                    last.then_inc(squared, 1)

                norm.scalar_copy(act, 0, 0, 0)
                square((0, 0, 0))
                norm.scalar_copy(act, 0, 1, 1)

                def group(at, before, after, after2):
                    i, s, it = at
                    act.wait_ge(summed, it + 1)
                    nc.scalar.activation(tn[:, s, :], tn2[s][:, :], ACT.Sqrt)
                    nc.scalar.activation(vn[:, s, :], vn2[:, 8 * s:8 * s + G], ACT.Sqrt).then_inc(rooted, 1)
                    if after:
                        square(after)
                    if after2:
                        norm.scalar_copy(act, *after2)
                stream(act, group)

            @block.tensor
            def _(pe):
                pe.wait_ge(weights, 64)

                def project(at):
                    i, s, it = at
                    pe.wait_ge(ctx_landed[s], i * 16 + 16)
                    nc.tensor.matmul(tps[0:H, :], wt[:, :], cT[:, s, :], start=True, stop=True)
                    pe.wait_ge(norm.xT_ready, it + 1)
                    nc.tensor.matmul(vps[0:H, :], wv[:, :], norm.xT[:, s, :], start=True,
                                     stop=True).then_inc(projected, 1)

                norm.tensor_turn(pe, 0, 0, 0)
                project((0, 0, 0))
                norm.tensor_turn(pe, 0, 1, 1)

                def group(at, before, after, after2):
                    i, s, it = at
                    pe.wait_ge(squared, it + 1)
                    pe.wait_ge(updated, it + 1)
                    for j in range(G):
                        js = slice(j * S, (j + 1) * S)
                        nc.tensor.matmul(dots[s][:, js], vT[:, s, js], tT[:, s, js], start=True, stop=True)
                        nc.tensor.matmul(vn2[:, 8 * s + j:8 * s + j + 1], v2[:, s, js], core.ones[0:H, 0:1],
                                         start=True, stop=True)
                    nc.tensor.matmul(tn2[s][:, :], core.ones[0:H, :], t2[:, s, :], start=True,
                                     stop=True).then_inc(summed, 1)
                    if after:
                        project(after)
                    if after2:
                        norm.tensor_turn(pe, *after2)
                stream(pe, group)


QUADS = 4
UNITS = G * QUADS


class Attention:

    def __init__(self, core, ctx, layer, score_banks, turn_banks, scale):
        self.core, self.nc, self.scale = core, core.nc, scale
        self.score_banks, self.turn_banks = score_banks, turn_banks
        sb = lambda name, shape: core.sbuf(f"{layer}_{name}", shape, ctx=ctx)
        sem = lambda name: core.sem(ctx, f"{layer}_{name}")
        self.negmax = sb("negmax", [S, 2, 4])
        self.shifted = sb("shifted", [S, 2, 4, S])
        self.weights = sb("probs", [S, 2, 4, S])
        self.turned = sb("probsT", [S, 2, 4, S])
        self.scored, self.maxed, self.shifts = sem("scored"), sem("maxed"), sem("shifts")
        self.exps, self.flips, self.copies, self.weighed = sem("exps"), sem("flips"), sem("copies"), sem("weighed")

    def tensor_scores(self, pe, it, u, matmuls):
        pe.wait_ge(self.shifts, it * UNITS + u + 1)
        matmuls(self.score_banks[u % 2], u // QUADS, u % QUADS).then_inc(self.scored, 1)

    def vector_shift(self, dve, it, u):
        scores = self.score_banks[u % 2][:, :].rearrange("p (h k) -> p h k", h=4)
        negmax = self.negmax[:, u % 2, :]
        dve.wait_ge(self.scored, it * UNITS + u + 1)
        self.nc.vector.tensor_reduce(negmax, scores, AX.X, ALU.max, negate=True).then_inc(self.maxed, 1)
        dve.wait_ge(self.exps, it * UNITS + u + 1)
        dve.wait_ge(self.maxed, it * UNITS + u + 1)
        self.nc.vector.tensor_tensor(self.shifted[:, u % 2], scores,
                                     negmax.unsqueeze(2).to_broadcast([S, 4, S]), ALU.add).then_inc(self.shifts, 1)

    def scalar_exp(self, act, it, u):
        act.wait_ge(self.flips, it * UNITS + u + 1)
        act.wait_ge(self.shifts, it * UNITS + u + 3)
        self.nc.scalar.activation(self.weights[:, u % 2], self.shifted[:, u % 2], ACT.Exp,
                                  scale=self.scale).then_inc(self.exps, 1)

    def tensor_turn(self, pe, it, u):
        pe.wait_ge(self.copies, it * UNITS + u + 1)
        pe.wait_ge(self.exps, it * UNITS + u + 3)
        for h in range(4):
            last = self.nc.tensor.transpose(self.turn_banks[u % 2][:, h * S:(h + 1) * S],
                                            self.weights[:, u % 2, h, :], self.core.ident[:, :])
        last.then_inc(self.flips, 1)

    def scalar_copy(self, act, it, u):
        act.wait_ge(self.weighed, it * UNITS + u + 1)
        act.wait_ge(self.flips, it * UNITS + u + 3)
        self.nc.scalar.activation(self.turned[:, u % 2], self.turn_banks[u % 2][:, :], ACT.Copy).then_inc(self.copies, 1)

    def tensor_weigh(self, pe, it, u, out, values):
        pe.wait_ge(self.copies, it * UNITS + u + 3)
        for k in range(4):
            last = self.nc.tensor.matmul(out(u // QUADS, u % QUADS * 4 + k), self.turned[:, u % 2, k, :],
                                         values(u // QUADS, u % QUADS * 4 + k), start=True, stop=True)
        last.then_inc(self.weighed, 1)

    def vector_start(self, dve):
        dve.sem_inc(self.shifts, 2)

    def scalar_start(self, act):
        act.sem_inc(self.exps, 2)
        act.sem_inc(self.copies, 2)

    def tensor_start(self, pe):
        pe.sem_inc(self.flips, 2)
        pe.sem_inc(self.weighed, 2)


def unit_at(at, after, u):
    return (at, u) if u < UNITS else (after, u - UNITS) if after else None


def layer2_attention(core, ctxT, wq, bq, wk, bk, wv, bv_rows, w1, b1, w2, b2_row, head_mask, ahead):
    nc, HEADS, DH, FF = core.nc, 16, 8, 2 * D
    with ExitStack() as ctx:
        sb = lambda name, shape: core.sbuf("a1_" + name, shape, ctx=ctx)
        sem = lambda name: core.sem(ctx, "a1_" + name)
        bank = [core.psum(ctx, f"a1_bank{k}", [128, 512]) for k in range(8)]
        norm = Norm(core, ctx, "a1", bank[0])
        att = Attention(core, ctx, "a1", bank[1:3], bank[3:5], DH ** -0.5)
        out_banks, mlp_bank = bank[5:7], bank[7]
        wq_s, wk_s, wv_s = sb("wq", [D, D]), sb("wk", [C, D]), sb("wv", [C, D])
        bq_s, bk_s, bv_s = sb("bq", [D, 1]), sb("bk", [D, 1]), sb("bv", [S, D])
        w1_s, b1_s = sb("w1", [D, FF]), sb("b1", [128, 2])
        w2_s, b2_s = sb("w2", [128, 2, D]), sb("b2", [S, D])
        bias = Bias(core, ctx, "a1", b2_s, 1)
        mask = sb("mask", [D, HEADS])
        cT = sb("cT", [C, 2, N])
        qT, kT = sb("qT", [D, 2, N]), sb("kT", [D, 2, N])
        km = sb("k_masked", [D, 2, HEADS, G, S])
        v = sb("v_ones", [S, 2, G, HEADS, DH + 1])
        rsum, o = sb("rsum", [S, 2, HEADS]), sb("o", [S, 2, G, D])
        oT, hT = sb("oT", [D, N]), sb("hT", [128, 2, N])
        weights, ctx_landed, ones_set = sem("weights"), [sem("ctx_landed0"), sem("ctx_landed1")], sem("ones_set")
        k_projected, q_projected, v_projected = sem("k_projected"), sem("q_projected"), sem("v_projected")
        k_ready, q_ready, v_ready = sem("k_ready"), sem("q_ready"), sem("v_ready")
        masked_dve, masked_pool = sem("k_masked_by_vector"), sem("k_masked_by_gpsimd")
        sums_inverted, normalised, passed = sem("sums_inverted"), sem("normalised"), sem("masks_passed")
        o_turned, oT_ready, hidden, h_ready, mixed, updated = (
            sem(n) for n in ("o_turned", "oT_ready", "hidden", "h_ready", "mixed", "updated"))
        ctx_groups = ctxT.rearrange("c (i s n) -> c i s n", s=2, n=N)
        loads = [(wq_s[:, :], wq), (wk_s[:, :], wk), (wv_s[:, :], wv), (bq_s[:, :], bq), (bk_s[:, :], bk),
                 (bv_s[:, :], bv_rows), (w1_s[:, :], w1), (b1_s[:, :], b1), (w2_s[:, :, :], w2), (b2_s[:, :], b2_row),
                 (mask[:, :], head_mask)]
        LOADED = 16 * len(loads)
        BY_VECTOR = 11
        BY_POOL = HEADS - BY_VECTOR
        FIRST, LAST = (0, 0, 0), (PAIRS - 1, 1, GROUPS - 1)
        K_AT, Q_AT, V_AT, TURN_AT, HIDDEN_AT, MIX_AT = 0, 2, 4, 1, (3, 5), 7

        with nc.Block() as block:
            @block.sync
            def _(sp):
                for s in range(2):
                    sp.dma_start(cT[:, s, :], ctx_groups[:, 0, s, :]).then_inc(ctx_landed[s], 16)
                load(sp, weights, loads)
                load_ahead(sp, ahead)
                with sp.Fori(1, PAIRS) as i:
                    for s in range(2):
                        sp.wait_ge(k_projected, i * 2 + s - 1)
                        sp.wait_ge(v_projected, i * 2 + s - 1)
                        sp.dma_start(cT[:, s, :], ctx_groups[:, i, s, :]).then_inc(ctx_landed[s], 16)

            @block.gpsimd
            def _(pool):
                nc.gpsimd.memset(v[:, :, :, :, :], 1.0).then_inc(ones_set, 1)
                for it in range(2):
                    norm.gpsimd_rstd(pool, 0, it, it)
                pool.wait_ge(weights, LOADED)

                def mask_keys(at):
                    i, s, it = at
                    settled(pool, k_ready, it + 1, passed)
                    for h in range(BY_VECTOR, HEADS):
                        nc.gpsimd.tensor_scalar(km[:, s, h, :, :], kT[:, s, :].rearrange("p (b k) -> p b k", b=G),
                                                mask[:, h:h + 1], None, ALU.mult).then_inc(masked_pool, 1)
                mask_keys(FIRST)
                bias.gpsimd_start(pool)

                def group(at, before, after, after2):
                    if after:
                        mask_keys(after)
                    if after2:
                        norm.gpsimd_rstd(pool, *after2)
                    bias.gpsimd_add(pool, at, norm.xn_done)
                stream(pool, group)

            @block.vector
            def _(dve):
                dve.sem_inc(normalised, 2)
                att.vector_start(dve)
                norm.vector(dve, 0, 0, 0)
                norm.vector(dve, 0, 1, 1)
                dve.wait_ge(weights, LOADED)
                bias.vector_start()
                dve.wait_ge(ones_set, 1)

                def bias_values(at, ps):
                    i, s, it = at
                    dve.wait_ge(v_projected, it + 1)
                    nc.vector.tensor_tensor(
                        v[:, s, :, :, 0:DH], ps[:, :].rearrange("p (b h e) -> p b h e", b=G, h=HEADS),
                        bv_s[:, :].rearrange("p (h e) -> p h e", h=HEADS).unsqueeze(1).to_broadcast([S, G, HEADS, DH]),
                        ALU.add).then_inc(v_ready, 1)

                def normalise(at, b):
                    i, s, it = at
                    heads = out_banks[b % 2][:, 0:HEADS * (DH + 1)].rearrange("p (h e) -> p h e", h=HEADS)
                    dve.wait_ge(att.weighed, it * UNITS + 4 * b + 4 + 2)
                    nc.vector.reciprocal(rsum[:, b % 2, :], heads[:, :, DH]).then_inc(sums_inverted, 1)
                    dve.wait_ge(sums_inverted, it * G + b + 1)
                    nc.vector.tensor_tensor(o[:, s, b, :].rearrange("p (h e) -> p h e", h=HEADS), heads[:, :, 0:DH],
                                            rsum[:, b % 2, :].unsqueeze(2).to_broadcast([S, HEADS, DH]),
                                            ALU.mult).then_inc(normalised, 1)

                def update(at):
                    i, s, it = at
                    x = core.X_groups[:, i, s]
                    bias.vector_wait(dve, at)
                    dve.wait_ge(mixed, it + 1)
                    nc.vector.scalar_tensor_tensor(
                        out=x, in0=mlp_bank[:, :].rearrange("p (j d) -> p j d", j=G), scalar=core.gates[:, 1:2],
                        in1=x, op0=ALU.mult, op1=ALU.add).then_inc(updated, 1)

                def mask_keys(at, h):
                    i, s, it = at
                    dve.wait_ge(k_ready, it + 1)
                    nc.vector.tensor_scalar(km[:, s, h, :, :], kT[:, s, :].rearrange("p (b k) -> p b k", b=G),
                                            mask[:, h:h + 1], None, ALU.mult).then_inc(masked_dve, 1)

                for h in range(BY_VECTOR):
                    mask_keys(FIRST, h)
                bias_values(FIRST, bank[5])
                for u in range(3):
                    att.vector_shift(dve, 0, u)

                def group(at, before, after, after2):
                    for u in range(UNITS):
                        unit = unit_at(at, after, u + 3)
                        if unit:
                            att.vector_shift(dve, unit[0][2], unit[1])
                        if after and u == V_AT:
                            bias_values(after, bank[0])
                        if after and 1 <= u <= BY_VECTOR:
                            mask_keys(after, u - 1)
                        if before and u == MIX_AT:
                            update(before)
                        if u % 4 == 3:
                            normalise(at, u // 4)
                        if after2 and u == 5:
                            norm.vector_stats(dve, *after2)
                        if after2 and u == 11:
                            norm.vector_normalise(dve, *after2)
                stream(dve, group)
                update(LAST)

            @block.scalar
            def _(act):
                att.scalar_start(act)
                act.wait_ge(weights, LOADED)

                def bias_keys(at, ps):
                    act.wait_ge(k_projected, at[2] + 1)
                    nc.scalar.activation(kT[:, at[1], :], ps[:, :], ACT.Identity, bias=bk_s[:, 0:1]).then_inc(k_ready, 1)

                def bias_queries(at, ps):
                    act.wait_ge(q_projected, at[2] + 1)
                    nc.scalar.activation(qT[:, at[1], :], ps[:, :], ACT.Identity, bias=bq_s[:, 0:1]).then_inc(q_ready, 1)

                def copy_turned(at):
                    act.wait_ge(o_turned, at[2] + 1)
                    nc.scalar.activation(oT[:, :], mlp_bank[:, :], ACT.Copy).then_inc(oT_ready, 1)

                def rectify(at, f):
                    act.wait_ge(hidden, at[2] * 2 + f + 1)
                    nc.scalar.activation(hT[:, f, :], mlp_bank[:, :], ACT.Relu, bias=b1_s[:, f:f + 1]).then_inc(h_ready, 1)

                bias_keys(FIRST, bank[3])
                norm.scalar_copy(act, 0, 0, 0)
                bias_queries(FIRST, bank[4])
                norm.scalar_copy(act, 0, 1, 1)
                att.scalar_exp(act, 0, 0)
                att.scalar_copy(act, 0, 0)
                att.scalar_exp(act, 0, 1)
                att.scalar_exp(act, 0, 2)

                def group(at, before, after, after2):
                    for u in range(UNITS):
                        if after and u == K_AT:
                            bias_keys(after, bank[0])
                        if after and u == Q_AT:
                            bias_queries(after, bank[0])
                        for ahead, step in ((1, att.scalar_copy), (3, att.scalar_exp)):
                            unit = unit_at(at, after, u + ahead)
                            if unit:
                                step(act, unit[0][2], unit[1])
                        if before and u == TURN_AT:
                            copy_turned(before)
                        if before and u in HIDDEN_AT:
                            rectify(before, HIDDEN_AT.index(u))
                        if after2 and u == 14:
                            norm.scalar_copy(act, *after2)
                stream(act, group)
                copy_turned(LAST)
                for f in range(2):
                    rectify(LAST, f)

            @block.tensor
            def _(pe):
                att.tensor_start(pe)
                pe.sem_inc(updated, 1)
                pe.wait_ge(weights, LOADED)

                def project_keys(at, ps):
                    i, s, it = at
                    pe.wait_ge(ctx_landed[s], i * 16 + 16)
                    nc.tensor.matmul(ps[:, :], wk_s[:, :], cT[:, s, :], start=True, stop=True).then_inc(k_projected, 1)

                def project_queries(at, ps):
                    pe.wait_ge(norm.xT_ready, at[2] + 1)
                    nc.tensor.matmul(ps[:, :], wq_s[:, :], norm.xT[:, at[1], :], start=True,
                                     stop=True).then_inc(q_projected, 1)

                def project_values(at, ps):
                    for b in range(G):
                        last = nc.tensor.matmul(ps[:, b * S:(b + 1) * S], cT[:, at[1], b * S:(b + 1) * S], wv_s[:, :],
                                                start=True, stop=True)
                    last.then_inc(v_projected, 1)

                def scores(at, u):
                    i, s, it = at

                    def quad_scores(ps, b, quad):
                        if b == 0:
                            pe.wait_ge(masked_dve, it * BY_VECTOR + min(4 * quad + 4, BY_VECTOR))
                            if 4 * quad + 4 > BY_VECTOR:
                                pe.wait_ge(masked_pool, it * BY_POOL + 4 * quad + 4 - BY_VECTOR)
                        return nc.tensor.matmul(ps[:, :], qT[:, s, b * S:(b + 1) * S],
                                                km[:, s, 4 * quad:4 * quad + 4, b, :], start=True, stop=True)
                    att.tensor_scores(pe, it, u, quad_scores)

                def turn_outputs(at):
                    i, s, it = at
                    pe.wait_ge(normalised, it * G + G + 2)
                    pe.wait_ge(updated, it + 1)
                    for b in range(G):
                        last = nc.tensor.transpose(mlp_bank[:, b * S:(b + 1) * S], o[:, s, b, :], core.ident[:, :])
                    last.then_inc(o_turned, 1)

                def hide(at, f):
                    if f == 0:
                        pe.wait_ge(oT_ready, at[2] + 1)
                    else:
                        pe.wait_ge(h_ready, at[2] * 2 + 1)
                    nc.tensor.matmul(mlp_bank[:, :], w1_s[:, f * 128:(f + 1) * 128], oT[:, :], start=True,
                                     stop=True).then_inc(hidden, 1)

                def mix(at):
                    pe.wait_ge(h_ready, at[2] * 2 + 2)
                    for b in range(G):
                        bs = slice(b * S, (b + 1) * S)
                        for f in range(2):
                            last = nc.tensor.matmul(mlp_bank[:, bs], hT[:, f, bs], w2_s[:, f, :], start=f == 0,
                                                    stop=f == 1)
                    last.then_inc(mixed, 1)

                project_keys(FIRST, bank[3])
                norm.tensor_turn(pe, 0, 0, 0)
                project_queries(FIRST, bank[4])
                project_values(FIRST, bank[5])
                norm.tensor_turn(pe, 0, 1, 1)
                pe.wait_ge(q_ready, 1)
                pe.wait_ge(v_ready, 1)
                for u in range(3):
                    scores(FIRST, u)
                att.tensor_turn(pe, 0, 0)

                def group(at, before, after, after2):
                    i, s, it = at
                    for u in range(UNITS):
                        if after and u == K_AT:
                            pe.wait_ge(norm.xT_ready, after[2] + 1)
                            project_keys(after, bank[0])
                        if after and u == Q_AT:
                            pe.wait_ge(k_ready, after[2] + 1)
                            project_queries(after, bank[0])
                        if after and u == V_AT:
                            pe.wait_ge(q_ready, after[2] + 1)
                            project_values(after, bank[0])
                        if after and u == UNITS - 3:
                            pe.wait_ge(v_ready, after[2] + 1)
                        unit = unit_at(at, after, u + 3)
                        if unit:
                            scores(*unit)
                        unit = unit_at(at, after, u + 1)
                        if unit:
                            att.tensor_turn(pe, unit[0][2], unit[1])
                        if before and u == TURN_AT:
                            turn_outputs(before)
                        if before and u in HIDDEN_AT:
                            hide(before, HIDDEN_AT.index(u))
                        if before and u == MIX_AT:
                            mix(before)
                        if u % 4 == 0:
                            pe.wait_ge(normalised, it * G + u // 4 + 1)
                        att.tensor_weigh(pe, it, u,
                                         lambda b, h: out_banks[b % 2][:, h * (DH + 1):(h + 1) * (DH + 1)],
                                         lambda b, h: v[:, s, b, h, :])
                        if after2 and u == 13:
                            norm.tensor_turn(pe, *after2)
                stream(pe, group)
                turn_outputs(LAST)
                for f in range(2):
                    hide(LAST, f)
                mix(LAST)


def layer6_attention(core, ctxT, held):
    nc, HEADS, DH = core.nc, 16, 64
    TILES = HEADS * DH // 128
    PROJECTIONS = 3 * TILES
    with ExitStack() as ctx:
        sb = lambda name, shape: core.sbuf("a3_" + name, shape, ctx=ctx)
        sem = lambda name: core.sem(ctx, "a3_" + name)
        bank = [core.psum(ctx, f"a3_bank{k}", [128, 512]) for k in range(8)]
        norm = Norm(core, ctx, "a3", bank[0])
        att = Attention(core, ctx, "a3", bank[1:3], bank[3:5], DH ** -0.5)
        out_banks, mix_bank = bank[5:7], bank[7]
        start_banks = bank[3:7]
        wq_s, wk_s, wv_s, wo_s, bo_s = held.tiles
        bias = Bias(core, ctx, "a3", bo_s, 3)
        cT = sb("cT", [C, 2, N])
        qT, kT = sb("qT", [128, 2, TILES, N]), sb("kT", [128, 2, TILES, N])
        v = sb("v_ones", [S, 2, G, HEADS, DH + 1])
        rsum, o, oT = sb("rsum", [S, 2, 4]), sb("o", [S, 2, HEADS * DH]), sb("oT", [128, TILES, S])
        ctx_landed, ones_set = [sem("ctx_landed0"), sem("ctx_landed1")], sem("ones_set")
        projected, emptied = [sem("projected_even"), sem("projected_odd")], [sem("emptied_by_scalar"), sem("emptied_by_vector")]
        sums_inverted, normalised = sem("sums_inverted"), sem("normalised")
        o_turned, oT_ready, mixed, updated = (sem(n) for n in ("o_turned", "oT_ready", "mixed", "updated"))
        ctx_groups = ctxT.rearrange("c (i s n) -> c i s n", s=2, n=N)
        HALF = PROJECTIONS // 2

        def projection_out(s, n):
            if n < TILES:
                return qT[:, s, n, :]
            if n < 2 * TILES:
                return kT[:, s, n - TILES, :]
            b, half = divmod(n - 2 * TILES, 2)
            return v[:, s, b, 8 * half:8 * half + 8, 0:DH]

        def projection_in(bank_of, n):
            return bank_of[:, :] if n < 2 * TILES else bank_of[:, :].rearrange("p (h e) -> p h e", e=DH)

        def tail_of(at, before, u):
            b, phase = divmod(u - 4, 4)
            return (at, b, phase) if b >= 0 else (before, G - 1, phase) if before else (None, 0, 3)

        with nc.Block() as block:
            @block.sync
            def _(sp):
                for s in range(2):
                    sp.dma_start(cT[:, s, :], ctx_groups[:, 0, s, :]).then_inc(ctx_landed[s], 16)
                with sp.Fori(1, PAIRS) as i:
                    for s in range(2):
                        for k in range(2):
                            sp.wait_ge(projected[k], (i * 2 + s - 1) * HALF)
                        sp.dma_start(cT[:, s, :], ctx_groups[:, i, s, :]).then_inc(ctx_landed[s], 16)

            @block.gpsimd
            def _(pool):
                nc.gpsimd.memset(v[:, :, :, :, :], 1.0).then_inc(ones_set, 1)
                for it in range(2):
                    norm.gpsimd_rstd(pool, 0, it, it)
                bias.gpsimd_start(pool)

                def group(at, before, after, after2):
                    bias.gpsimd_add(pool, at, norm.xn_done)
                    if after2:
                        norm.gpsimd_rstd(pool, *after2)
                stream(pool, group)

            @block.vector
            def _(dve):
                dve.sem_inc(normalised, 2)
                dve.sem_inc(updated, 1)
                att.vector_start(dve)
                norm.vector(dve, 0, 0, 0)
                norm.vector(dve, 0, 1, 1)
                dve.wait_ge(held.landed, held.all)
                bias.vector_start()
                dve.wait_ge(ones_set, 1)

                def empty(at, n, bank_of):
                    i, s, it = at
                    dve.wait_ge(projected[1], it * HALF + n // 2 + 1)
                    nc.vector.tensor_copy(projection_out(s, n), projection_in(bank_of, n)).then_inc(emptied[1], 1)

                def normalise(it, u):
                    heads = out_banks[u % 2][:, 0:4 * (DH + 1)].rearrange("p (h e) -> p h e", h=4)
                    dve.wait_ge(att.weighed, it * UNITS + u + 3)
                    nc.vector.reciprocal(rsum[:, u % 2, :], heads[:, :, DH]).then_inc(sums_inverted, 1)
                    dve.wait_ge(sums_inverted, it * UNITS + u + 1)
                    b, quad = divmod(u, 4)
                    nc.vector.tensor_tensor(
                        o[:, b % 2, quad * 4 * DH:(quad + 1) * 4 * DH].rearrange("p (h e) -> p h e", h=4),
                        heads[:, :, 0:DH], rsum[:, u % 2, :].unsqueeze(2).to_broadcast([S, 4, DH]),
                        ALU.mult).then_inc(normalised, 1)

                def update(at, b):
                    i, s, it = at
                    x = core.X_groups[:, i, s, b, :]
                    bias.vector_wait(dve, at)
                    dve.wait_ge(mixed, it * G + b + 1)
                    nc.vector.scalar_tensor_tensor(out=x, in0=mix_bank[:, 0:D], scalar=core.gates[:, 3:4],
                                                   in1=x, op0=ALU.mult, op1=ALU.add).then_inc(updated, 1)

                for n in range(1, PROJECTIONS, 2):
                    empty((0, 0, 0), n, start_banks[n % 4])
                for u in range(3):
                    att.vector_shift(dve, 0, u)

                def group(at, before, after, after2):
                    for u in range(UNITS):
                        ahead = unit_at(at, after, u + 3)
                        if ahead:
                            att.vector_shift(dve, ahead[0][2], ahead[1])
                        if after and u < HALF:
                            empty(after, 2 * u + 1, bank[0])
                        place, b, phase = tail_of(at, before, u)
                        if phase == 2 and place:
                            update(place, b)
                        normalise(at[2], u)
                        if after2 and u == 5:
                            norm.vector_stats(dve, *after2)
                        if after2 and u == 9:
                            norm.vector_normalise(dve, *after2)
                stream(dve, group)
                update((PAIRS - 1, 1, GROUPS - 1), G - 1)

            @block.scalar
            def _(act):
                att.scalar_start(act)
                norm.scalar_copy(act, 0, 0, 0)
                act.wait_ge(ones_set, 1)

                def empty(at, n, bank_of):
                    i, s, it = at
                    act.wait_ge(projected[0], it * HALF + n // 2 + 1)
                    nc.scalar.activation(projection_out(s, n), projection_in(bank_of, n), ACT.Copy)\
                        .then_inc(emptied[0], 1)

                def copy_turned(at, b, half):
                    act.wait_ge(o_turned, at[2] * 2 * G + 2 * b + half + 1)
                    nc.scalar.activation(oT[:, 4 * half:4 * half + 4, :],
                                         mix_bank[:, :].rearrange("p (t n) -> p t n", t=4), ACT.Copy).then_inc(oT_ready, 1)

                for n in range(0, PROJECTIONS, 2):
                    empty((0, 0, 0), n, start_banks[n % 4])
                norm.scalar_copy(act, 0, 1, 1)
                att.scalar_exp(act, 0, 0)
                att.scalar_copy(act, 0, 0)
                att.scalar_exp(act, 0, 1)
                att.scalar_exp(act, 0, 2)

                def group(at, before, after, after2):
                    for u in range(UNITS):
                        if after and u < HALF:
                            empty(after, 2 * u, bank[0])
                        for ahead, step in ((1, att.scalar_copy), (3, att.scalar_exp)):
                            unit = unit_at(at, after, u + ahead)
                            if unit:
                                step(act, unit[0][2], unit[1])
                        place, b, phase = tail_of(at, before, u)
                        if phase < 2 and place:
                            copy_turned(place, b, phase)
                        if after2 and u == 14:
                            norm.scalar_copy(act, *after2)
                stream(act, group)
                for half in range(2):
                    copy_turned((PAIRS - 1, 1, GROUPS - 1), G - 1, half)

            @block.tensor
            def _(pe):
                att.tensor_start(pe)
                pe.wait_ge(held.landed, held.all)

                def project(at, n, ps):
                    i, s, it = at
                    kind, t = divmod(n, TILES)
                    if kind < 2:
                        w, tokens = ((wq_s, norm.xT), (wk_s, cT))[kind]
                        mm = nc.tensor.matmul(ps[:, :], w[:, t * 128:(t + 1) * 128], tokens[:, s, :],
                                              start=True, stop=True)
                    else:
                        b, half = divmod(t, 2)
                        mm = nc.tensor.matmul(ps[:, :], cT[:, s, b * S:(b + 1) * S],
                                              wv_s[:, half * 512:half * 512 + 512], start=True, stop=True)
                    mm.then_inc(projected[n % 2], 1)

                def project_ahead(at, n):
                    i, s, it = at
                    if n == 0:
                        pe.wait_ge(ctx_landed[s], i * 16 + 16)
                        pe.wait_ge(norm.xT_ready, it + 1)
                    else:
                        pe.wait_ge(emptied[(n - 1) % 2], it * HALF + (n - 1) // 2 + 1)
                    project(at, n, bank[0])

                def wait_emptied(it):
                    for k in range(2):
                        pe.wait_ge(emptied[k], it * HALF + HALF)

                def scores(at, u):
                    i, s, it = at

                    def quad_scores(ps, b, quad):
                        r = 64 * (quad % 2)
                        for k in range(4):
                            t = 4 * (quad // 2) + k
                            last = nc.tensor.matmul(ps[:, k * S:(k + 1) * S], qT[r:r + 64, s, t, b * S:(b + 1) * S],
                                                    kT[r:r + 64, s, t, b * S:(b + 1) * S], start=True, stop=True)
                        return last
                    att.tensor_scores(pe, it, u, quad_scores)

                def tail(at, b, phase):
                    it = at[2]
                    if phase < 2:
                        if phase == 0:
                            pe.wait_ge(normalised, it * UNITS + 4 * b + 4 + 2)
                            pe.wait_ge(updated, it * G + b + 1)
                        else:
                            pe.wait_ge(oT_ready, it * 2 * G + 2 * b + 1)
                        for k in range(4):
                            t = 4 * phase + k
                            last = nc.tensor.transpose(mix_bank[:, k * S:(k + 1) * S], o[:, b % 2, t * 128:(t + 1) * 128],
                                                       core.ident[:, :])
                        last.then_inc(o_turned, 1)
                    elif phase == 2:
                        pe.wait_ge(oT_ready, it * 2 * G + 2 * b + 2)
                        for t in range(TILES):
                            last = nc.tensor.matmul(mix_bank[:, 0:D], oT[:, t, :], wo_s[:, t, :], start=t == 0,
                                                    stop=t == TILES - 1)
                        last.then_inc(mixed, 1)

                norm.tensor_turn(pe, 0, 0, 0)
                pe.wait_ge(ctx_landed[0], 16)
                pe.wait_ge(norm.xT_ready, 1)
                for n in range(PROJECTIONS):
                    if n >= 4:
                        pe.wait_ge(emptied[n % 2], (n - 4) // 2 + 1)
                    project((0, 0, 0), n, start_banks[n % 4])
                norm.tensor_turn(pe, 0, 1, 1)
                wait_emptied(0)
                for u in range(3):
                    scores((0, 0, 0), u)
                att.tensor_turn(pe, 0, 0)

                def group(at, before, after, after2):
                    i, s, it = at
                    for u in range(UNITS):
                        if after and u < HALF:
                            project_ahead(after, 2 * u)
                        if after and u == UNITS - 3:
                            wait_emptied(after[2])
                        unit = unit_at(at, after, u + 3)
                        if unit:
                            scores(*unit)
                        unit = unit_at(at, after, u + 1)
                        if unit:
                            att.tensor_turn(pe, unit[0][2], unit[1])
                        if after and u < HALF:
                            project_ahead(after, 2 * u + 1)
                        place, b, phase = tail_of(at, before, u)
                        if place:
                            tail(place, b, phase)
                        pe.wait_ge(normalised, it * UNITS + u + 1)
                        att.tensor_weigh(pe, it, u,
                                         lambda b, h: out_banks[u % 2][:, h % 4 * (DH + 1):(h % 4 + 1) * (DH + 1)],
                                         lambda b, h: v[:, s, b, h, :])
                        if after2 and u == 13:
                            norm.tensor_turn(pe, *after2)
                stream(pe, group)
                for phase in range(3):
                    tail((PAIRS - 1, 1, GROUPS - 1), G - 1, phase)


def layer7_selected_gelu(core, w_router, w_block, out):
    nc, SELECTED = core.nc, S * 3 // 4
    ROUNDS = SELECTED // 8
    with ExitStack() as ctx:
        sb = lambda name, shape: core.sbuf("f3_" + name, shape, ctx=ctx)
        sem = lambda name: core.sem(ctx, "f3_" + name)
        bank = [core.psum(ctx, f"f3_bank{k}", [128, 512]) for k in range(8)]
        norm = Norm(core, ctx, "f3", bank[0])
        wr, wb = sb("wr", [D, 1]), sb("wb", [D, D])
        scores = sb("scores", [S, B])
        scores_v = scores[:, :].rearrange("p (i s j) -> p i s j", s=2, j=G)
        gelu, diff, gn = sb("gelu", [S, 2, G, D]), sb("diff", [S, B, D]), sb("gated_n", [S, 2, G, D])
        diff_v = diff[:, :, :].rearrange("p (i s j) d -> p i s j d", s=2, j=G)
        cand, top8, selected, pick = sb("cand", [B, 2, S]), sb("top8", [B, 8]), sb("selected", [B, S]), sb("pick", [S, B])
        weights, scored, score_kept, gelu_done, diff_done, updated = (
            sem(n) for n in ("weights", "scored", "score_kept", "gelu_done", "diff_done", "updated"))
        turned, chain, selected_done, selected_turned, pick_done = (
            sem(n) for n in ("scores_turned", "ranking", "selected_done", "selected_turned", "pick_done"))
        gated, finished, stored = sem("gated"), sem("finished"), sem("stored")
        out_groups = out.rearrange("(g j) s d -> s g j d", j=G)
        with nc.Block() as block:
            @block.sync
            def _(sp):
                load(sp, weights, [(wr[:, :], w_router), (wb[:, :], w_block)])
                for g in range(GROUPS):
                    sp.wait_ge(finished, g + 1)
                    sp.dma_start(out_groups[:, g], core.X[:, g * G:g * G + G, :]).then_inc(stored, 16)
                sp.wait_ge(stored, 16 * GROUPS)

            @block.gpsimd
            def _(pool):
                pool.sem_inc(diff_done, 2)
                for it in range(2):
                    norm.gpsimd_rstd(pool, 0, it, it)

                def group(at, before, after, after2):
                    i, s, it = at
                    if after2:
                        norm.gpsimd_rstd(pool, *after2)
                    x = core.X_groups[:, i, s]
                    pool.wait_ge(gated, it + 1)
                    nc.gpsimd.tensor_tensor(x, x, gn[:, s], ALU.add).then_inc(updated, 1)
                    pool.wait_ge(gelu_done, it + 1)
                    nc.gpsimd.tensor_tensor(diff_v[:, i, s], gelu[:, s], norm.xn[:, s], ALU.subtract)\
                        .then_inc(diff_done, 1)
                stream(pool, group)

            @block.vector
            def _(dve):
                norm.vector(dve, 0, 0, 0)
                norm.vector(dve, 0, 1, 1)

                def group(at, before, after, after2):
                    i, s, it = at
                    if after2:
                        norm.vector_stats(dve, *after2)
                    dve.wait_ge(scored, it + 1)
                    nc.vector.tensor_copy(scores_v[:, i, s, :], bank[4 + s][:, 0:G]).then_inc(score_kept, 1)
                    if after2:
                        dve.wait_ge(diff_done, it + 3)
                        dve.wait_ge(gated, it + 1)
                        norm.vector_normalise(dve, *after2)
                stream(dve, group)
                dve.wait_ge(turned, 1)
                nc.vector.tensor_copy(cand[:, 0, :], bank[6][0:B, 0:S]).then_inc(chain, 1)
                for r in range(ROUNDS):
                    dve.wait_ge(chain, 2 * r + 1)
                    nc.vector.max(top8[:, :], cand[:, r % 2, :]).then_inc(chain, 1)
                    dve.wait_ge(chain, 2 * r + 2)
                    nc.vector.match_replace(cand[:, 1 - r % 2, :], top8[:, :], cand[:, r % 2, :], -BIG)\
                        .then_inc(chain, 1)
                dve.wait_ge(chain, 2 * ROUNDS + 1)
                nc.vector.tensor_scalar(selected[:, :], cand[:, ROUNDS % 2, :], -BIG, None, ALU.is_equal)\
                    .then_inc(selected_done, 1)
                dve.wait_ge(selected_turned, 1)
                nc.vector.tensor_scalar(pick[:, :], bank[7][:, 0:B], core.gates[:, 7:8], None, ALU.mult)\
                    .then_inc(pick_done, 1)
                dve.wait_ge(pick_done, 1)
                dve.wait_ge(updated, GROUPS)
                dve.wait_ge(diff_done, GROUPS + 2)
                for b in range(B):
                    last = nc.vector.scalar_tensor_tensor(out=core.X[:, b, :], in0=diff[:, b, :], scalar=pick[:, b:b + 1],
                                                          in1=core.X[:, b, :], op0=ALU.mult, op1=ALU.add)
                    if b % G == G - 1:
                        last.then_inc(finished, 1)

            @block.scalar
            def _(act):
                norm.scalar_copy(act, 0, 0, 0)
                norm.scalar_copy(act, 0, 1, 1)

                def group(at, before, after, after2):
                    i, s, it = at
                    act.wait_ge(norm.xn_done, it + 1)
                    act.wait_ge(diff_done, it + 1)
                    nc.scalar.activation(gn[:, s], norm.xn[:, s], ACT.Copy, scale=core.gates[:, 7:8]).then_inc(gated, 1)
                    act.wait_ge(scored, it + 1)
                    nc.scalar.activation(gelu[:, s].rearrange("p j d -> p (j d)"), bank[2 + s][:, :],
                                         ACT.Gelu_apprx_tanh).then_inc(gelu_done, 1)
                    if after2:
                        norm.scalar_copy(act, *after2)
                stream(act, group)

            @block.tensor
            def _(pe):
                pe.wait_ge(weights, 32)
                norm.tensor_turn(pe, 0, 0, 0)
                pe.wait_ge(norm.xT_ready, 1)
                norm.tensor_turn(pe, 0, 1, 1)

                def group(at, before, after, after2):
                    i, s, it = at
                    pe.wait_ge(norm.xT_ready, it + 1)
                    pe.wait_ge(diff_done, it + 1)
                    for b in range(G):
                        xT = norm.xT[:, s, b * S:(b + 1) * S]
                        nc.tensor.matmul(bank[2 + s][:, b * S:(b + 1) * S], xT, wb[:, :], start=True, stop=True)
                        last = nc.tensor.matmul(bank[4 + s][:, b:b + 1], xT, wr[:, :], start=True, stop=True)
                    last.then_inc(scored, 1)
                    if after2:
                        pe.wait_ge(norm.xT_ready, it + 2)
                        norm.tensor_turn(pe, *after2)
                stream(pe, group)
                pe.wait_ge(score_kept, GROUPS)
                nc.tensor.transpose(bank[6][0:B, 0:S], scores[:, :], core.ident[:, :]).then_inc(turned, 1)
                pe.wait_ge(selected_done, 1)
                nc.tensor.transpose(bank[7][:, 0:B], selected[:, :], core.ident[0:B, 0:B]).then_inc(selected_turned, 1)


def layer5_experts(core, gate_wT, w1T, b1, w2T, b2, ahead):
    nc, E, TOP = core.nc, 8, 2
    CAPACITY = int(1.25 * B * S / E)
    PAD = 8 - TOP
    with ExitStack() as ctx:
        sb = lambda name, shape: core.sbuf("f2_" + name, shape, ctx=ctx)
        sem = lambda name: core.sem(ctx, "f2_" + name)
        bank = [core.psum(ctx, f"f2_bank{k}", [128, 512]) for k in range(8)]
        norm = Norm(core, ctx, "f2", bank[0])
        gw, w1, b1_s, w2, b2_s = (sb("gw", [D, E]), sb("w1", [D, E, D]), sb("b1", [D, E]), sb("w2", [D, E, D]),
                                  sb("b2", [E, D]))
        xT_all = sb("xT_all", [D, B * S])
        xT_groups = xT_all[:, :].rearrange("d (i s n) -> d i s n", s=2, n=N)
        logits = sb("logits", [S, B, E])
        logits_v = logits[:, :, :].rearrange("p (i s j) e -> p i s (j e)", s=2, j=G)
        negmax, shifted, exps, sums, rsums = (sb("negmax", [S, B]), sb("shifted", [S, B, E]), sb("exps", [S, B, E]),
                                              sb("sums", [S, B]), sb("rsums", [S, B]))
        cand, top8, marked = sb("cand", [S, B, PAD + E]), sb("top8", [S, B, 8]), sb("marked", [S, B, PAD + E])
        chosen, counts, keep = sb("chosen", [S, B, E]), sb("counts", [S, E]), sb("keep", [S, E])
        w, wk, wg = sb("w", [S, B, E]), sb("w_kept", [S, B, E]), sb("w_gated", [S, B, E])
        wg_v = wg[:, :, :].rearrange("p (i s j) e -> p i s j e", s=2, j=G)
        wT = sb("wT", [E, B * S])
        h = sb("h", [D, 2, N])
        weights, scored, kept, all_turned = sem("weights"), sem("scored"), sem("logits_kept"), sem("xT_kept")
        chain, exp_done, ready, counts_in, counted, wg_done = (
            sem(n) for n in ("weighting", "exp_done", "ready_for_exp", "counts_in", "counted", "wg_done"))
        wT_turned, wT_kept, biased, bias_added = (sem(n) for n in ("wT_turned", "wT_kept", "biased", "bias_added"))
        hidden, activated, mixed, added = (sem(n) for n in ("hidden", "activated", "mixed", "added"))
        loads = [(gw[:, :], gate_wT), (w1[:, :, :], w1T), (b1_s[:, :], b1), (w2[:, :, :], w2T), (b2_s[:, :], b2)]
        LOADED = 16 * len(loads)
        with nc.Block() as block:
            @block.sync
            def _(sp):
                load(sp, weights, loads)
                load_ahead(sp, ahead)

            @block.gpsimd
            def _(pool):
                for it in range(2):
                    norm.gpsimd_rstd(pool, 0, it, it)
                stream(pool, lambda at, before, after, after2: after2 and norm.gpsimd_rstd(pool, *after2))

            @block.scalar
            def _(act):
                norm.scalar_copy(act, 0, 0, 0)
                norm.scalar_copy(act, 0, 1, 1)

                def group(at, before, after, after2):
                    i, s, it = at
                    act.wait_ge(norm.xT_ready, it + 1)
                    nc.scalar.activation(xT_groups[:, i, s, :], norm.xT[:, s, :], ACT.Copy).then_inc(all_turned, 1)
                    if after2:
                        norm.scalar_copy(act, *after2)
                stream(act, group)
                act.wait_ge(ready, 1)
                nc.scalar.activation(exps[:, :, :], shifted[:, :, :], ACT.Exp).then_inc(exp_done, 1)
                for g in range(GROUPS):
                    act.wait_ge(wT_turned, g + 1)
                    nc.scalar.activation(wT[:, g * N:(g + 1) * N], bank[2 + g % 2][0:E, :], ACT.Copy).then_inc(wT_kept, 1)

            @block.vector
            def _(dve):
                norm.vector(dve, 0, 0, 0)
                norm.vector(dve, 0, 1, 1)

                def group(at, before, after, after2):
                    i, s, it = at
                    if after2:
                        norm.vector_stats(dve, *after2)
                    dve.wait_ge(scored, it + 1)
                    nc.vector.tensor_copy(logits_v[:, i, s, :], bank[4 + s][:, 0:G * E]).then_inc(kept, 1)
                    if after2:
                        norm.vector_normalise(dve, *after2)
                stream(dve, group)
                wide = lambda a: a.unsqueeze(2).to_broadcast([S, B, E])
                dve.wait_ge(kept, GROUPS)
                nc.vector.tensor_reduce(negmax[:, :], logits[:, :, :], AX.X, ALU.max, negate=True).then_inc(chain, 1)
                dve.wait_ge(chain, 1)
                nc.vector.tensor_tensor(shifted[:, :, :], logits[:, :, :], wide(negmax[:, :]), ALU.add).then_inc(ready, 1)
                nc.vector.memset(cand[:, :, :], BIG).then_inc(chain, 1)
                dve.wait_ge(exp_done, 1)
                nc.vector.tensor_reduce(sums[:, :], exps[:, :, :], AX.X, ALU.add).then_inc(chain, 1)
                dve.wait_ge(chain, 3)
                nc.vector.reciprocal(rsums[:, :], sums[:, :]).then_inc(chain, 1)
                dve.wait_ge(chain, 4)
                nc.vector.tensor_tensor(cand[:, :, PAD:], exps[:, :, :], wide(rsums[:, :]), ALU.mult).then_inc(chain, 1)
                dve.wait_ge(chain, 5)
                for b in range(B):
                    nc.vector.max(top8[:, b, :], cand[:, b, :]).then_inc(chain, 1)
                dve.wait_ge(chain, 5 + B)
                for b in range(B):
                    nc.vector.match_replace(marked[:, b, :], top8[:, b, :], cand[:, b, :], -BIG).then_inc(chain, 1)
                dve.wait_ge(chain, 5 + 2 * B)
                nc.vector.tensor_scalar(chosen[:, :, :], marked[:, :, PAD:], -BIG, None, ALU.is_equal).then_inc(chain, 1)
                dve.wait_ge(chain, 6 + 2 * B)
                nc.vector.tensor_reduce(counts[:, :], chosen[:, :, :].rearrange("p b e -> p e b"), AX.X,
                                        ALU.add).then_inc(counts_in, 1)
                nc.vector.tensor_tensor(w[:, :, :], chosen[:, :, :], cand[:, :, PAD:], ALU.mult).then_inc(chain, 1)
                dve.wait_ge(counted, 1)
                nc.vector.tensor_scalar(keep[:, :], bank[6][:, 0:E], float(CAPACITY), None, ALU.is_le).then_inc(chain, 1)
                dve.wait_ge(chain, 8 + 2 * B)
                nc.vector.tensor_tensor(wk[:, :, :], w[:, :, :], keep[:, :].unsqueeze(1).to_broadcast([S, B, E]),
                                        ALU.mult).then_inc(chain, 1)
                dve.wait_ge(chain, 9 + 2 * B)
                nc.vector.tensor_scalar(wg[:, :, :], wk[:, :, :], core.gates[:, 6:7], None, ALU.mult).then_inc(wg_done, 1)
                for g in range(GROUPS):
                    x = core.X[:, g * G:(g + 1) * G, :]
                    dve.wait_ge(biased, g + 1)
                    nc.vector.tensor_tensor(x, bank[4 + g % 2][:, :].rearrange("p (j d) -> p j d", j=G), x,
                                            ALU.add).then_inc(bias_added, 1)

            @block.tensor
            def _(pe):
                pe.wait_ge(weights, LOADED)
                norm.tensor_turn(pe, 0, 0, 0)
                pe.wait_ge(norm.xT_ready, 1)
                norm.tensor_turn(pe, 0, 1, 1)

                def group(at, before, after, after2):
                    i, s, it = at
                    pe.wait_ge(norm.xT_ready, it + 1)
                    for b in range(G):
                        last = nc.tensor.matmul(bank[4 + s][:, b * E:(b + 1) * E], norm.xT[:, s, b * S:(b + 1) * S],
                                                gw[:, :], start=True, stop=True)
                    last.then_inc(scored, 1)
                    if after2:
                        pe.wait_ge(kept, it + 1)
                        pe.wait_ge(all_turned, it + 1)
                        pe.wait_ge(norm.xT_ready, it + 2)
                        norm.tensor_turn(pe, *after2)
                stream(pe, group)
                pe.wait_ge(counts_in, 1)
                nc.tensor.matmul(bank[6][:, 0:E], core.ones[:, :], counts[:, :], start=True, stop=True)\
                    .then_inc(counted, 1)
                pe.wait_ge(wg_done, 1)

                def turn(g):
                    if g >= 2:
                        pe.wait_ge(wT_kept, g - 1)
                    for j in range(G):
                        last = nc.tensor.transpose(bank[2 + g % 2][0:E, j * S:(j + 1) * S], wg[:, g * G + j, :],
                                                   core.ident[:, :])
                    last.then_inc(wT_turned, 1)

                turn(0)
                for g in range(GROUPS):
                    if g + 1 < GROUPS:
                        turn(g + 1)
                    pe.wait_ge(wT_kept, g + 1)
                    if g >= 2:
                        pe.wait_ge(bias_added, g - 1)
                    for j in range(G):
                        b = g * G + j
                        last = nc.tensor.matmul(bank[4 + g % 2][:, j * S:(j + 1) * S], wT[:, b * S:(b + 1) * S],
                                                b2_s[:, :], start=True, stop=True)
                    last.then_inc(biased, 1)

        with nc.Block() as block:
            @block.tensor
            def _(pe):
                pe.sem_inc(mixed, 2)

                def expand(i, s, it, e):
                    pe.wait_ge(activated, it * E + e + 1)
                    nc.tensor.matmul(bank[e % 2][:, :], w1[:, e, :], xT_groups[:, i, s, :], start=True,
                                     stop=True).then_inc(hidden, 1)

                expand(0, 0, 0, 0)

                def group(i, s, it, nxt):
                    for e in range(E):
                        if e + 1 < E:
                            expand(i, s, it, e + 1)
                        elif nxt:
                            expand(nxt[0], nxt[1], nxt[2], 0)
                        pe.wait_ge(activated, it * E + e + 3)
                        pe.wait_ge(added, it * E + e + 1)
                        for j in range(G):
                            last = nc.tensor.matmul(bank[2 + e % 2][:, j * S:(j + 1) * S],
                                                    h[:, e % 2, j * S:(j + 1) * S], w2[:, e, :], start=True, stop=True)
                        last.then_inc(mixed, 1)
                turns(pe, group)

            @block.scalar
            def _(act):
                act.sem_inc(activated, 2)

                def group(i, s, it, nxt):
                    for e in range(E):
                        act.wait_ge(mixed, it * E + e + 1)
                        act.wait_ge(hidden, it * E + e + 1)
                        nc.scalar.activation(h[:, e % 2, :], bank[e % 2][:, :], ACT.Silu,
                                             bias=b1_s[:, e:e + 1]).then_inc(activated, 1)
                turns(act, group)

            @block.vector
            def _(dve):
                dve.sem_inc(added, 2)

                def group(i, s, it, nxt):
                    x = core.X_groups[:, i, s]
                    for e in range(E):
                        dve.wait_ge(mixed, it * E + e + 3)
                        if e >= 1:
                            dve.wait_ge(added, it * E + e + 2)
                        for j in range(G):
                            last = nc.vector.scalar_tensor_tensor(
                                out=x[:, j, :], in0=bank[2 + e % 2][:, j * S:(j + 1) * S],
                                scalar=wg_v[:, i, s, j, e:e + 1], in1=x[:, j, :], op0=ALU.mult, op1=ALU.add)
                        last.then_inc(added, 1)
                turns(dve, group)


def layer3_experts(core, held, ahead):
    nc, ER, EZ, TOP, I, SCALE = core.nc, 32, 8, 6, 64, 2.5
    E, OCT, PAD = ER + EZ, 8, 8 - TOP
    PER = ER // OCT
    LAG, DOWN_LAG = 3, 4
    with ExitStack() as ctx:
        sb = lambda name, shape: core.sbuf("f1_" + name, shape, ctx=ctx)
        sem = lambda name: core.sem(ctx, "f1_" + name)
        norm_bank = core.psum(ctx, "f1_norm_bank", [128, 512])
        acc = core.psum(ctx, "f1_acc", [128, 512])
        turn_banks = [core.psum(ctx, f"f1_turn{k}", [128, 512]) for k in range(2)]
        gu_ps = [core.psum(ctx, f"f1_gu{k}", [128, 1024]) for k in range(2)]
        norm = Norm(core, ctx, "f1", norm_bank)
        rw, bias, gu_w, down_w = held.tiles
        gscale = sb("gate_scale", [128, 1])
        negmax, shifted, exps = sb("negmax", [S, G]), sb("shifted", [S, G, E]), sb("exps", [S, G, E])
        sums, rsums, probs = sb("sums", [S, G]), sb("rsums", [S, G]), sb("probs", [S, G, E])
        cand, top8, marked = sb("cand", [S, G, PAD + E]), sb("top8", [S, G, 8]), sb("marked", [S, G, PAD + E])
        chosen, w, wz = sb("chosen", [S, G, E]), sb("w", [S, 2, G, E]), sb("w_identity", [S, 2, G])
        silu, gated, h, hT = (sb("silu", [S, 2, OCT, I]), sb("gated", [S, 2, OCT, I]), sb("h", [S, 2, OCT, I]),
                              sb("hT", [2 * I, 2, OCT // 2, S]))
        logits_in, shift_done, exp_done, routed, chain = (
            sem(n) for n in ("logits_in", "shift_done", "exp_done", "routed", "routing"))
        gu_done, silus, gateds, weighted, flips, copies, downs = (
            sem(n) for n in ("gate_up_done", "silus", "gateds", "weighteds", "flips", "copies", "downs"))
        identity_added, updated, passed = (sem(n) for n in ("identity_added", "updated", "passed_routing"))
        CHAIN = 15
        weights, LOADED = held.landed, held.all
        with nc.Block() as block:
            @block.sync
            def _(sp):
                load_ahead(sp, ahead)

            @block.gpsimd
            def _(pool):
                pool.sem_inc(weighted, 2)
                norm.gpsimd_rstd(pool, 0, 0, 0)

                def group(i, s, it, nxt):
                    for u in range(G * PER):
                        if u == 4 and nxt:
                            norm.gpsimd_rstd(pool, *nxt)
                        b, o = divmod(u, PER)
                        unit = it * G * PER + u
                        pool.wait_ge(flips, unit + 1)
                        if u == 0:
                            pool.wait_ge(routed, it + 1)
                        pool.wait_ge(gateds, unit + 3)
                        nc.gpsimd.tensor_tensor(
                            h[:, u % 2], gated[:, u % 2],
                            w[:, s, b, o * OCT:(o + 1) * OCT].unsqueeze(2).to_broadcast([S, OCT, I]),
                            ALU.mult).then_inc(weighted, 1)
                turns(pool, group)

            @block.vector
            def _(dve):
                dve.sem_inc(gateds, 2)
                dve.sem_inc(updated, 2)
                nc.vector.memset(cand[:, :, :], BIG).then_inc(chain, 1)
                nc.vector.tensor_scalar(gscale[:, :], core.gates[:, 5:6], SCALE, None, ALU.mult).then_inc(chain, 1)
                dve.wait_ge(weights, LOADED)
                wide = lambda a: a.unsqueeze(2).to_broadcast([S, G, E])

                def route(s, it):
                    step = lambda n: it * CHAIN + n + 2
                    logits = norm_bank[:, 0:G * E].rearrange("p (j e) -> p j e", j=G)
                    dve.wait_ge(logits_in, it + 1)
                    nc.vector.tensor_reduce(negmax[:, :], logits, AX.X, ALU.max, negate=True).then_inc(chain, 1)
                    dve.wait_ge(chain, step(1))
                    nc.vector.tensor_tensor(shifted[:, :, :], logits, wide(negmax[:, :]), ALU.add).then_inc(shift_done, 1)
                    dve.wait_ge(exp_done, it + 1)
                    nc.vector.tensor_reduce(sums[:, :], exps[:, :, :], AX.X, ALU.add).then_inc(chain, 1)
                    dve.wait_ge(chain, step(2))
                    nc.vector.reciprocal(rsums[:, :], sums[:, :]).then_inc(chain, 1)
                    dve.wait_ge(chain, step(3))
                    nc.vector.tensor_tensor(probs[:, :, :], exps[:, :, :], wide(rsums[:, :]), ALU.mult).then_inc(chain, 1)
                    dve.wait_ge(chain, step(4))
                    nc.vector.tensor_tensor(cand[:, :, PAD:], probs[:, :, :],
                                            bias[:, :].unsqueeze(1).to_broadcast([S, G, E]), ALU.add).then_inc(chain, 1)
                    settled(dve, chain, step(5), passed)
                    for j in range(G):
                        nc.vector.max(top8[:, j, :], cand[:, j, :]).then_inc(chain, 1)
                    settled(dve, chain, step(5 + G), passed)
                    for j in range(G):
                        nc.vector.match_replace(marked[:, j, :], top8[:, j, :], cand[:, j, :], -BIG).then_inc(chain, 1)
                    dve.wait_ge(chain, step(5 + 2 * G))
                    nc.vector.tensor_scalar(chosen[:, :, :], marked[:, :, PAD:], -BIG, gscale[:, 0:1], ALU.is_equal,
                                            ALU.mult).then_inc(chain, 1)
                    dve.wait_ge(chain, step(6 + 2 * G))
                    nc.vector.tensor_tensor(w[:, s], chosen[:, :, :], probs[:, :, :], ALU.mult).then_inc(chain, 1)
                    dve.wait_ge(chain, step(7 + 2 * G))
                    nc.vector.tensor_reduce(wz[:, s, :], w[:, s, :, ER:], AX.X, ALU.add).then_inc(routed, 1)

                norm.vector(dve, 0, 0, 0)
                route(0, 0)

                def group(i, s, it, nxt):
                    x = core.X_groups[:, i, s]
                    for u in range(G * PER):
                        unit = it * G * PER + u
                        up = gu_ps[u % 2][:, :].rearrange("p (e c) -> p e c", e=OCT)[:, :, I:]
                        dve.wait_ge(weighted, unit + 1)
                        dve.wait_ge(silus, unit + 1)
                        nc.vector.tensor_tensor(gated[:, u % 2], silu[:, u % 2], up, ALU.mult).then_inc(gateds, 1)
                        if nxt and u == 2:
                            norm.vector_stats(dve, *nxt)
                        if nxt and u == 5:
                            norm.vector_normalise(dve, *nxt)
                        if nxt and u == 12:
                            route(nxt[1], nxt[2])
                    dve.wait_ge(routed, it + 1)
                    for j in range(G):
                        last = nc.vector.scalar_tensor_tensor(out=x[:, j, :], in0=norm.xn[:, s, j, :],
                                                              scalar=wz[:, s, j:j + 1], in1=x[:, j, :],
                                                              op0=ALU.mult, op1=ALU.add)
                    last.then_inc(identity_added, 1)
                    dve.wait_ge(identity_added, it + 1)
                    dve.wait_ge(downs, (it + 1) * G * PER + 2)
                    nc.vector.tensor_tensor(x, acc[:, :].rearrange("p (j d) -> p j d", j=G), x, ALU.add)\
                        .then_inc(updated, 1)
                turns(dve, group)

            @block.scalar
            def _(act):
                act.sem_inc(copies, 2)

                def exp_of(it):
                    act.wait_ge(shift_done, it + 1)
                    nc.scalar.activation(exps[:, :, :], shifted[:, :, :], ACT.Exp).then_inc(exp_done, 1)

                norm.scalar_copy(act, 0, 0, 0)
                exp_of(0)

                def group(i, s, it, nxt):
                    for step in range(G * PER + LAG + 1):
                        if step < G * PER:
                            unit = it * G * PER + step
                            gate = gu_ps[step % 2][:, :].rearrange("p (e c) -> p e c", e=OCT)[:, :, 0:I]
                            act.wait_ge(gateds, unit + 1)
                            act.wait_ge(gu_done, unit + 1)
                            nc.scalar.activation(silu[:, step % 2], gate, ACT.Silu).then_inc(silus, 1)
                        if nxt and step == 8:
                            norm.scalar_copy(act, *nxt)
                        if nxt and step == 12:
                            exp_of(nxt[2])
                        if 0 <= step - LAG < G * PER:
                            u = step - LAG
                            unit = it * G * PER + u
                            act.wait_ge(downs, unit + 1)
                            act.wait_ge(flips, unit + 3)
                            nc.scalar.activation(hT[:, u % 2].rearrange("p e t -> p (e t)"), turn_banks[u % 2][:, :],
                                                 ACT.Copy).then_inc(copies, 1)
                turns(act, group)

            @block.tensor
            def _(pe):
                pe.sem_inc(flips, 2)
                pe.sem_inc(downs, 2)
                pe.wait_ge(weights, LOADED)

                def router(s, it):
                    pe.wait_ge(norm.xT_ready, it + 1)
                    for j in range(G):
                        last = nc.tensor.matmul(norm_bank[:, j * E:(j + 1) * E], norm.xT[:, s, j * S:(j + 1) * S],
                                                rw[:, :], start=True, stop=True)
                    last.then_inc(logits_in, 1)

                norm.tensor_turn(pe, 0, 0, 0)
                router(0, 0)

                def group(i, s, it, nxt):
                    for step in range(G * PER + DOWN_LAG):
                        if step < G * PER:
                            b, o = divmod(step, PER)
                            unit = it * G * PER + step
                            pe.wait_ge(gateds, unit + 1)
                            for k in range(2):
                                last = nc.tensor.matmul(
                                    gu_ps[step % 2][:, k * 512:(k + 1) * 512], norm.xT[:, s, b * S:(b + 1) * S],
                                    gu_w[:, o * OCT + 4 * k:o * OCT + 4 * k + 4, :], start=True, stop=True)
                            last.then_inc(gu_done, 1)
                        if nxt and step == 7:
                            pe.wait_ge(routed, it + 1)
                            norm.tensor_turn(pe, *nxt)
                        if nxt and step == 10:
                            router(nxt[1], nxt[2])
                        if 0 <= step - LAG < G * PER:
                            u = step - LAG
                            unit = it * G * PER + u
                            pe.wait_ge(copies, unit + 1)
                            pe.wait_ge(weighted, unit + 3)
                            hw = h[:, u % 2].rearrange("p e c -> p (e c)")
                            for k in range(OCT // 2):
                                last = nc.tensor.transpose(turn_banks[u % 2][:, k * S:(k + 1) * S],
                                                           hw[:, k * 2 * I:(k + 1) * 2 * I], core.ident[:, :])
                            last.then_inc(flips, 1)
                        if step >= DOWN_LAG:
                            u = step - DOWN_LAG
                            unit = it * G * PER + u
                            b, o = divmod(u, PER)
                            if u == 0:
                                pe.wait_ge(updated, it + 2)
                            pe.wait_ge(copies, unit + 3)
                            for k in range(OCT // 2):
                                p = o * OCT // 2 + k
                                last = nc.tensor.matmul(acc[:, b * S:(b + 1) * S], hT[:, u % 2, k, :], down_w[:, p, :],
                                                        start=p == 0, stop=p == ER // 2 - 1)
                            last.then_inc(downs, 1)
                turns(pe, group)


def layer4_perceiver(core, ctx_nat, lnx_g, lnx_b, lnl_g, lnl_b, q_gamma, k_gamma, held):
    nc, H, DH = core.nc, 2, 64
    MASKED = 3.4e38
    QK_TINY = 1e-8 ** 2
    with ExitStack() as ctx:
        sb = lambda name, shape, dt=F32: core.sbuf("a2_" + name, shape, dt, ctx=ctx)
        sem = lambda name: core.sem(ctx, "a2_" + name)
        bank = [core.psum(ctx, f"a2_bank{k}", [128, 512]) for k in range(8)]
        c_nat = sb("ctx", [S, 2, G, C])
        n_x = Norm(core, ctx, "a2x", None)
        n_l = Norm(core, ctx, "a2l", bank[0], source=lambda i, s: n_x.xn[:, s])
        n_c = Norm(core, ctx, "a2c", bank[1], width=C, source=lambda i, s: c_nat[:, s])
        q_gain = sb("q_gain", [128, 1])
        vecs = sb("vecs", [128, 6])
        wc, wl, wo, bo, mask_u8 = held.tiles
        neg = sb("neg", [S, B, 2, S])
        bias = Bias(core, ctx, "a2", bo, 2)
        neg_v = neg[:, :, :, :].rearrange("p (i s j) c k -> p i s j (c k)", s=2, j=G)
        lT, cT = sb("latT", [D, 2, N]), sb("ctxT", [C, 2, N])
        qk = sb("qk", [S, 2, G, 3, D])
        v = sb("v", [S, 2, G, 2, D])
        sq, ss, ms, rn, qkn = (sb("sq", [S, G * 3 * D]), sb("ss", [S, G * 6]), sb("ms", [S, G * 6]),
                               sb("rn", [S, 2, G * 6]), sb("qkn", [S, 2, G, 3, D]))
        qT, kT = sb("qT", [D, 2, G, S]), sb("kT", [D, 2, G, 2, S])
        sc, negmax = sb("scores", [S, 2, H, G, 2 * S]), sb("negmax", [S, H, G])
        probs, psum_, rsum = sb("probs", [S, 2, H, G, 2 * S]), sb("prob_sums", [S, 2, G, H]), sb("rsum", [S, G, H])
        pT = sb("probsT", [S, 2, 4, 4, S])
        o, oT = sb("o", [S, 2, G, D]), sb("oT", [D, 2, N])
        weights, ctx_landed = sem("weights"), [sem("ctx_landed0"), sem("ctx_landed1")]
        neg_done, gain_done, sums_done, sums_inverted = (sem(n) for n in ("neg_done", "gain_done", "squares_summed", "sums_inverted"))
        lT_ready, cT_ready, lat_proj, ctx_proj, lat_kept, ctx_kept = (
            sem(n) for n in ("lT_ready", "cT_ready", "lat_projected", "ctx_projected", "lat_kept", "ctx_kept"))
        squares, ms_done, rn_done, qkn_done, qk_turned, qkT_ready = (
            sem(n) for n in ("squares", "ms_done", "rn_done", "qkn_done", "qk_turned", "qkT_ready"))
        scored, masked, shift_ready, exps, flips, pT_act, pT_dve, weighed = (
            sem(n) for n in ("scored", "masked", "shift_ready", "exps", "flips", "pT_by_scalar", "pT_by_vector",
                             "weighed"))
        normalised, o_turned, oT_ready, mixed, updated = (
            sem(n) for n in ("normalised", "o_turned", "oT_ready", "mixed", "updated"))
        FIRST, SECOND = (0, 0, 0), (0, 1, 1)
        lat_bank, ctx_bank = (lambda b: bank[(0, 6)[b % 2]]), (lambda b: bank[(1, 7)[b % 2]])
        nat_groups = ctx_nat.rearrange("(i s j) t c -> t i s j c", s=2, j=G)
        loads = [(vecs[0:C, 0:1], lnx_g), (vecs[0:C, 1:2], lnx_b),
                 (vecs[:, 2:3], lnl_g), (vecs[:, 3:4], lnl_b), (vecs[:, 4:5], q_gamma), (vecs[:, 5:6], k_gamma)]
        LOADED = 16 * len(loads)
        with nc.Block() as block:
            @block.sync
            def _(sp):
                load(sp, weights, loads)
                for s in range(2):
                    sp.dma_start(c_nat[:, s], nat_groups[:, 0, s]).then_inc(ctx_landed[s], 16)
                with sp.Fori(1, PAIRS) as i:
                    for s in range(2):
                        sp.wait_ge(n_c.xn_done, i * 2 + s - 1)
                        sp.dma_start(c_nat[:, s], nat_groups[:, i, s]).then_inc(ctx_landed[s], 16)

            @block.gpsimd
            def _(pool):
                nc.gpsimd.memset(neg[:, :, 1, :], 0.0).then_inc(neg_done, 1)

                def root(at):
                    i, s, it = at
                    pool.wait_ge(ms_done, it + 1)
                    nc.gpsimd.tensor_tensor(rn[:, s, :], ms[:, :], core.minus_half[:, 0:G * 6], ALU.pow)\
                        .then_inc(rn_done, 1)

                for at in (FIRST, SECOND):
                    n_x.gpsimd_rstd(pool, *at)
                    n_c.gpsimd_rstd(pool, *at)
                    n_l.gpsimd_rstd(pool, *at)
                root(FIRST)
                bias.gpsimd_start(pool)

                def group(at, before, after, after2):
                    bias.gpsimd_add(pool, at, n_x.xn_done)
                    if after2:
                        n_x.gpsimd_rstd(pool, *after2)
                        n_c.gpsimd_rstd(pool, *after2)
                    if after:
                        root(after)
                    if after2:
                        n_l.gpsimd_rstd(pool, *after2)
                stream(pool, group)

            @block.vector
            def _(dve):
                dve.sem_inc(updated, 1)

                def statistics(at):
                    i, s, it = at
                    n_x.vector_stats(dve, i, s, it)
                    dve.wait_ge(ctx_landed[s], i * 16 + 16)
                    n_c.vector_stats(dve, i, s, it)

                def normalise_inputs(at):
                    n_x.vector_normalise(dve, *at)
                    n_c.vector_normalise(dve, *at)

                def normalise_latents(at):
                    dve.wait_ge(n_x.xn_done, at[2] + 1)
                    n_l.vector_stats(dve, *at)
                    n_l.vector_normalise(dve, *at)

                def mean_squares(at):
                    dve.wait_ge(squares, at[2] + 1)
                    nc.vector.tensor_reduce(ss[:, :], sq[:, :].rearrange("p (n e) -> p n e", e=DH), AX.X, ALU.add)\
                        .then_inc(sums_done, 1)
                    dve.wait_ge(sums_done, at[2] + 1)
                    nc.vector.tensor_scalar(ms[:, :], ss[:, :], 1.0 / DH, QK_TINY, ALU.mult, ALU.max).then_inc(ms_done, 1)

                def scale_queries_keys(at):
                    i, s, it = at
                    dve.wait_ge(rn_done, it + 1)
                    nc.vector.tensor_tensor(
                        qkn[:, s].rearrange("p b c (h e) -> p (b c h) e", h=H),
                        qk[:, s].rearrange("p b c (h e) -> p (b c h) e", h=H),
                        rn[:, s, :].unsqueeze(2).to_broadcast([S, G * 6, DH]), ALU.mult).then_inc(qkn_done, 1)

                statistics(FIRST)
                normalise_inputs(FIRST)
                normalise_latents(FIRST)
                dve.wait_ge(held.landed, held.all)
                dve.wait_ge(weights, LOADED)
                nc.vector.tensor_scalar(q_gain[:, :], vecs[:, 4:5], DH ** -0.5, None, ALU.mult).then_inc(gain_done, 1)
                bias.vector_start()
                statistics(SECOND)
                normalise_inputs(SECOND)
                normalise_latents(SECOND)
                mean_squares(FIRST)
                nc.vector.tensor_scalar(neg[:, :, 0, :], mask_u8[:, :, :], 1.0, MASKED, ALU.subtract, ALU.mult)\
                    .then_inc(neg_done, 1)
                scale_queries_keys(FIRST)
                dve.wait_ge(neg_done, 2)

                def group(at, before, after, after2):
                    i, s, it = at
                    for h in range(H):
                        for p in range(2):
                            dve.wait_ge(scored, it * 4 + 2 * h + p + 1)
                            last = nc.vector.tensor_tensor(
                                sc[:, s, h, 2 * p:2 * p + 2, :],
                                bank[2 + 2 * h + p][:, :].rearrange("p (b k) -> p b k", b=2),
                                neg_v[:, i, s, 2 * p:2 * p + 2, :], ALU.add)
                    last.then_inc(masked, 1)
                    dve.wait_ge(masked, it + 1)
                    nc.vector.tensor_reduce(negmax[:, :, :].rearrange("p h b -> p (h b)"),
                                            sc[:, s].rearrange("p h b k -> p (h b) k"), AX.X, ALU.max,
                                            negate=True).then_inc(shift_ready, 1)
                    if after2:
                        statistics(after2)
                    if after:
                        mean_squares(after)
                    for n in (0, 1):
                        dve.wait_ge(flips, it * 4 + n + 1)
                        nc.vector.tensor_copy(pT[:, s, n].rearrange("p a k -> p (a k)"), bank[6 + n % 2][:, :])\
                            .then_inc(pT_dve, 1)
                    dve.wait_ge(exps, it * G + G)
                    nc.vector.reciprocal(rsum[:, :, :], psum_[:, s]).then_inc(sums_inverted, 1)
                    dve.wait_ge(weighed, it + 1)
                    dve.wait_ge(sums_inverted, it + 1)
                    nc.vector.tensor_tensor(o[:, s].rearrange("p b (h e) -> p (b h) e", h=H),
                                            bank[2][:, :].rearrange("p (n e) -> p n e", e=DH),
                                            rsum[:, :, :].rearrange("p b h -> p (b h)").unsqueeze(2)
                                            .to_broadcast([S, G * H, DH]), ALU.mult).then_inc(normalised, 1)
                    if after:
                        scale_queries_keys(after)
                    if after2:
                        normalise_inputs(after2)
                    bias.vector_wait(dve, at)
                    dve.wait_ge(mixed, it + 1)
                    x = core.X_groups[:, i, s]
                    nc.vector.scalar_tensor_tensor(
                        out=x, in0=bank[4][:, :].rearrange("p (j d) -> p j d", j=G), scalar=core.gates[:, 2:3],
                        in1=x, op0=ALU.mult, op1=ALU.add).then_inc(updated, 1)
                    if after2:
                        normalise_latents(after2)
                stream(dve, group)

            @block.scalar
            def _(act):
                act.wait_ge(weights, LOADED)

                def copy_inputs(at):
                    i, s, it = at
                    act.wait_ge(n_c.turned, it + 1)
                    nc.scalar.activation(cT[:, s, :], bank[1][0:C, :], ACT.Identity, bias=vecs[0:C, 1:2],
                                         scale=vecs[0:C, 0:1]).then_inc(cT_ready, 1)
                    act.wait_ge(n_l.turned, it + 1)
                    nc.scalar.activation(lT[:, s, :], bank[0][:, :], ACT.Identity, bias=vecs[:, 3:4],
                                         scale=vecs[:, 2:3]).then_inc(lT_ready, 1)

                def keep_projections(at):
                    i, s, it = at
                    for b in range(G):
                        act.wait_ge(lat_proj, it * G + b + 1)
                        nc.scalar.activation(qk[:, s, b, 0:2, :].rearrange("p c d -> p (c d)"), lat_bank(b)[:, 0:2 * D],
                                             ACT.Copy)
                        nc.scalar.activation(v[:, s, b, 1, :], lat_bank(b)[:, 2 * D:3 * D], ACT.Copy).then_inc(lat_kept, 1)
                        act.wait_ge(ctx_proj, it * G + b + 1)
                        nc.scalar.activation(qk[:, s, b, 2, :], ctx_bank(b)[:, 0:D], ACT.Copy)
                        nc.scalar.activation(v[:, s, b, 0, :], ctx_bank(b)[:, D:2 * D], ACT.Copy).then_inc(ctx_kept, 1)

                def square(at):
                    i, s, it = at
                    act.wait_ge(ctx_kept, it * G + G)
                    act.wait_ge(lat_kept, it * G + G)
                    nc.scalar.activation(sq[:, :], qk[:, s].rearrange("p b c d -> p (b c d)"), ACT.Square)\
                        .then_inc(squares, 1)

                def copy_queries_keys(at):
                    i, s, it = at
                    for c, (out, gain) in enumerate(((qT[:, s], q_gain[:, 0:1]), (kT[:, s, :, 1, :], vecs[:, 5:6]),
                                                      (kT[:, s, :, 0, :], vecs[:, 5:6]))):
                        act.wait_ge(qk_turned, it * 3 + c + 1)
                        nc.scalar.activation(out, bank[c % 2][:, :].rearrange("p (b k) -> p b k", b=G), ACT.Copy,
                                             scale=gain).then_inc(qkT_ready, 1)

                copy_inputs(FIRST)
                keep_projections(FIRST)
                square(FIRST)
                act.wait_ge(gain_done, 1)
                copy_queries_keys(FIRST)

                def group(at, before, after, after2):
                    i, s, it = at
                    if after:
                        copy_inputs(after)
                        keep_projections(after)
                        square(after)
                    act.wait_ge(shift_ready, it + 1)
                    for b in range(G):
                        for h in range(H):
                            last = nc.scalar.activation(probs[:, s, h, b, :], sc[:, s, h, b, :], ACT.Exp,
                                                        bias=negmax[:, h, b:b + 1], accum_out=psum_[:, s, b, h:h + 1])
                        last.then_inc(exps, 1)
                    for n in (2, 3):
                        act.wait_ge(flips, it * 4 + n + 1)
                        nc.scalar.activation(pT[:, s, n].rearrange("p a k -> p (a k)"), bank[6 + n % 2][:, :], ACT.Copy)\
                            .then_inc(pT_act, 1)
                    act.wait_ge(o_turned, it + 1)
                    nc.scalar.activation(oT[:, s, :], bank[3][:, :], ACT.Copy).then_inc(oT_ready, 1)
                    if after:
                        copy_queries_keys(after)
                stream(act, group)

            @block.tensor
            def _(pe):
                pe.wait_ge(held.landed, held.all)

                def turn_inputs(at):
                    n_c.tensor_turn(pe, *at)
                    n_l.tensor_turn(pe, *at)

                def project(at):
                    i, s, it = at
                    pe.wait_ge(lT_ready, it + 1)
                    pe.wait_ge(cT_ready, it + 1)
                    for b in range(G):
                        bs = slice(b * S, (b + 1) * S)
                        if b >= 2:
                            pe.wait_ge(lat_kept, it * G + b - 1)
                        nc.tensor.matmul(lat_bank(b)[:, 0:3 * D], lT[:, s, bs], wl[:, :], start=True, stop=True)\
                            .then_inc(lat_proj, 1)
                        if b >= 2:
                            pe.wait_ge(ctx_kept, it * G + b - 1)
                        nc.tensor.matmul(ctx_bank(b)[:, 0:2 * D], cT[:, s, bs], wc[:, :], start=True, stop=True)\
                            .then_inc(ctx_proj, 1)

                def turn_queries_keys(at, kinds):
                    i, s, it = at
                    for c in kinds:
                        if c == 0:
                            pe.wait_ge(qkn_done, it + 1)
                        if c == 2:
                            pe.wait_ge(qkT_ready, it * 3 + 1)
                        for b in range(G):
                            last = nc.tensor.transpose(bank[c % 2][:, b * S:(b + 1) * S], qkn[:, s, b, c, :],
                                                       core.ident[:, :])
                        last.then_inc(qk_turned, 1)

                turn_inputs(FIRST)
                project(FIRST)
                turn_queries_keys(FIRST, range(3))

                def group(at, before, after, after2):
                    i, s, it = at
                    pe.wait_ge(qkT_ready, it * 3 + 3)
                    pe.wait_ge(updated, it + 1)
                    for h in range(H):
                        r = slice(DH * h, DH * h + DH)
                        for p in range(2):
                            for b in (2 * p, 2 * p + 1):
                                last = nc.tensor.matmul(bank[2 + 2 * h + p][:, (b % 2) * 256:(b % 2) * 256 + 256],
                                                        qT[r, s, b, :], kT[r, s, b, :, :].rearrange("p c k -> p (c k)"),
                                                        start=True, stop=True)
                            last.then_inc(scored, 1)
                    if after:
                        turn_inputs(after)
                        project(after)

                    def weigh(b):
                        if b < 2:
                            pe.wait_ge(pT_dve, it * 2 + b + 1)
                        else:
                            pe.wait_ge(pT_act, it * 2 + b - 1)
                        for h in range(H):
                            for half in range(2):
                                last = nc.tensor.matmul(bank[2][:, (b * H + h) * DH:(b * H + h + 1) * DH],
                                                        pT[:, s, b, 2 * h + half, :], v[:, s, b, half, h * DH:(h + 1) * DH],
                                                        start=half == 0, stop=half == 1)
                        return last

                    for n in range(4):
                        if n >= 2:
                            weigh(n - 2)
                        pe.wait_ge(exps, it * G + n + 1)
                        for k in range(4):
                            last = nc.tensor.transpose(bank[6 + n % 2][:, k * S:(k + 1) * S],
                                                       probs[:, s, k // 2, n, (k % 2) * S:(k % 2) * S + S],
                                                       core.ident[:, :])
                        last.then_inc(flips, 1)
                    weigh(2)
                    last = weigh(3)
                    last.then_inc(weighed, 1)
                    pe.wait_ge(normalised, it + 1)
                    for b in range(G):
                        last = nc.tensor.transpose(bank[3][:, b * S:(b + 1) * S], o[:, s, b, :], core.ident[:, :])
                    last.then_inc(o_turned, 1)
                    pe.wait_ge(oT_ready, it + 1)
                    for b in range(G):
                        bs = slice(b * S, (b + 1) * S)
                        last = nc.tensor.matmul(bank[4][:, bs], oT[:, s, bs], wo[:, :], start=True, stop=True)
                    last.then_inc(mixed, 1)
                    if after:
                        turn_queries_keys(after, range(3))
                stream(pe, group)


def layer1_soft_moe(core, held, w, bias):
    nc, E, SLOTS = core.nc, 64, 32
    EC = 8
    CH = EC * SLOTS
    CHUNKS = E // EC
    KT = CH // 128
    NB = B // 2
    with ExitStack() as ctx:
        sb = lambda name, shape: core.sbuf("f0_" + name, shape, ctx=ctx)
        sem = lambda name: core.sem(ctx, "f0_" + name)
        xn, xT = sb("xn", [S, B, D]), sb("xT", [D, B, S])
        phi_s, = held.tiles
        slot_max = sb("slot_max", [S, E * SLOTS])
        row_parts, neg_row = sb("row_parts", [S, 4, B]), sb("neg_row_max", [S, B])
        row_sum, acc = sb("row_sum", [S, B]), sb("acc", [S, B, D])
        with ExitStack() as c1:
            sb1 = lambda name, shape: core.sbuf("f0_" + name, shape, ctx=c1)
            bank = [core.psum(c1, f"f0_bank{k}", [128, 512]) for k in range(2)]
            wide_bank = [core.psum(c1, f"f0_wide_bank{k}", [128, 1024]) for k in range(3)]
            stats, mv, veps, rstd = sb1("stats", [S, B, 6]), sb1("mean_var", [S, B, 2]), sb1("var_eps", [S, B]), sb1("rstd", [S, B])
            stats_done, mv_done, veps_done, rstd_done = (
                sem(n) for n in ("stats_done", "mv_done", "veps_done", "rstd_done"))
            xn_done, turned, xT_ready, l_done = (sem(n) for n in ("xn_done", "turned", "xT_ready", "logits"))
            slot_seen, row_seen = sem("slot_seen"), sem("row_seen")
            NB1 = B // 2
            phi_q = phi_s[:, :].rearrange("d (q n) -> d q n", n=512)
            pair_max = sb1("slot_max_of_parities", [S, 4, 2, 512])
            row_parts_q = row_parts[:, :, :].rearrange("p q (n k) -> p q n k", k=2)
            with nc.Block() as block:
                @block.gpsimd
                def _(pool):
                    nc.gpsimd.memset(pair_max[:, :, :, :], -BIG).then_inc(slot_seen, 1)
                    for g in range(GROUPS):
                        gs = slice(g * G, g * G + G)
                        pool.wait_ge(mv_done, g + 1)
                        nc.gpsimd.tensor_tensor(veps[:, gs], mv[:, gs, 1], core.eps[:, gs], ALU.add).then_inc(veps_done, 1)
                        pool.wait_ge(veps_done, g + 1)
                        nc.gpsimd.tensor_tensor(rstd[:, gs], veps[:, gs], core.minus_half[:, gs], ALU.pow)\
                            .then_inc(rstd_done, 1)
                    nc.gpsimd.memset(acc[:, :, :], 0.0)
                    nc.gpsimd.memset(row_sum[:, :], 0.0)

                @block.vector
                def _(dve):
                    for step in range(GROUPS + 2):
                        if step < GROUPS:
                            for b in range(step * G, step * G + G):
                                last = nc.vector.bn_stats(stats[:, b, :], core.X[:, b, :])
                            last.then_inc(stats_done, 1)
                        if 1 <= step <= GROUPS:
                            dve.wait_ge(stats_done, step)
                            for b in range((step - 1) * G, step * G):
                                last = nc.vector.bn_aggr(mv[:, b, :], stats[:, b, :])
                            last.then_inc(mv_done, 1)
                        if step >= 2:
                            dve.wait_ge(rstd_done, step - 1)
                            for b in range((step - 2) * G, (step - 1) * G):
                                nc.vector.tensor_scalar(xn[:, b, :], core.X[:, b, :], mv[:, b, 0:1], rstd[:, b:b + 1],
                                                        ALU.subtract, ALU.mult).then_inc(xn_done, 1)
                    with dve.Fori(0, 4) as q:
                        for p in range(NB1):
                            ps = wide_bank[p % 3][:, :].rearrange("p (k n) -> p k n", k=2)
                            dve.wait_ge(l_done, q * NB1 + p + 1)
                            dve.wait_ge(slot_seen, q * NB1 + p + 1)
                            nc.vector.tensor_tensor(pair_max[:, q], ps, pair_max[:, q], ALU.max).then_inc(slot_seen, 1)
                            nc.vector.tensor_reduce(row_parts_q[:, q, p, :], ps, AX.X, ALU.max).then_inc(row_seen, 1)
                    dve.wait_ge(slot_seen, 4 * NB1 + 1)
                    dve.wait_ge(row_seen, 4 * NB1 + 3)
                    nc.vector.tensor_tensor(slot_max[:, :].rearrange("p (q n) -> p q n", q=4), pair_max[:, :, 0, :],
                                            pair_max[:, :, 1, :], ALU.max)
                    nc.vector.tensor_reduce(neg_row[:, :], row_parts[:, :, :].rearrange("p q b -> p b q"), AX.X, ALU.max,
                                            negate=True)

                @block.scalar
                def _(act):
                    for g in range(GROUPS):
                        act.wait_ge(turned, g + 1)
                        nc.scalar.activation(xT[:, g * G:(g + 1) * G, :].rearrange("d b t -> d (b t)"), bank[g % 2][:, :],
                                             ACT.Copy).then_inc(xT_ready, 1)

                @block.tensor
                def _(pe):
                    pe.sem_inc(row_seen, 3)
                    for g in range(GROUPS):
                        pe.wait_ge(xn_done, g * G + G)
                        if g >= 2:
                            pe.wait_ge(xT_ready, g - 1)
                        for j in range(G):
                            last = nc.tensor.transpose(bank[g % 2][:, j * S:(j + 1) * S], xn[:, g * G + j, :],
                                                       core.ident[:, :])
                        last.then_inc(turned, 1)
                    pe.wait_ge(xT_ready, GROUPS)
                    pe.wait_ge(held.landed, held.all)
                    with pe.Fori(0, 4) as q:
                        for p in range(NB1):
                            if p < 3:
                                pe.wait_ge(row_seen, q * NB1 + 3)
                            else:
                                pe.wait_ge(row_seen, q * NB1 + p + 1)
                            for k in range(2):
                                last = nc.tensor.matmul(wide_bank[p % 3][:, k * 512:(k + 1) * 512], xT[:, 2 * p + k, :],
                                                        phi_q[:, q, :], start=True, stop=True)
                            last.then_inc(l_done, 1)

        with ExitStack() as c2:
            sb2 = lambda name, shape: core.sbuf("f0_" + name, shape, ctx=c2)
            bank = [core.psum(c2, f"f0_chunk_bank{k}", [128, 512]) for k in range(8)]
            w_s, bias_s = sb2("w", [D, EC, D]), sb2("bias", [D, EC])
            disp = sb2("dispatch", [S, B, CH])
            y = disp[:, :, :].rearrange("p b (k d) -> p k b d", k=KT)
            SLOTS_OF_BACK = 8
            back = sb2("combine", [S, SLOTS_OF_BACK, 2, CH])
            backT = sb2("combineT", [128, KT, B, S])
            part, sums, rsums = sb2("part_sums", [S, 2, CH]), sb2("slot_sums", [S, CH]), sb2("slot_rsums", [S, CH])
            row_part, row_r, row_g = sb2("row_part", [S, B]), sb2("row_r", [S, B]), sb2("row_gate", [S, B])
            slots = sb2("slots", [D, KT, B, 4, SLOTS])
            w_landed, logits, shifts, backs, disps, flips, backT_dve, pair_sums = (
                sem(n) for n in ("w_landed", "chunk_logits", "shifts", "backs", "disps", "flips", "backT_by_vector", "pair_sums"))
            backT_act = sem("backT_by_scalar")
            rows_added, sums_done, rsums_done, scaled_dve, scaled_pool = (
                sem(n) for n in ("rows_added", "sums_done", "rsums_done", "scaled_by_vector", "scaled_by_gpsimd"))
            dispatched, slots_act, expanded, biased = (
                sem(n) for n in ("dispatched", "slots_kept", "expanded", "biased"))
            y_flips, y_act, y_dve, returned, added, row_r_done, row_g_done = (
                sem(n) for n in ("y_flips", "y_by_scalar", "y_by_vector", "returned", "added", "row_r_done", "row_g_done"))
            phi_c = phi_s[:, :].rearrange("d (c n) -> d c n", n=CH)
            max_c = slot_max[:, :].rearrange("d (c n) -> d c n", n=CH)
            BY_POOL = (2, 5)
            BY_VECTOR = tuple(g for g in range(GROUPS) if g not in BY_POOL)
            LAG = 6
            ACT_COPIES = 3
            DVE_COPIES = NB - ACT_COPIES
            logit_bank = lambda p: bank[(0, 1, 6, 7)[p % 4]]
            y_bank = lambda n: bank[(2, 3, 4, 5)[n % 4]]
            pair = lambda p: slice(2 * p, 2 * p + 2)
            half_of_expert = lambda u: slots[:, u // 8, 16 * (u % 2):16 * (u % 2) + 16, u // 2 % 4, :]
            scale_group = lambda g: (disp[:, g * G:(g + 1) * G, :], rsums[:, :].unsqueeze(1).to_broadcast([S, G, CH]))
            with nc.Block() as block:
                @block.sync
                def _(sp):
                    def fetch(c):
                        sp.dma_start(w_s[:, :, :], w[:, c, :, :]).then_inc(w_landed, 16)
                        sp.dma_start(bias_s[:, :], bias[:, c, :]).then_inc(w_landed, 16)
                    fetch(0)
                    with sp.Fori(0, CHUNKS - 1) as c:
                        sp.wait_ge(biased, c * 16 + 16)
                        fetch(c + 1)

                @block.tensor
                def _(pe):
                    def wait_copied(c, p):
                        if p < DVE_COPIES:
                            pe.wait_ge(backT_dve, c * DVE_COPIES + p + 1)
                        else:
                            pe.wait_ge(backT_act, c * ACT_COPIES + p - DVE_COPIES + 1)

                    def give_back(c, g):
                        if g == 0:
                            pe.wait_ge(y_act, c * GROUPS + GROUPS)
                            pe.wait_ge(y_dve, c * GROUPS + GROUPS)
                        if g >= 2:
                            pe.wait_ge(added, c * GROUPS + g - 1 + GROUPS)
                        for j in range(G):
                            for kt in range(KT):
                                last = nc.tensor.matmul(bank[4 + g % 2][:, j * D:(j + 1) * D],
                                                        backT[:, kt, g * G + j, :], y[:, kt, g * G + j, :],
                                                        start=kt == 0, stop=kt == KT - 1)
                        last.then_inc(returned, 1)

                    def chunk(c, first):
                        for step in range(NB + LAG):
                            if step < NB:
                                p = step
                                if not first and p % 2 == 0 and p > 0:
                                    give_back(c - 1, p // 2)
                                if p >= 4:
                                    pe.wait_ge(backs, c * NB + p - 3)
                                for k in range(2):
                                    last = nc.tensor.matmul(logit_bank(p)[:, k * CH:(k + 1) * CH], xT[:, 2 * p + k, :],
                                                            phi_c[:, c, :], start=True, stop=True)
                                last.then_inc(logits, 1)
                                if not first and p == 1:
                                    give_back(c - 1, 0)
                            if step >= LAG:
                                p = step - LAG
                                if p >= 2:
                                    wait_copied(c, p - 2)
                                pe.wait_ge(backs, c * NB + p + 1)
                                for kt in range(KT):
                                    for k in range(2):
                                        at = (kt * 2 + k) * S
                                        last = nc.tensor.transpose(bank[2 + p % 2][:, at:at + S],
                                                                   back[:, p % SLOTS_OF_BACK, k, kt * 128:(kt + 1) * 128],
                                                                   core.ident[:, :])
                                last.then_inc(flips, 1)
                        pe.wait_ge(added, c * GROUPS + GROUPS)
                        for p in range(NB):
                            g = p // 2
                            if p % 2 == 0:
                                if g in BY_POOL:
                                    pe.wait_ge(scaled_pool, c * len(BY_POOL) + BY_POOL.index(g) + 1)
                                else:
                                    pe.wait_ge(scaled_dve, c * len(BY_VECTOR) + BY_VECTOR.index(g) + 1)
                            if p >= 2:
                                pe.wait_ge(slots_act, c * NB + p - 1)
                            for k in range(2):
                                last = nc.tensor.matmul(bank[4 + p % 2][:, k * CH:(k + 1) * CH], xn[:, 2 * p + k, :],
                                                        disp[:, 2 * p + k, :], start=True, stop=True)
                            last.then_inc(dispatched, 1)
                        pe.wait_ge(slots_act, c * NB + NB)
                        pe.wait_ge(w_landed, c * 32 + 32)
                        pe.wait_ge(backs, c * NB + NB)

                        def turn_outputs(n):
                            kt, g = divmod(n, GROUPS)
                            if g == 0:
                                pe.wait_ge(biased, c * 16 + 8 * kt + 8)
                            if n == 0:
                                wait_copied(c, DVE_COPIES - 1)
                                wait_copied(c, NB - 1)
                            if n >= 4:
                                pe.wait_ge((y_act, y_dve)[n % 2], c * GROUPS + (n - 4) // 2 + 1)
                            for j in range(G):
                                last = nc.tensor.transpose(y_bank(n)[:, j * D:(j + 1) * D],
                                                           slots[:, kt, g * G + j].rearrange("d e s -> d (e s)"), core.ident[:, :])
                            last.then_inc(y_flips, 1)

                        for u in range(16):
                            if u >= 4:
                                pe.wait_ge(biased, c * 16 + u - 3)
                            nc.tensor.matmul(logit_bank(u)[:, :], w_s[:, u // 2, :],
                                             half_of_expert(u), start=True,
                                             stop=True).then_inc(expanded, 1)
                            if u >= 9:
                                turn_outputs(u - 9)
                        for n in range(7, 16):
                            turn_outputs(n)

                    chunk(0, True)
                    with pe.Fori(1, CHUNKS) as c:
                        chunk(c, False)
                    for g in range(GROUPS):
                        give_back(CHUNKS - 1, g)

                @block.scalar
                def _(act):
                    with act.Fori(0, CHUNKS) as c:
                        for p in range(NB):
                            act.wait_ge(shifts, c * NB + p + 1)
                            nc.scalar.activation(disp[:, pair(p), :], disp[:, pair(p), :], ACT.Exp).then_inc(disps, 1)
                            if p >= SLOTS_OF_BACK:
                                act.wait_ge(flips, c * NB + p - SLOTS_OF_BACK + 1)
                            for k in range(2):
                                b = 2 * p + k
                                last = nc.scalar.activation(back[:, p % SLOTS_OF_BACK, k, :],
                                                            logit_bank(p)[:, k * CH:(k + 1) * CH],
                                                            ACT.Exp, bias=neg_row[:, b:b + 1],
                                                            accum_out=row_part[:, b:b + 1])
                            last.then_inc(backs, 1)
                        for p in range(DVE_COPIES, NB):
                            act.wait_ge(flips, c * NB + p + 1)
                            nc.scalar.activation(backT[:, :, pair(p), :],
                                                 bank[2 + p % 2][:, :].rearrange("p (k b t) -> p k b t", k=KT, b=2),
                                                 ACT.Copy).then_inc(backT_act, 1)
                        for p in range(NB):
                            act.wait_ge(dispatched, c * NB + p + 1)
                            nc.scalar.activation(slots[:, :, pair(p)].rearrange("d k b e s -> d b k (e s)"),
                                                 bank[4 + p % 2][:, :].rearrange("d (b k n) -> d b k n", b=2, k=KT),
                                                 ACT.Copy).then_inc(slots_act, 1)
                        act.wait_ge(w_landed, c * 32 + 32)
                        done = 0
                        for u in range(16):
                            act.wait_ge(expanded, c * 16 + u + 1)
                            nc.scalar.activation(half_of_expert(u),
                                                 logit_bank(u)[:, :].rearrange("d (b s) -> d b s", b=16), ACT.Identity,
                                                 bias=bias_s[:, u // 2:u // 2 + 1]).then_inc(biased, 1)
                            if u >= 10 and u % 2 == 0:
                                n = u - 10
                                act.wait_ge(y_flips, c * 16 + n + 1)
                                nc.scalar.activation(y[:, 0, n * G:n * G + G, :], y_bank(n)[:, :].rearrange(
                                    "p (j d) -> p j d", j=G), ACT.Copy).then_inc(y_act, 1)
                                done = n + 2
                        for n in range(done, 16, 2):
                            kt, g = divmod(n, GROUPS)
                            act.wait_ge(y_flips, c * 16 + n + 1)
                            nc.scalar.activation(y[:, kt, g * G:g * G + G, :], y_bank(n)[:, :].rearrange(
                                "p (j d) -> p j d", j=G), ACT.Copy).then_inc(y_act, 1)

                @block.gpsimd
                def _(pool):
                    with pool.Fori(0, CHUNKS) as c:
                        for p in range(1, NB):
                            if p >= 2:
                                pool.wait_ge(pair_sums, c * (NB - 1) + p - 1)
                            pool.wait_ge(disps, c * NB + p + 1)
                            nc.gpsimd.tensor_tensor(part[:, :, :], part[:, :, :] if p > 1 else disp[:, pair(0), :],
                                                    disp[:, pair(p), :], ALU.add).then_inc(pair_sums, 1)
                        for g in BY_POOL:
                            pool.wait_ge(rsums_done, c + 1)
                            e, r = scale_group(g)
                            nc.gpsimd.tensor_tensor(e, e, r, ALU.mult).then_inc(scaled_pool, 1)

                @block.vector
                def _(dve):
                    dve.sem_inc(added, GROUPS)
                    dve.sem_inc(rows_added, 1)

                    def add(c, g):
                        dve.wait_ge(added, c * GROUPS + g + 1)
                        dve.wait_ge(returned, c * GROUPS + g + 1)
                        a = acc[:, g * G:g * G + G, :]
                        nc.vector.tensor_tensor(a, bank[4 + g % 2][:, :].rearrange("p (j d) -> p j d", j=G), a,
                                                ALU.add).then_inc(added, 1)

                    def copy_turned(c, p):
                        dve.wait_ge(flips, c * NB + p + 1)
                        nc.vector.tensor_copy(backT[:, :, pair(p), :],
                                              bank[2 + p % 2][:, :].rearrange("p (k b t) -> p k b t", k=KT, b=2))\
                            .then_inc(backT_dve, 1)

                    def chunk(c, first):
                        for p in range(NB):
                            if not first and p % 2 == 0:
                                add(c - 1, p // 2)
                            dve.wait_ge(logits, c * NB + p + 1)
                            nc.vector.tensor_tensor(disp[:, pair(p), :],
                                                    logit_bank(p)[:, :].rearrange("p (b n) -> p b n", b=2),
                                                    max_c[:, c, :].unsqueeze(1).to_broadcast([S, 2, CH]),
                                                    ALU.subtract).then_inc(shifts, 1)
                            if p >= LAG:
                                copy_turned(c, p - LAG)
                        for p in range(NB - LAG, DVE_COPIES):
                            copy_turned(c, p)
                        dve.wait_ge(pair_sums, (c + 1) * (NB - 1))
                        nc.vector.tensor_tensor(sums[:, :], part[:, 0, :], part[:, 1, :], ALU.add).then_inc(sums_done, 1)
                        dve.wait_ge(sums_done, c + 1)
                        nc.vector.reciprocal(rsums[:, :], sums[:, :]).then_inc(rsums_done, 1)
                        dve.wait_ge(rsums_done, c + 1)
                        for g in BY_VECTOR:
                            e, r = scale_group(g)
                            nc.vector.tensor_tensor(e, e, r, ALU.mult).then_inc(scaled_dve, 1)
                        dve.wait_ge(backs, c * NB + NB)
                        dve.wait_ge(rows_added, c + 1)
                        nc.vector.tensor_tensor(row_sum[:, :], row_sum[:, :], row_part[:, :], ALU.add)\
                            .then_inc(rows_added, 1)
                        for n in range(1, 16, 2):
                            kt, g = divmod(n, GROUPS)
                            dve.wait_ge(y_flips, c * 16 + n + 1)
                            nc.vector.tensor_copy(y[:, kt, g * G:g * G + G, :],
                                                  y_bank(n)[:, :].rearrange("p (j d) -> p j d", j=G)).then_inc(y_dve, 1)

                    chunk(0, True)
                    with dve.Fori(1, CHUNKS) as c:
                        chunk(c, False)
                    dve.wait_ge(rows_added, CHUNKS + 1)
                    nc.vector.reciprocal(row_r[:, :], row_sum[:, :]).then_inc(row_r_done, 1)
                    dve.wait_ge(row_r_done, 1)
                    nc.vector.tensor_scalar(row_g[:, :], row_r[:, :], core.gates[:, 4:5], None, ALU.mult)\
                        .then_inc(row_g_done, 1)
                    dve.wait_ge(row_g_done, 1)
                    for g in range(GROUPS):
                        add(CHUNKS - 1, g)
                        dve.wait_ge(added, CHUNKS * GROUPS + g + 1)
                        for b in range(g * G, g * G + G):
                            nc.vector.scalar_tensor_tensor(out=core.X[:, b, :], in0=acc[:, b, :], scalar=row_g[:, b:b + 1],
                                                           in1=core.X[:, b, :], op0=ALU.mult, op1=ALU.add)


def arrays(inputs):
    a = {k: np.asarray(v) for k, v in inputs.items()}
    col = lambda v: v.reshape(-1, 1)
    rows = lambda v, n=128: np.tile(v.reshape(1, -1), (n, 1))
    in_halves = lambda w: w.reshape(-1, 2, 2, 4, 64).transpose(0, 1, 3, 2, 4).reshape(-1, 1024)
    laid = {
        "x": a["x"],
        "ctxT": a["ctx_768"].transpose(2, 0, 1).reshape(C, B * S),
        "gates": rows(np.concatenate([a["g_xattn"], a["g_ffn"]])),
        "c0_wvT": a["L0_xattn_Wv"].T, "c0_bv": col(a["L0_xattn_bv"]),
        "c0_wtT": a["L0_xattn_Wt"].T, "c0_bt": col(a["L0_xattn_bt"]),
        "a1_wq": a["L1_xattn_Wq"], "a1_bq": col(a["L1_xattn_bq"]),
        "a1_wk": a["L1_xattn_Wk"], "a1_bk": col(a["L1_xattn_bk"]),
        "a1_wv": a["L1_xattn_Wv"], "a1_bv": rows(a["L1_xattn_bv"]),
        "a1_w1": a["L1_xattn_W1"], "a1_b1": a["L1_xattn_b1"].reshape(2, 128).T,
        "a1_w2": a["L1_xattn_W2"].reshape(2, 128, D).transpose(1, 0, 2),
        "a1_b2": rows(a["L1_xattn_b2"]),
        "a1_mask": np.repeat(np.eye(16, dtype=np.float32), 8, axis=0),
        "f0_phi": a["L0_ffn_phi"].reshape(D, 64 * 32),
        "f0_w": a["L0_ffn_W"].reshape(8, 8, D, D).transpose(2, 0, 1, 3), "f0_bias": a["L0_ffn_b"].reshape(8, 8, D).transpose(2, 0, 1),
        "f1_routerT": a["L1_ffn_classifier_weight"].T, "f1_bias": rows(a["L1_ffn_e_score_correction_bias"]),
        "f1_guT": a["L1_ffn_gate_up_proj"][:32].transpose(2, 0, 1),
        "f1_downT": a["L1_ffn_down_proj"].transpose(0, 2, 1).reshape(16, 128, D).transpose(1, 0, 2),
        "ctx": a["ctx_768"], "a2_mask": np.tile(np.asarray(a["mask_BxS2_bk0"]).reshape(1, B, S), (S, 1, 1)),
        "a2_lnx_g": col(a["L2_xattn_ln_x_g"]), "a2_lnx_b": col(a["L2_xattn_ln_x_b"]),
        "a2_lnl_g": col(a["L2_xattn_ln_l_g"]), "a2_lnl_b": col(a["L2_xattn_ln_l_b"]),
        "a2_qn": col(np.tile(a["L2_xattn_qn_g"], 2)), "a2_kn": col(np.tile(a["L2_xattn_kn_g"], 2)),
        "a2_wc": a["L2_xattn_Wkv"].T, "a2_wl": np.concatenate([a["L2_xattn_Wq"], a["L2_xattn_Wlkv"]]).T,
        "a2_wo": a["L2_xattn_Wo"].T, "a2_bo": rows(a["L2_xattn_bo"]),
        "f2_gateT": a["L2_ffn_gate_w"].T,
        "f2_w1T": a["L2_ffn_w1"].transpose(2, 0, 1), "f2_b1": a["L2_ffn_b1"].T,
        "f2_w2T": a["L2_ffn_w2"].transpose(2, 0, 1), "f2_b2": a["L2_ffn_b2"],
        "a3_wq": in_halves(a["L3_xattn_w_q"]), "a3_wk": in_halves(a["L3_xattn_w_kv"][:, :1024]),
        "a3_wv": a["L3_xattn_w_kv"][:, 1024:],
        "a3_wo": a["L3_xattn_w_out"].reshape(8, 128, D).transpose(1, 0, 2), "a3_bo": rows(a["L3_xattn_b_out"]),
        "f3_wr": col(a["L3_ffn_w_router"]), "f3_wb": a["L3_ffn_w_block"],
    }
    return {k: np.ascontiguousarray(v) for k, v in laid.items()}


def build(nc, t, out):
    with ExitStack() as ctx:
        core = Core(nc, ctx)
        setup(core, t["x"], t["gates"])
        core.end_layer()
        with ExitStack() as weights:
            phi = core.hold(weights, "f0", [("phi", [D, 2048], F32, t["f0_phi"])])
            layer0_cosine(core, t["ctxT"], t["c0_wvT"], t["c0_bv"], t["c0_wtT"], t["c0_bt"], phi)
            core.end_layer()
            layer1_soft_moe(core, phi, t["f0_w"], t["f0_bias"])
            core.end_layer()
        with ExitStack() as weights:
            held4 = core.hold(weights, "a2", [
                ("w_ctx", [C, 2 * D], F32, t["a2_wc"]), ("w_lat", [D, 3 * D], F32, t["a2_wl"]),
                ("wo", [D, D], F32, t["a2_wo"]), ("bo", [S, D], F32, t["a2_bo"]),
                ("mask", [S, B, S], mybir.dt.uint8, t["a2_mask"])])
            with ExitStack() as weights3:
                held3 = core.hold(weights3, "f1", [
                    ("router", [D, 40], F32, t["f1_routerT"]), ("bias", [S, 40], F32, t["f1_bias"]),
                    ("gate_up", [D, 32, 128], F32, t["f1_guT"]), ("down", [128, 16, D], F32, t["f1_downT"])])
                layer2_attention(core, t["ctxT"], t["a1_wq"], t["a1_bq"], t["a1_wk"], t["a1_bk"], t["a1_wv"], t["a1_bv"],
                                 t["a1_w1"], t["a1_b1"], t["a1_w2"], t["a1_b2"], t["a1_mask"], held3)
                core.end_layer()
                layer3_experts(core, held3, held4)
                core.end_layer()
            layer4_perceiver(core, t["ctx"], t["a2_lnx_g"], t["a2_lnx_b"], t["a2_lnl_g"], t["a2_lnl_b"],
                             t["a2_qn"], t["a2_kn"], held4)
            core.end_layer()
        with ExitStack() as weights:
            held6 = core.hold(weights, "a3", [
                ("wq", [D, 1024], F32, t["a3_wq"]), ("wk", [C, 1024], F32, t["a3_wk"]), ("wv", [C, 1024], F32, t["a3_wv"]),
                ("wo", [128, 8, D], F32, t["a3_wo"]), ("bo", [S, D], F32, t["a3_bo"])])
            layer5_experts(core, t["f2_gateT"], t["f2_w1T"], t["f2_b1"], t["f2_w2T"], t["f2_b2"], held6)
            core.end_layer()
            layer6_attention(core, t["ctxT"], held6)
            core.end_layer()
        layer7_selected_gelu(core, t["f3_wr"], t["f3_wb"], out)


def kernel(**inputs):
    import concourse.bacc as bacc
    from concourse.bass_utils import run_bass_kernel_spmd

    nc = bacc.Bacc("TRN2", target_bir_lowering=False, num_devices=1)
    laid = arrays(inputs)
    t = {k: nc.dram_tensor("in_" + k, v.shape, mybir.dt.from_np(v.dtype), kind="ExternalInput").ap() for k, v in laid.items()}
    out = nc.dram_tensor("out", (B, S, D), F32, kind="ExternalOutput").ap()
    build(nc, t, out)
    return run_bass_kernel_spmd(nc, [{"in_" + k: v for k, v in laid.items()}], core_ids=[0]).results[0]["out"]
```
